# Optimizing a Trainium2 kernel written in Bass

```python
import numpy as np
import jax
import jax.numpy as jnp

def _softmax(x, axis=-1):
    return jax.nn.softmax(x, axis=axis)

def _gelu(x):
    return jax.nn.gelu(x, approximate=True)

def _silu(x):
    return jax.nn.silu(x)

def _sigmoid(x):
    return jax.nn.sigmoid(x)

def _layernorm(x, axis=-1, eps=1e-05):
    m = jnp.mean(x, axis=axis, keepdims=True)
    v = jnp.var(x, axis=axis, keepdims=True)
    return (x - m) / jnp.sqrt(v + eps)

def _scatter_add(tgt, idx, src, axis=0):
    return tgt.at[idx].add(src)

def _segment_sum(src, seg, n):
    return jax.ops.segment_sum(src, seg, n)
kernel_name = 'mk_prb_d1_jaxref_r8_f47e89'

def setup_inputs(seed: int=0):
    np.random.seed(seed)
    _w = jnp.asarray

    def _L0_attn_setup():
        import jax, jax.numpy as jnp
        import numpy as np
        D_MODEL = 128
        N_HEADS = 16
        LN_EPS = 1e-06

        def _layernorm(t, scale):
            mu = jnp.mean(t, axis=-1, keepdims=True)
            var = jnp.var(t, axis=-1, keepdims=True)
            return (t - mu) * jax.lax.rsqrt(var + LN_EPS) * scale
        key = jax.random.key(seed)
        k1, k2, k3 = jax.random.split(key, 3)
        B, S = (2, 256)
        x = jax.random.normal(k1, (B, S, D_MODEL), dtype=jnp.float32)
        W_qkv = jax.random.normal(k2, (D_MODEL, 3 * D_MODEL), dtype=jnp.float32) / np.sqrt(D_MODEL)
        W_out = jax.random.normal(k3, (D_MODEL, D_MODEL), dtype=jnp.float32) / np.sqrt(D_MODEL)
        q_scale = jnp.ones((D_MODEL,), dtype=jnp.float32)
        k_scale = jnp.ones((D_MODEL,), dtype=jnp.float32)
        return {'x': x, 'W_qkv': W_qkv, 'q_scale': q_scale, 'k_scale': k_scale, 'W_out': W_out}
    _L0_attn_in = _L0_attn_setup()

    def _L0_ffn_setup():
        import jax, jax.numpy as jnp
        import numpy as np
        DIM = 128
        DEPTH = 6
        HEADS = 16
        DIM_HEAD = 64
        WINDOW = 32
        INNER = HEADS * DIM_HEAD
        DIM_INNER = int(DIM * 4 * 2 / 3)
        QK_SCALE = 8.0

        def shift_tokens(t):
            a, s = jnp.split(t, 2, -1)
            s = jnp.pad(s, ((0, 0), (1, 0), (0, 0)))[:, :-1]
            return jnp.concatenate([a, s], -1)

        def l2norm(t):
            return t / jnp.maximum(jnp.linalg.norm(t, axis=-1, keepdims=True), 1e-12)

        def rotate_half(x):
            x1, x2 = jnp.split(x, 2, -1)
            return jnp.concatenate([-x2, x1], -1)

        def rotary_tables(n):
            half = jnp.arange(0, DIM_HEAD, 2, dtype=jnp.float32)
            inv_freq = 1.0 / 10000.0 ** (half / DIM_HEAD)
            t = jnp.arange(n, dtype=jnp.float32)
            freqs = t[:, None] * inv_freq[None, :]
            freqs = jnp.concatenate([freqs, freqs], -1)
            base_scale = (half + 0.4 * DIM_HEAD) / (1.4 * DIM_HEAD)
            power = (t - n // 2) / (WINDOW // 2)
            scale = base_scale[None, :] ** power[:, None]
            scale = jnp.concatenate([scale, scale], -1)
            return (freqs, scale)

        def local_attention(q, k, v):
            b, h, n, d = q.shape
            w = WINDOW
            nw = n // w
            bq = q.reshape(b, h, nw, w, d)
            bk = k.reshape(b, h, nw, w, d)
            bv = v.reshape(b, h, nw, w, d)

            def look(t):
                p = jnp.pad(t, ((0, 0), (0, 0), (1, 0), (0, 0), (0, 0)))
                return jnp.concatenate([p[:, :, :nw], p[:, :, 1:]], axis=3)
            bk2, bv2 = (look(bk), look(bv))
            seq = jnp.arange(n).reshape(nw, w)
            seq_p = jnp.pad(seq, ((1, 0), (0, 0)), constant_values=-1)
            jt = jnp.concatenate([seq_p[:nw], seq_p[1:]], axis=1)
            it = seq[:, :, None]
            jb = jt[:, None, :]
            mask = (it < jb) | (it > jb + w) | (jb == -1)
            sim = jnp.einsum('bhwie,bhwje->bhwij', bq, bk2) * QK_SCALE
            sim = jnp.where(mask, -jnp.finfo(sim.dtype).max, sim)
            attn = jax.nn.softmax(sim, -1)
            out = jnp.einsum('bhwij,bhwje->bhwie', attn, bv2)
            return out.reshape(b, h, n, d)

        def attn_layer(x, Wqkv, qs, ksc, Wo):
            b, n, _ = x.shape
            qkv = x @ Wqkv
            q, k, v = jnp.split(qkv, 3, -1)
            sh = lambda t: t.reshape(b, n, HEADS, DIM_HEAD).transpose(0, 2, 1, 3)
            q, k, v = (sh(q), sh(k), sh(v))
            q = l2norm(q) * qs
            k = l2norm(k) * ksc
            freqs, scale = rotary_tables(n)
            cos, sin = (jnp.cos(freqs), jnp.sin(freqs))
            q = q * cos * scale + rotate_half(q) * sin * scale
            inv = 1.0 / scale
            k = k * cos * inv + rotate_half(k) * sin * inv
            out = local_attention(q, k, v)
            out = out.transpose(0, 2, 1, 3).reshape(b, n, INNER)
            return out @ Wo

        def ffn_layer(x, g, bln, W1, b1, W2, b2):
            mu = x.mean(-1, keepdims=True)
            var = ((x - mu) ** 2).mean(-1, keepdims=True)
            xn = (x - mu) / jnp.sqrt(var + 1e-05) * g + bln
            hg = xn @ W1 + b1
            a, gate = jnp.split(hg, 2, -1)
            return a * jax.nn.gelu(gate, approximate=False) @ W2 + b2
        key = jax.random.key(seed)
        ks = jax.random.split(key, 8)
        B, N = (2, 256)
        init = lambda k, shape: jax.random.normal(k, shape, jnp.float32) * 0.02
        return {'x': jax.random.normal(ks[0], (B, N, DIM), jnp.float32), 'Wqkv': init(ks[1], (DEPTH, DIM, 3 * INNER)), 'q_scale': jnp.ones((DEPTH, DIM_HEAD), jnp.float32), 'k_scale': jnp.ones((DEPTH, DIM_HEAD), jnp.float32), 'Wo': init(ks[2], (DEPTH, INNER, DIM)), 'ln_g': jnp.ones((DEPTH, DIM), jnp.float32), 'ln_b': jnp.zeros((DEPTH, DIM), jnp.float32), 'W1': init(ks[3], (DEPTH, DIM, 2 * DIM_INNER)), 'b1': jnp.zeros((DEPTH, 2 * DIM_INNER), jnp.float32), 'W2': init(ks[4], (DEPTH, DIM_INNER, DIM)), 'b2': jnp.zeros((DEPTH, DIM), jnp.float32)}
    _L0_ffn_in = _L0_ffn_setup()
    _d = {'L0_attn_x': _L0_attn_in['x'], 'L0_attn_W_qkv': _L0_attn_in['W_qkv'], 'L0_attn_q_scale': _L0_attn_in['q_scale'], 'L0_attn_k_scale': _L0_attn_in['k_scale'], 'L0_attn_W_out': _L0_attn_in['W_out'], 'L0_ffn_Wqkv': _L0_ffn_in['Wqkv'], 'L0_ffn_q_scale': _L0_ffn_in['q_scale'], 'L0_ffn_k_scale': _L0_ffn_in['k_scale'], 'L0_ffn_Wo': _L0_ffn_in['Wo'], 'L0_ffn_ln_g': _L0_ffn_in['ln_g'], 'L0_ffn_ln_b': _L0_ffn_in['ln_b'], 'L0_ffn_W1': _L0_ffn_in['W1'], 'L0_ffn_b1': _L0_ffn_in['b1'], 'L0_ffn_W2': _L0_ffn_in['W2'], 'L0_ffn_b2': _L0_ffn_in['b2']}
    _x0 = _d['L0_attn_x']
    _d['L0_attn_x'] = jax.random.normal(jax.random.fold_in(jax.random.key(seed), 1), (4, 1024, 128), dtype=_x0.dtype)
    del _x0
    return _d

def reference(L0_attn_x, L0_attn_W_qkv, L0_attn_q_scale, L0_attn_k_scale, L0_attn_W_out, L0_ffn_Wqkv, L0_ffn_q_scale, L0_ffn_k_scale, L0_ffn_Wo, L0_ffn_ln_g, L0_ffn_ln_b, L0_ffn_W1, L0_ffn_b1, L0_ffn_W2, L0_ffn_b2):

    def _L0_attn_ref(x, W_qkv, q_scale, k_scale, W_out):
        import jax, jax.numpy as jnp
        import numpy as np
        D_MODEL = 128
        N_HEADS = 16
        LN_EPS = 1e-06

        def _layernorm(t, scale):
            mu = jnp.mean(t, axis=-1, keepdims=True)
            var = jnp.var(t, axis=-1, keepdims=True)
            return (t - mu) * jax.lax.rsqrt(var + LN_EPS) * scale
        B, S, D = x.shape
        H = N_HEADS
        Hd = D // H
        qkv = jnp.einsum('bsd,de->bse', x, W_qkv)
        q, k, v = jnp.split(qkv, 3, axis=-1)
        q = _layernorm(q, q_scale)
        k = _layernorm(k, k_scale)
        q = q.reshape(B, S, H, Hd)
        k = k.reshape(B, S, H, Hd)
        v = v.reshape(B, S, H, Hd)
        scores = jnp.einsum('bshd,bthd->bhst', q / jnp.sqrt(Hd).astype(q.dtype), k)
        future = jnp.triu(jnp.ones((S, S), dtype=bool), 1)
        scores = jnp.where(future[None, None, :, :], jnp.finfo(scores.dtype).min, scores)
        attn = jax.nn.softmax(scores, axis=-1)
        ctx = jnp.einsum('bhst,bthd->bshd', attn, v)
        out = jnp.einsum('bsd,de->bse', ctx.reshape(B, S, D), W_out)
        return out

    def _L0_ffn_ref(x, Wqkv, q_scale, k_scale, Wo, ln_g, ln_b, W1, b1, W2, b2):
        import jax, jax.numpy as jnp
        import numpy as np
        DIM = 128
        DEPTH = 6
        HEADS = 16
        DIM_HEAD = 64
        WINDOW = 32
        INNER = HEADS * DIM_HEAD
        DIM_INNER = int(DIM * 4 * 2 / 3)
        QK_SCALE = 8.0

        def shift_tokens(t):
            a, s = jnp.split(t, 2, -1)
            s = jnp.pad(s, ((0, 0), (1, 0), (0, 0)))[:, :-1]
            return jnp.concatenate([a, s], -1)

        def l2norm(t):
            return t / jnp.maximum(jnp.linalg.norm(t, axis=-1, keepdims=True), 1e-12)

        def rotate_half(x):
            x1, x2 = jnp.split(x, 2, -1)
            return jnp.concatenate([-x2, x1], -1)

        def rotary_tables(n):
            half = jnp.arange(0, DIM_HEAD, 2, dtype=jnp.float32)
            inv_freq = 1.0 / 10000.0 ** (half / DIM_HEAD)
            t = jnp.arange(n, dtype=jnp.float32)
            freqs = t[:, None] * inv_freq[None, :]
            freqs = jnp.concatenate([freqs, freqs], -1)
            base_scale = (half + 0.4 * DIM_HEAD) / (1.4 * DIM_HEAD)
            power = (t - n // 2) / (WINDOW // 2)
            scale = base_scale[None, :] ** power[:, None]
            scale = jnp.concatenate([scale, scale], -1)
            return (freqs, scale)

        def local_attention(q, k, v):
            b, h, n, d = q.shape
            w = WINDOW
            nw = n // w
            bq = q.reshape(b, h, nw, w, d)
            bk = k.reshape(b, h, nw, w, d)
            bv = v.reshape(b, h, nw, w, d)

            def look(t):
                p = jnp.pad(t, ((0, 0), (0, 0), (1, 0), (0, 0), (0, 0)))
                return jnp.concatenate([p[:, :, :nw], p[:, :, 1:]], axis=3)
            bk2, bv2 = (look(bk), look(bv))
            seq = jnp.arange(n).reshape(nw, w)
            seq_p = jnp.pad(seq, ((1, 0), (0, 0)), constant_values=-1)
            jt = jnp.concatenate([seq_p[:nw], seq_p[1:]], axis=1)
            it = seq[:, :, None]
            jb = jt[:, None, :]
            mask = (it < jb) | (it > jb + w) | (jb == -1)
            sim = jnp.einsum('bhwie,bhwje->bhwij', bq, bk2) * QK_SCALE
            sim = jnp.where(mask, -jnp.finfo(sim.dtype).max, sim)
            attn = jax.nn.softmax(sim, -1)
            out = jnp.einsum('bhwij,bhwje->bhwie', attn, bv2)
            return out.reshape(b, h, n, d)

        def attn_layer(x, Wqkv, qs, ksc, Wo):
            b, n, _ = x.shape
            qkv = x @ Wqkv
            q, k, v = jnp.split(qkv, 3, -1)
            sh = lambda t: t.reshape(b, n, HEADS, DIM_HEAD).transpose(0, 2, 1, 3)
            q, k, v = (sh(q), sh(k), sh(v))
            q = l2norm(q) * qs
            k = l2norm(k) * ksc
            freqs, scale = rotary_tables(n)
            cos, sin = (jnp.cos(freqs), jnp.sin(freqs))
            q = q * cos * scale + rotate_half(q) * sin * scale
            inv = 1.0 / scale
            k = k * cos * inv + rotate_half(k) * sin * inv
            out = local_attention(q, k, v)
            out = out.transpose(0, 2, 1, 3).reshape(b, n, INNER)
            return out @ Wo

        def ffn_layer(x, g, bln, W1, b1, W2, b2):
            mu = x.mean(-1, keepdims=True)
            var = ((x - mu) ** 2).mean(-1, keepdims=True)
            xn = (x - mu) / jnp.sqrt(var + 1e-05) * g + bln
            hg = xn @ W1 + b1
            a, gate = jnp.split(hg, 2, -1)
            return a * jax.nn.gelu(gate, approximate=False) @ W2 + b2
        for i in range(DEPTH):
            x = attn_layer(shift_tokens(x), Wqkv[i], q_scale[i], k_scale[i], Wo[i]) + x
            x = ffn_layer(shift_tokens(x), ln_g[i], ln_b[i], W1[i], b1[i], W2[i], b2[i]) + x
        return x
    x = L0_attn_x
    xn = _layernorm(x, axis=-1)
    x = x + _L0_attn_ref(xn, L0_attn_W_qkv, L0_attn_q_scale, L0_attn_k_scale, L0_attn_W_out) + _L0_ffn_ref(xn, L0_ffn_Wqkv, L0_ffn_q_scale, L0_ffn_k_scale, L0_ffn_Wo, L0_ffn_ln_g, L0_ffn_ln_b, L0_ffn_W1, L0_ffn_b1, L0_ffn_W2, L0_ffn_b2)
    return x

_drawn_inputs = setup_inputs


def setup_inputs(seed=0):
    import zlib

    import numpy as np

    out = dict(_drawn_inputs(seed))
    spreads = {'L0_attn_q_scale': (1.0, 0.6),
     'L0_attn_k_scale': (1.0, 0.6),
     'L0_ffn_q_scale': (1.0, 0.6),
     'L0_ffn_k_scale': (1.0, 0.6),
     'L0_ffn_ln_g': (1.0, 0.6),
     'L0_ffn_ln_b': (0.0, 0.8),
     'L0_ffn_b1': (0.0, 0.8),
     'L0_ffn_b2': (0.0, 0.1)}
    factors = {'L0_ffn_W1': 3.65, 'L0_ffn_W2': 3.585}
    for name, (base, spread) in spreads.items():
        noise = np.random.default_rng([zlib.crc32(name.encode()), seed]).standard_normal(out[name].shape)
        drawn = base * np.exp(spread * noise) if base else spread * noise
        out[name] = jnp.asarray(drawn.astype(out[name].dtype))
    for name, factor in factors.items():
        out[name] = (out[name] * factor).astype(out[name].dtype)
    return out
```

```python
from contextlib import ExitStack

import numpy as np
import concourse.bass as bass
from concourse import mybir

F32 = mybir.dt.float32
BF16 = mybir.dt.bfloat16
I32 = mybir.dt.int32
ALU = mybir.AluOpType
ACT = mybir.ActivationFunctionType
AX = mybir.AxisListType

P = 128
B, S, D = 4, 1024, 128
CHUNKS = B * S // P
PAIRS = CHUNKS // 2
PAIRS_B = PAIRS // B
COLS = B * (S + 1)

AHD = 8
AG = 4
GROUPS = D // AHD // AG

LAYERS = 6
HEADS, HD = 16, 64
INNER = HEADS * HD
BAND = 32
KEYS = BAND + P
SIM_SCALE = 8.0
FF = int(D * 4 * 2 / 3)
FPARTS = [(f, min(P, FF - f)) for f in range(0, FF, P)]
NF = len(FPARTS)
MASKED = -1e30
RSQRT_MAGIC = float(0x5F3759DF)


def wait(engine, semaphore, value):
    if isinstance(value, int) and value <= 0:
        return
    engine.wait_ge(semaphore, value)


def rsqrt_steps(nc, dve, link, link_from, y, x, half, n):
    v = nc.vector
    at = link_from

    def next_step(instruction):
        nonlocal at
        at += 1
        instruction.then_inc(link, 1)
        dve.wait_ge(link, at)

    yi, xi = y.bitcast(I32), x.bitcast(I32)
    next_step(v.tensor_scalar(yi, xi, 1, None, ALU.logical_shift_right))
    next_step(v.tensor_scalar(yi, yi, -1.0, RSQRT_MAGIC, ALU.mult, ALU.add))
    for _ in range(3):
        next_step(v.tensor_tensor(half, y, y, ALU.mult))
        next_step(v.scalar_tensor_tensor(half, half, -0.5, x, ALU.mult, ALU.mult))
        next_step(v.scalar_tensor_tensor(y, half, 1.5, y, ALU.add, ALU.mult))
    return at


def prepare(nc, t):
    with ExitStack() as ctx:
        stats = ctx.enter_context(nc.sbuf_tensor("pre_stats", [P, CHUNKS, 6], F32))
        mean_var = ctx.enter_context(nc.sbuf_tensor("pre_mean_var", [P, CHUNKS, 2], F32))
        var = ctx.enter_context(nc.sbuf_tensor("pre_var", [P, CHUNKS], F32))
        rstd = ctx.enter_context(nc.sbuf_tensor("pre_rstd", [P, CHUNKS], F32))
        half = ctx.enter_context(nc.sbuf_tensor("pre_half", [P, CHUNKS], F32))
        xn = ctx.enter_context(nc.sbuf_tensor("pre_xn", [P, CHUNKS, D], F32))
        turned = [ctx.enter_context(nc.psum_tensor(f"pre_turned{i}", [P, 512], F32)) for i in range(2)]
        x_loaded = ctx.enter_context(nc.semaphore("pre_x_loaded"))
        stats_done = ctx.enter_context(nc.semaphore("pre_stats_done"))
        link = ctx.enter_context(nc.semaphore("pre_link"))
        xn_done = ctx.enter_context(nc.semaphore("pre_xn_done"))
        turned_full = ctx.enter_context(nc.semaphore("pre_turned_full"))
        turned_read = ctx.enter_context(nc.semaphore("pre_turned_read"))
        padded = ctx.enter_context(nc.semaphore("pre_padded"))
        block = ctx.enter_context(nc.Block())

        @block.sync
        def _(sp):
            sp.dma_start(t.xtok[:], t.x.rearrange("b (c p) d -> p (b c) d", p=P)).then_inc(x_loaded, 16)
            sp.dma_start(t.ident[:], t.ident_d).then_inc(x_loaded, 16)
            sp.wait_ge(x_loaded, 32)

        @block.vector
        def _(dve):
            dve.wait_ge(x_loaded, 32)
            for c in range(CHUNKS):
                nc.vector.bn_stats(stats[:, c, :], t.xtok[:, c, :]).then_inc(stats_done, 1)
            for c in range(CHUNKS):
                dve.wait_ge(stats_done, c + 1)
                nc.vector.bn_aggr(mean_var[:, c, :], stats[:, c, :]).then_inc(stats_done, 1)
            dve.wait_ge(stats_done, 2 * CHUNKS)
            nc.vector.tensor_scalar(var[:], mean_var[:, :, 1], 1e-5, None, ALU.add).then_inc(link, 1)
            dve.wait_ge(link, 1)
            rsqrt_steps(nc, dve, link, 1, rstd[:], var[:], half[:], CHUNKS)
            for c in range(CHUNKS):
                nc.vector.tensor_scalar(xn[:, c, :], t.xtok[:, c, :], mean_var[:, c, 0:1], rstd[:, c:c + 1],
                                        ALU.subtract, ALU.mult).then_inc(xn_done, 1)

        @block.tensor
        def _(pe):
            for n in range(CHUNKS // 4):
                pe.wait_ge(xn_done, 4 * n + 4)
                if n >= 2:
                    pe.wait_ge(turned_read, n - 1)
                for k in range(4):
                    mm = nc.tensor.transpose(turned[n % 2][:, k * P:(k + 1) * P], xn[:, 4 * n + k, :], t.ident[:])
                mm.then_inc(turned_full, 1)

        @block.scalar
        def _(act):
            act.wait_ge(padded, 1)
            for n in range(CHUNKS // 4):
                at = 4 * n * P + (4 * n) // (S // P) + 1
                act.wait_ge(turned_full, n + 1)
                nc.scalar.copy(t.xa[:, at:at + 512], turned[n % 2][:]).then_inc(turned_read, 1)

        @block.gpsimd
        def _(pool):
            nc.gpsimd.memset(t.xa[:], 0.0).then_inc(padded, 1)
            nc.gpsimd.memset(t.xb[:], 0.0).then_inc(padded, 1)


def attention(nc, t):
    N_TURNS = 2 * B * S // 512
    with ExitStack() as ctx:
        def sb(name, shape, dt=F32):
            return ctx.enter_context(nc.sbuf_tensor("a_" + name, shape, dt))

        def sem(name):
            return ctx.enter_context(nc.semaphore("a_" + name))

        v_all = sb("v_all", [P, CHUNKS, D])
        w_out = sb("w_out", [P, D])
        ident_bf = sb("ident_bf", [P, P], BF16)
        mask_qk = sb("mask_qk", [P, P], BF16)
        mask_kq = sb("mask_kq", [P, P], BF16)
        q_stack = [sb(f"q_stack{n}", [P, AG, S], BF16) for n in range(GROUPS)]
        k_stack = [sb(f"k_stack{n}", [P, AG, S], BF16) for n in range(GROUPS)]
        v_pad = [sb(f"v_pad{n}", [P, S // P, AG, BAND]) for n in range(2)]
        neg_max = sb("neg_max", [P, S // P, AG, BAND], BF16)

        with ExitStack() as pre:
            def psb(name, shape, dt=F32):
                return pre.enter_context(nc.sbuf_tensor("ap_" + name, shape, dt))

            def psem(name):
                return pre.enter_context(nc.semaphore("ap_" + name))

            wqkv = psb("wqkv", [P, 3 * D])
            masks = psb("masks", [P, 2, P])
            qk = psb("qk", [P, 2, CHUNKS, D])
            stats = psb("stats", [P, 2 * CHUNKS, 6])
            mean_var = psb("mean_var", [P, 2 * CHUNKS, 2])
            var = psb("var", [P, 2 * CHUNKS])
            rstd = psb("rstd", [P, 2 * CHUNKS])
            half = psb("half", [P, 2 * CHUNKS])
            cols = psb("cols", [P, 2])
            full = [psb(f"full{n}", [P, 512]) for n in range(2)]
            parts = [psb(f"parts{n}", [P, 3, 512], BF16) for n in range(2)]
            rest = [psb(f"rest{n}", [P, 512]) for n in range(2)]
            bank = [pre.enter_context(nc.psum_tensor(f"ap_bank{n}", [P, 512], F32)) for n in range(4)]
            loaded, proj_full, proj_read, stats_done = psem("loaded"), psem("proj_full"), psem("proj_read"), psem("stats_done")
            link, normal, cols_ready, filled = psem("link"), psem("normal"), psem("cols_ready"), psem("filled")
            turned, scaled, rested, parted, last_part = (psem("turned"), psem("scaled"), psem("rested"), psem("parted"),
                                                         psem("last_part"))
            stored = [psem(f"stored{n}") for n in range(2)]
            LOADED = 16 * 5
            block = pre.enter_context(nc.Block())

            @block.sync
            def _(sp):
                sp.dma_start(wqkv[:], t.awqkv_d).then_inc(loaded, 16)
                sp.dma_start(w_out[:], t.awout_d).then_inc(loaded, 16)
                sp.dma_start(cols[:, 0:1], t.aqs_d.unsqueeze(1)).then_inc(loaded, 16)
                sp.dma_start(cols[:, 1:2], t.aks_d.unsqueeze(1)).then_inc(loaded, 16)
                sp.dma_start(masks[:], t.amasks_d).then_inc(loaded, 16)
                for n in range(N_TURNS):
                    sp.wait_ge(last_part, n + 1)
                    dst = (t.q_parts_d, t.k_parts_d)[n % 2][:, :, (n // 2) * 512:(n // 2 + 1) * 512]
                    sp.dma_start(dst.rearrange("a f t -> f a t"), parts[n % 2][:]).then_inc(stored[n % 2], 16)
                for n in range(2):
                    sp.wait_ge(stored[n], 16 * (N_TURNS // 2))

            @block.tensor
            def _(pe):
                pe.wait_ge(loaded, LOADED)
                for c in range(CHUNKS):
                    if c >= 4:
                        pe.wait_ge(stats_done, 2 * (c - 3))
                    at = c * P + c // (S // P) + 1
                    nc.tensor.matmul(bank[c % 4][:, 0:3 * D], t.xa[:, at:at + P], wqkv[:], start=True, stop=True
                                     ).then_inc(proj_full, 1)
                pe.wait_ge(stats_done, 2 * CHUNKS)
                for n in range(N_TURNS):
                    if n >= 4:
                        pe.wait_ge(scaled, n - 3)
                    pe.wait_ge(normal, 4 * n + 4)
                    for k in range(4):
                        mm = nc.tensor.transpose(bank[n % 4][:, k * P:(k + 1) * P], qk[:, n % 2, 4 * (n // 2) + k, :], t.ident[:])
                    mm.then_inc(turned, 1)

            @block.vector
            def _(dve):
                for c in range(CHUNKS):
                    dve.wait_ge(proj_full, c + 1)
                    dve.wait_ge(proj_read, c + 1)
                    for w in range(2):
                        nc.vector.bn_stats(stats[:, 2 * c + w, :], bank[c % 4][:, w * D:(w + 1) * D]).then_inc(stats_done, 1)
                for c in range(2 * CHUNKS):
                    dve.wait_ge(stats_done, c + 1)
                    nc.vector.bn_aggr(mean_var[:, c, :], stats[:, c, :]).then_inc(link, 1)
                dve.wait_ge(link, 2 * CHUNKS)
                nc.vector.tensor_scalar(var[:], mean_var[:, :, 1], 1e-6, None, ALU.add).then_inc(link, 1)
                dve.wait_ge(link, 2 * CHUNKS + 1)
                rsqrt_steps(nc, dve, link, 2 * CHUNKS + 1, rstd[:], var[:], half[:], 2 * CHUNKS)
                dve.wait_ge(loaded, LOADED)
                nc.vector.tensor_scalar(cols[:, 0:1], cols[:, 0:1], float(AHD) ** -0.5, None, ALU.mult).then_inc(cols_ready, 1)
                for n in range(N_TURNS):
                    for k in range(4):
                        c, w = 4 * (n // 2) + k, n % 2
                        m = 2 * c + w
                        nc.vector.tensor_scalar(qk[:, w, c, :], qk[:, w, c, :], mean_var[:, m, 0:1], rstd[:, m:m + 1],
                                                ALU.subtract, ALU.mult).then_inc(normal, 1)
                dve.wait_ge(filled, 1)
                for n in range(GROUPS):
                    nc.vector.memset(k_stack[n][96:99, :, :], 1.0)
                for n in range(2):
                    nc.vector.memset(v_pad[n][:, :, :, AHD:AHD + 1], 1.0)

            @block.scalar
            def _(act):
                act.wait_ge(loaded, LOADED)
                nc.scalar.copy(ident_bf[:], t.ident[:])
                nc.scalar.copy(mask_qk[:], masks[:, 0, :])
                nc.scalar.copy(mask_kq[:], masks[:, 1, :])
                for c in range(CHUNKS):
                    act.wait_ge(proj_full, c + 1)
                    nc.scalar.copy(qk[:, :, c, :], bank[c % 4][:, 0:2 * D].rearrange("p (w d) -> p w d", w=2))
                    nc.scalar.copy(v_all[:, c, :], bank[c % 4][:, 2 * D:3 * D]).then_inc(proj_read, 1)
                act.wait_ge(cols_ready, 1)
                for n in range(N_TURNS):
                    s = n % 2
                    act.wait_ge(turned, n + 1)
                    if n >= 2:
                        act.wait_ge(rested, n - 1)
                        act.wait_ge(stored[s], 16 * (n // 2))
                    nc.scalar.activation(full[s][:], bank[n % 4][:], ACT.Copy, scale=cols[:, s:s + 1]).then_inc(scaled, 1)
                    act.wait_ge(scaled, n + 1)
                    nc.scalar.copy(parts[s][:, 0, :], full[s][:]).then_inc(parted, 1)
                    if n >= 1:
                        act.wait_ge(rested, n)
                        nc.scalar.copy(parts[1 - s][:, 1, :], rest[1 - s][:]).then_inc(parted, 1)
                act.wait_ge(rested, N_TURNS)
                nc.scalar.copy(parts[1][:, 1, :], rest[1][:]).then_inc(parted, 1)

            @block.gpsimd
            def _(pool):
                for buf in (*k_stack, *v_pad, *q_stack, neg_max):
                    last = nc.gpsimd.memset(buf[:], 0.0)
                last.then_inc(filled, 1)
                for n in range(N_TURNS + 1):
                    if n < N_TURNS:
                        s = n % 2
                        pool.wait_ge(parted, max(2 * n, 1))
                        nc.gpsimd.tensor_tensor(rest[s][:], full[s][:], parts[s][:, 0, :], ALU.subtract).then_inc(rested, 1)
                    if n >= 1:
                        s = (n - 1) % 2
                        pool.wait_ge(parted, min(2 * n + 1, 2 * N_TURNS))
                        nc.gpsimd.tensor_tensor(parts[s][:, 2, :], rest[s][:], parts[s][:, 1, :], ALU.subtract
                                                ).then_inc(last_part, 1)

        probs = [sb(f"probs{n}", [P, AG, S]) for n in range(2)]
        row_max = sb("row_max", [P, AG, S // P])
        max_b = sb("max_b", [P, AG, S // P])
        max_rest = sb("max_rest", [P, AG, S // P])
        ctx_t = sb("ctx_t", [P, S])
        inv = sb("inv", [P, 2, 4, AG])
        ctx_tok = sb("ctx_tok", [P, S // P, D])
        ctx_f = sb("ctx_f", [P, S])

        ring = [ctx.enter_context(nc.psum_tensor(f"a_ring{n}", [P, 512], F32)) for n in range(2)]
        wide_bank = [ctx.enter_context(nc.psum_tensor(f"a_wide{n}", [P, S], F32)) for n in range(2)]
        out_bank = ctx.enter_context(nc.psum_tensor("a_out", [P, S], F32))

        stacked = [sem(f"stacked{n}") for n in range(GROUPS)]
        r_full, r_done = sem("r_full"), sem("r_done")
        split_done, max_placed = sem("split_done"), sem("max_placed")
        wide_full, exp_done, pv_done, pv_read = sem("wide_full"), sem("exp_done"), sem("pv_done"), sem("pv_read")
        v_ready, link = sem("v_ready"), sem("link")

        units = [(c, k0, min(512, (c + 1) * P - k0)) for c in range(S // P) for k0 in range(0, (c + 1) * P, 512)]
        KC = S // P
        NMAX = AG * len(units)
        TURN_MAX, TURN_CTX, PROJECT = NMAX, NMAX + 1, NMAX + 3
        STEP, BATCH = NMAX + 3, GROUPS * (NMAX + 3) + 4

        def ring_at(b, hg, n):
            if isinstance(b, int) and b == 0 and hg == 0:
                return n
            return BATCH * b + (STEP * hg + (4 if hg > 0 else 0) - 6 + n)

        def bank_at(hg, n):
            return ring[(STEP * hg + n) % 2]

        def is_first(b, hg):
            return isinstance(b, int) and b == 0 and hg == 0

        def over_batches(engine, step, last):
            for hg in range(GROUPS):
                step(0, hg)
            with engine.Fori(1, B) as b:
                for hg in range(GROUPS):
                    step(b, hg)
            last()

        block = ctx.enter_context(nc.Block())

        @block.sync
        def _(sp):
            def stacks(b, hg):
                toks = bass.ds(b * S, S)
                rows = slice(AG * AHD * hg, AG * AHD * (hg + 1))
                for a in range(3):
                    for j in range(3):
                        at = AHD * (3 * a + j)
                        for stack, src in ((q_stack, t.q_parts_d[a]), (k_stack, t.k_parts_d[j])):
                            sp.dma_start(stack[hg][at:at + AHD, :, :], src[rows, toks].rearrange("(h r) t -> r h t", h=AG)
                                         ).then_inc(stacked[hg], 16)

            for hg in range(GROUPS):
                stacks(0, hg)
            with sp.Fori(1, B) as b:
                for hg in range(GROUPS):
                    sp.wait_ge(wide_full, AG * KC * GROUPS * b + (AG * KC * (hg + 1 - GROUPS)))
                    stacks(b, hg)
            for hg in range(GROUPS):
                sp.wait_ge(stacked[hg], 16 * 18 * B)

        @block.tensor
        def _(pe):
            def maxima(b, hg, n):
                hh, (c, k0, width) = n // len(units), units[n % len(units)]
                wait(pe, r_done, ring_at(b, hg, n) - 1)
                bank = bank_at(hg, n)
                diagonal = k0 + width == (c + 1) * P
                mm = nc.tensor.matmul(bank[:, 0:width], q_stack[hg][0:96, hh, c * P:(c + 1) * P],
                                      k_stack[hg][0:96, hh, k0:k0 + width], start=True, stop=True)
                if diagonal:
                    mm = nc.tensor.matmul(bank[:, width - P:width], ident_bf[:], mask_qk[:], start=False, stop=True,
                                          skip_group_check=True)
                mm.then_inc(r_full, 1)

            def turn_maxima(b, hg):
                wait(pe, r_done, ring_at(b, hg, TURN_MAX) - 1)
                wait(pe, split_done, GROUPS * b + (hg + 1))
                bank = bank_at(hg, TURN_MAX)[:].bitcast(BF16)
                for c in range(KC):
                    mm = nc.tensor.transpose(bank[:, c * P:(c + 1) * P], neg_max[:, c, :, :].rearrange("p h k -> p (h k)"),
                                             ident_bf[:])
                mm.then_inc(r_full, 1)

            def scores(n2, hg, kc, hh):
                width = S - kc * P
                if kc == 0 and hh == 0:
                    wait(pe, max_placed, n2 + 1)
                w = AG * kc + hh
                wait(pe, exp_done, n2 * (AG * KC) + (w - 1))
                bank = wide_bank[w % 2]
                for at in range(0, width, 512):
                    n = min(512, width - at)
                    mm = nc.tensor.matmul(bank[:, at:at + n], k_stack[hg][:, hh, kc * P:(kc + 1) * P],
                                          q_stack[hg][:, hh, kc * P + at:kc * P + at + n], start=True, stop=True)
                mm = nc.tensor.matmul(bank[:, 0:P], ident_bf[:], mask_kq[:], start=False, stop=True, skip_group_check=True)
                mm.then_inc(wide_full, 1)

            def values(n2, hg, kc):
                wait(pe, exp_done, n2 * (AG * KC) + AG * (kc + 1))
                if kc == 0:
                    wait(pe, pv_read, n2)
                    wait(pe, v_ready, n2 + 1)
                for q0 in range(0, S, 512):
                    lo = max(q0, kc * P)
                    if lo >= q0 + 512:
                        continue
                    for hh in range(AG):
                        mm = nc.tensor.matmul(out_bank[BAND * hh:BAND * (hh + 1), lo:q0 + 512], v_pad[hg % 2][:, kc, hh, :],
                                              probs[kc % 2][:, hh, lo - kc * P:q0 + 512 - kc * P],
                                              start=(kc == 0), stop=(kc == KC - 1), skip_group_check=True)
                mm.then_inc(pv_done, 1)

            def turn_context(n2, b, hg, n0):
                wait(pe, pv_read, n2 + 1)
                for n in range(2):
                    wait(pe, r_done, ring_at(b, hg, n0 + n) - 1)
                    for k in range(4):
                        c = 4 * n + k
                        mm = nc.tensor.transpose(bank_at(hg, n0 + n)[:, k * P:(k + 1) * P], ctx_t[:, c * P:(c + 1) * P], t.ident[:])
                    mm.then_inc(r_full, 1)

            def project(b, hg, n0):
                for n in range(2):
                    wait(pe, r_done, ring_at(b, hg, n0))
                    if n == 1:
                        wait(pe, r_done, ring_at(b, hg, n0 + n) - 1)
                    for k in range(4):
                        mm = nc.tensor.transpose(bank_at(hg, n0 + n)[:, k * P:(k + 1) * P], ctx_tok[:, 4 * n + k, :], t.ident[:])
                    mm.then_inc(r_full, 1)
                for n in range(2):
                    wait(pe, r_done, ring_at(b, hg, n0 + 2))
                    for k in range(4):
                        c = 4 * n + k
                        mm = nc.tensor.matmul(bank_at(hg, n0 + 2 + n)[:, k * P:(k + 1) * P], ctx_f[:, c * P:(c + 1) * P],
                                              w_out[:], start=True, stop=True)
                    mm.then_inc(r_full, 1)

            def step(b, hg):
                wait(pe, stacked[hg], 16 * 18 * (b + 1))
                n2, before = GROUPS * b + (hg - 1), (hg - 1) % GROUPS
                share = NMAX // KC
                for kc in range(KC):
                    for m in range(share):
                        maxima(b, hg, kc * share + m)
                        if not is_first(b, hg) and m < AG:
                            scores(n2, before, kc, m)
                    if not is_first(b, hg) and kc >= 1:
                        values(n2, before, kc - 1)
                turn_maxima(b, hg)
                if not is_first(b, hg):
                    values(n2, before, KC - 1)
                    turn_context(n2, b, hg, TURN_CTX)
                    if hg == 0:
                        project(b, hg, PROJECT)

            def last():
                n2, before = GROUPS * B - 1, GROUPS - 1
                for kc in range(KC):
                    for hh in range(AG):
                        scores(n2, before, kc, hh)
                    if kc >= 1:
                        values(n2, before, kc - 1)
                values(n2, before, KC - 1)
                turn_context(n2, B, 0, 0)
                project(B, 0, 2)

            over_batches(pe, step, last)

        @block.scalar
        def _(act):
            def exps(n2):
                for kc in range(KC):
                    for hh in range(AG):
                        w = AG * kc + hh
                        width = S - kc * P
                        wait(act, wide_full, n2 * (AG * KC) + (w + 1))
                        if hh == 0:
                            wait(act, pv_done, n2 * KC + (kc - 1))
                        nc.scalar.activation(probs[kc % 2][:, hh, 0:width], wide_bank[w % 2][:, 0:width], ACT.Exp
                                             ).then_inc(exp_done, 1)

            def copy_context(n2, b, hg):
                wait(act, pv_done, n2 * KC + KC)
                nc.scalar.copy(ctx_t[:], out_bank[:]).then_inc(pv_read, 1)

            def step(b, hg):
                if is_first(b, hg):
                    return
                n2 = GROUPS * b + (hg - 1)
                exps(n2)
                copy_context(n2, b, hg)

            def last():
                exps(GROUPS * B - 1)
                copy_context(GROUPS * B - 1, B, 0)

            over_batches(act, step, last)

        @block.gpsimd
        def _(pool):
            def step(b, hg):
                wait(pool, pv_done, KC * GROUPS * b + KC * (hg - 1))
                src = v_all[:, bass.ds(b * KC, KC), AG * AHD * hg:AG * AHD * (hg + 1)]
                nc.gpsimd.tensor_copy(v_pad[hg % 2][:, :, :, 0:AHD], src.rearrange("p c (h d) -> p c h d", h=AG)
                                      ).then_inc(v_ready, 1)

            over_batches(pool, step, lambda: None)

        @block.vector
        def _(dve):
            def maxima(b, hg, n):
                hh, (c, k0, width) = n // len(units), units[n % len(units)]
                wait(dve, r_full, ring_at(b, hg, n) + 1)
                into = (max_b if k0 > 0 else row_max)[:, hh, c:c + 1]
                nc.vector.tensor_reduce(into, bank_at(hg, n)[:, 0:width], AX.X, ALU.max).then_inc(r_done, 1)

            def split_maxima(b, hg):
                dve.sem_clear(link)
                wait(dve, r_done, ring_at(b, hg, NMAX))
                part = [neg_max[:, :, :, n].rearrange("p c h -> p h c") for n in range(3)]
                half = KC // 2
                at = 0

                def linked(instruction):
                    nonlocal at
                    at += 1
                    instruction.then_inc(link, 1)
                    dve.wait_ge(link, at)

                linked(nc.vector.tensor_tensor(row_max[:, :, half:KC], row_max[:, :, half:KC], max_b[:, :, half:KC], ALU.max))
                linked(nc.vector.tensor_scalar(part[0], row_max[:], -1.0, None, ALU.mult))
                linked(nc.vector.scalar_tensor_tensor(max_rest[:], row_max[:], -1.0, part[0], ALU.mult, ALU.subtract))
                linked(nc.vector.tensor_copy(part[1], max_rest[:]))
                nc.vector.tensor_tensor(part[2], max_rest[:], part[1], ALU.subtract).then_inc(split_done, 1)

            def place_maxima(b, hg):
                wait(dve, r_full, ring_at(b, hg, TURN_MAX) + 1)
                bank = bank_at(hg, TURN_MAX)[:].bitcast(BF16)
                for hh in range(AG):
                    last = nc.vector.tensor_copy(q_stack[hg][96:P, hh, :], bank[BAND * hh:BAND * (hh + 1), :])
                    if hh < AG - 1:
                        last.then_inc(max_placed_parts, 1)
                last.then_inc(max_placed, 1)
                dve.wait_ge(max_placed, GROUPS * b + (hg + 1))
                dve.sem_inc(r_done, 1)

            def normalise(b, hg, n0, before):
                dve.sem_clear(link)
                for n in range(2):
                    wait(dve, r_full, ring_at(b, hg, n0 + n) + 1)
                    bank = bank_at(hg, n0 + n)[:].rearrange("p (c h d) -> p c h d", c=4, h=AG)
                    nc.vector.reciprocal(inv[:, n], bank[:, :, :, AHD]).then_inc(link, 1)
                    dve.wait_ge(link, n + 1)
                    out = ctx_tok[:, 4 * n:4 * n + 4, AG * AHD * before:AG * AHD * (before + 1)]
                    nc.vector.tensor_tensor(out.rearrange("p c (h d) -> p c h d", h=AG), bank[:, :, :, 0:AHD],
                                            inv[:, n].unsqueeze(3).broadcast_to([P, 4, AG, AHD]), ALU.mult).then_inc(r_done, 1)

            def project(b, hg, n0):
                for n in range(2):
                    wait(dve, r_full, ring_at(b, hg, n0 + n) + 1)
                    nc.vector.tensor_copy(ctx_f[:, 512 * n:512 * (n + 1)], bank_at(hg, n0 + n)[:]).then_inc(r_done, 1)
                for n in range(2):
                    wait(dve, r_full, ring_at(b, hg, n0 + 2 + n) + 1)
                    chunk = t.xtok[:, bass.ds((b - 1) * KC + 4 * n, 4), :].rearrange("p c d -> p (c d)")
                    nc.vector.tensor_tensor(chunk, bank_at(hg, n0 + 2 + n)[:], chunk, ALU.add).then_inc(r_done, 1)

            max_placed_parts = sem("max_placed_parts")

            def step(b, hg):
                for n in range(NMAX):
                    maxima(b, hg, n)
                split_maxima(b, hg)
                place_maxima(b, hg)
                if not is_first(b, hg):
                    normalise(b, hg, TURN_CTX, (hg - 1) % GROUPS)
                    if hg == 0:
                        project(b, hg, PROJECT)

            def last():
                normalise(B, 0, 0, GROUPS - 1)
                project(B, 0, 2)

            over_batches(dve, step, last)


def windowed(nc, t):
    with ExitStack() as ctx:
        def sb(name, shape, dt=F32):
            return ctx.enter_context(nc.sbuf_tensor("w_" + name, shape, dt))

        def sem(name):
            return ctx.enter_context(nc.semaphore("w_" + name))

        wqkv = sb("wqkv", [P, 2, 3 * INNER])
        scales = sb("scales", [P, 2, 4 * HD])
        wo = sb("wo", [P, HEADS // 2, D])
        w1 = sb("w1", [P, 2 * FF])
        w2 = sb("w2", [P, NF, D])
        b1 = sb("b1", [P, 2 * NF])
        vecs = sb("vecs", [P, 3])
        rope_tab = sb("rope_tab", [P, S // P, 4 * HD])
        mask_tab = sb("mask_tab", [P, PAIRS_B, KEYS + 1])
        mask_odd = sb("mask_odd", [P, KEYS])
        xs = [sb(f"xs{u}", [P, P]) for u in range(2)]
        raw = sb("raw", [P, 4, 512])
        sq = sb("sq", [P, 2, 512])
        rot = sb("rot", [P, 4, 512])
        rope = sb("rope", [P, 4, 512])
        tc = [sb(f"tc{u}", [P, 4 * HD]) for u in range(2)]
        ss = sb("ss", [P, 2 * HEADS])
        rn = [sb(f"rn{u}", [P, 2 * HEADS]) for u in range(2)]
        nhalf = sb("nhalf", [P, 2 * HEADS])
        qt = sb("qt", [P, HEADS // 2, P])
        kb = sb("kb", [P, HEADS // 2, 2, KEYS])
        mask = sb("mask", [P, KEYS + 1])
        v = [sb(f"v{u}", [P, INNER]) for u in range(2)]
        vr = [sb(f"vr{u}", [P, 4, HD]) for u in range(2)]
        p = [sb(f"p{u}", [P, HEADS, KEYS]) for u in range(2)]
        pc = [sb(f"pc{u}", [P, 4, 4, BAND]) for u in range(2)]
        nb = [sb(f"nb{u}", [P, HEADS]) for u in range(2)]
        rs = [sb(f"rs{u}", [P, HEADS]) for u in range(2)]
        rinv = [sb(f"rinv{u}", [P, HEADS]) for u in range(2)]
        pts = sb("pts", [P, 2, 512])
        bd = sb("bd", [P, 4, 4, BAND])
        ot = sb("ot", [P, HEADS // 2, P])
        xf = sb("xf", [P, 2 * P])
        st = sb("st", [P, 2, 6])
        mv = sb("mv", [P, 2, 2])
        ve = sb("ve", [P, 2])
        vh = sb("vh", [P, 2])
        vr_std = sb("vr_std", [P, 2])
        xnt = sb("xnt", [P, 2, P])
        xnf = sb("xnf", [P, 2 * P])
        gl = sb("gl", [P, 2 * P])
        hid = sb("hid", [P, NF, 2 * P])

        def banks(name, n):
            return [ctx.enter_context(nc.psum_tensor(f"w_{name}{i}", [P, 512], F32)) for i in range(n)]

        px, pt, ps = banks("px", 2), banks("pt", 2), banks("ps", 2)
        po, pm = banks("po", 1)[0], banks("pm", 1)[0]

        w_early = sem("w_early")
        w_wo = sem("w_wo")
        w_ffn = sem("w_ffn")
        consts = sem("consts")
        xs_built = sem("xs_built")
        x_full, x_done = sem("x_full"), sem("x_done")
        sq_ready, red_done = sem("sq_ready"), sem("red_done")
        kn_ready, tc_ready, rot_ready, rope_ready = sem("kn_ready"), sem("tc_ready"), sem("rot_ready"), sem("rope_ready")
        t_full, t_act, t_dve = sem("t_full"), sem("t_act"), sem("t_dve")
        s_full, s_done = sem("s_full"), sem("s_done")
        mask_ready = sem("mask_ready")
        corner_ready = sem("corner_ready")
        exp_done, rinv_ready, p_ready = sem("exp_done"), sem("rinv_ready"), sem("p_ready")
        pv_full, o_done = sem("pv_full"), sem("o_done")
        vr_ready = [sem(f"vr_ready{u}") for u in range(2)]
        m_full, m_done, g_ready = sem("m_full"), sem("m_done"), sem("g_ready")
        xf_ready, xa_ready = sem("xf_ready"), sem("xa_ready")
        link, ffn_link = sem("link"), sem("ffn_link")
        apart = sem("apart")
        CONSTS = 3 * 16

        with nc.Block() as block:
            @block.sync
            def _(sp):
                sp.dma_start(rope_tab[:], t.rope_d).then_inc(consts, 16)
                sp.dma_start(mask_tab[:], t.mask_d).then_inc(consts, 16)
                sp.dma_start(mask_odd[:], t.mask_odd_d).then_inc(consts, 16)
                sp.wait_ge(consts, CONSTS)

            @block.gpsimd
            def _(pool):
                for buf in (rope, kb, v[0], v[1], vr[0], vr[1], p[0], p[1], pc[0], pc[1], bd, rn[0], rn[1], qt, raw):
                    nc.gpsimd.memset(buf[:], 0.0)

        def m_use(pp, k):
            if isinstance(pp, int) and pp < 2:
                return 2 * pp + (k == M_WO[1])
            return 8 * pp + (k - 12)

        def m_read(pp, k):
            if isinstance(pp, int) and pp < 2:
                return 2 * pp + (k == M_WO[1])
            return 7 * pp + (min(k, M_OUT) - 10)

        M_TURN, M_BACK, M_HID0, M_HID1, M_HID2, M_OUT = 0, 1, 2, 4, 5, 6
        M_WO = (3, 7)
        M_HID = (M_HID0, M_HID1, M_HID2)

        def wide(ap, heads=8):
            return ap.unsqueeze(1).broadcast_to([P, heads, ap.shape[-1]])

        def col0(pair):
            q = pair % PAIRS
            return q * (2 * P) + q // PAIRS_B + 1

        block = ctx.enter_context(nc.Block())

        @block.sync
        def _(sp):
            def load_early(layer, slot):
                sp.dma_start(wqkv[:, bass.ds(slot, 1), :].rearrange("p s n -> p (s n)"), t.wqkv_d[bass.ds(layer, 1)].rearrange("l p n -> (l p) n")
                             ).then_inc(w_early, 16)
                for which, scale in ((0, t.qs_d), (2, t.ks_d)):
                    row = scale[bass.ds(layer, 1)]
                    for n, half in enumerate((row, row[:, HD // 2:HD], row[:, 0:HD // 2])):
                        at = which * HD + (0, HD, HD + HD // 2)[n]
                        width = half.shape[-1]
                        sp.dma_start(scales[:, bass.ds(slot, 1), at:at + width].rearrange("p s n -> p (s n)"), half.broadcast_to([P, width])
                                     ).then_inc(w_early, 16)

            def load_wo(layer):
                sp.dma_start(wo[:], t.wo_d[bass.ds(layer, 1)].rearrange("l (j p) n -> p (l j) n", p=P)
                             ).then_inc(w_wo, 16)

            def load_ffn(layer):
                one = bass.ds(layer, 1)
                sp.dma_start(w1[:], t.w1_d[one].rearrange("l p n -> (l p) n")).then_inc(w_ffn, 16)
                for n, (f, m) in enumerate(FPARTS):
                    sp.dma_start(w2[0:m, n, :], t.w2_d[one, f:f + m].rearrange("l p n -> (l p) n")).then_inc(w_ffn, 16)
                    for half in range(2):
                        src = t.b1_d[one, half * FF + f:half * FF + f + m].rearrange("l p -> p l")
                        at = half * NF + n
                        sp.dma_start(b1[0:m, at:at + 1], src).then_inc(w_ffn, 16)
                for n, vec in enumerate((t.g_d, t.b_d, t.b2_d)):
                    sp.dma_start(vecs[:, n:n + 1], vec[one].rearrange("l p -> p l")).then_inc(w_ffn, 16)

            def v_tail(pair, u):
                g = 2 * pair + u
                wait(sp, x_done, 6 * g + 6)
                wait(sp, pv_full, 2 * g + 4)
                src = v[u][P - BAND:P, :].rearrange("p (r h e d) -> p h r e d", r=2, h=4, e=2)
                for hh in range(4):
                    for r in range(2):
                        sp.dma_start(vr[u][BAND * hh:BAND * (hh + 1), 2 * r:2 * r + 2, :], src[:, hh, r]
                                     ).then_inc(vr_ready[u], 16)

            load_early(0, 0)
            load_wo(0)
            load_ffn(0)
            v_tail(0, 0)
            v_tail(0, 1)
            load_early(1, 1)
            with sp.Fori(1, PAIRS) as q:
                v_tail(q, 0)
                v_tail(q, 1)

            def layer_loads(layer, more):
                first = layer * PAIRS
                v_tail(first, 0)
                sp.wait_ge(m_full, m_use(first, M_WO[1]) + 1)
                load_wo(layer)
                v_tail(first, 1)
                v_tail(first + 1, 0)
                sp.wait_ge(xa_ready, first + PAIRS)
                load_ffn(layer)
                v_tail(first + 1, 1)
                if more:
                    load_early(layer + 1, (layer + 1) % 2)
                with sp.Fori(2, PAIRS) as q:
                    v_tail(first + q, 0)
                    v_tail(first + q, 1)

            if LAYERS > 2:
                with sp.Fori(1, LAYERS - 1) as layer:
                    layer_loads(layer, True)
            layer_loads(LAYERS - 1, False)
            v_tail(LAYERS * PAIRS, 0)
            v_tail(LAYERS * PAIRS, 1)
            for u in range(2):
                sp.wait_ge(vr_ready[u], 128 * (LAYERS * PAIRS + 1))

        steps = LAYERS * PAIRS + 2

        def over_pairs(engine, body):
            body(0)
            body(1)
            with engine.Fori(2, steps - 2) as pair:
                body(pair)
            body(steps - 2)
            body(steps - 1)

        def layer_loaded(engine, semaphore, per_layer, pair, lag):
            if isinstance(pair, int):
                layer = min(max(pair - lag, 0) // PAIRS, LAYERS - 1)
                engine.wait_ge(semaphore, per_layer * (layer + 1))
            else:
                engine.wait_ge(semaphore, ((pair + (PAIRS - lag)) // PAIRS) * per_layer)

        N_EARLY, N_WO, N_FFN = 16 * 7, 16, 16 * (1 + 3 * NF + 3)

        @block.tensor
        def _(pe):
            def qkv(pair, g, u, i):
                if i == 0:
                    layer_loaded(pe, w_early, N_EARLY, pair, 0)
                    wait(pe, xs_built, g + 1)
                wait(pe, x_done, 6 * g + i - 1)
                slot = (pair // PAIRS) % 2
                rhs = wqkv[:, bass.ds(slot, 1), i * 512:(i + 1) * 512].rearrange("p s n -> p (s n)")
                nc.tensor.matmul(px[i % 2][:], xs[u][:], rhs, start=True, stop=True).then_inc(x_full, 1)

            def t_bank(u, k):
                return pt[(9 * u + k) % 2]

            def turn_qk(g, u, i):
                wait(pe, rope_ready, 4 * g + i + 1)
                if i == 0:
                    wait(pe, t_act, 7 * g - 1)
                if i == 1:
                    wait(pe, t_act, 7 * g)
                if i >= 2:
                    wait(pe, t_act, 7 * g + i - 1)
                for j in range(4):
                    mm = nc.tensor.transpose(t_bank(u, i)[:, j * P:(j + 1) * P], rope[:, i, j * P:(j + 1) * P], t.ident[:])
                mm.then_inc(t_full, 1)

            def turn_p(g, u, i):
                k = (4, 5, 7, 8)[i]
                wait(pe, p_ready, 4 * g + i + 1)
                if i == 0:
                    wait(pe, t_dve, 2 * g + 1)
                if i == 1:
                    wait(pe, t_dve, 2 * g + 2)
                if i >= 2:
                    wait(pe, t_act, 7 * g + i + 2)
                for j in range(4):
                    mm = nc.tensor.transpose(t_bank(u, k)[:, j * P:(j + 1) * P], p[u][:, 4 * i + j, BAND:KEYS], t.ident[:])
                mm.then_inc(t_full, 1)

            def turn_corner(g, u):
                wait(pe, corner_ready, 4 * g + 4)
                wait(pe, t_act, 7 * g + 3)
                pe.sem_inc(apart, 1)
                for s in range(4):
                    src = pc[u][0:BAND, s, :, :].rearrange("p h k -> p (h k)")
                    mm = nc.tensor.transpose(t_bank(u, 6)[:, s * BAND:(s + 1) * BAND], src, t.ident[0:BAND, 0:BAND])
                mm.then_inc(t_full, 1)

            def scores(g, u, j):
                if j == 0:
                    wait(pe, t_act, 7 * g + 2)
                    wait(pe, t_dve, 2 * g + 2)
                wait(pe, s_done, 8 * g + j - 1)
                nc.tensor.matmul(ps[j % 2][:, 0:2 * KEYS], qt[:, j, :], kb[:, j, :, :].rearrange("p e k -> p (e k)"),
                                 start=True, stop=True).then_inc(s_full, 1)

            def context(pair, g, u, r):
                wait(pe, t_act, 7 * g + (5, 7)[r])
                wait(pe, o_done, 2 * g + r)
                if r == 0:
                    wait(pe, x_done, 6 * (g - 2) + 6)
                    wait(pe, vr_ready[1 - u], 128 * (pair - 1 + u))
                for j in range(4):
                    for e in range(2):
                        h = 2 * (4 * r + j) + e
                        nc.tensor.matmul(po[HD * e:HD * (e + 1), j * P:(j + 1) * P], v[u][:, h * HD:(h + 1) * HD],
                                         pts[:, (h // 4) % 2, (h % 4) * P:(h % 4 + 1) * P],
                                         start=(j == 0), stop=False, skip_group_check=True)
                for e in range(2):
                    out = po[HD * e:HD * (e + 1), :].rearrange("p (j i) -> p j i", j=4)[:, :, 0:BAND]
                    mm = nc.tensor.matmul(out, vr[1 - u][:, 2 * r + e, :], bd[:, 2 * r + e, :, :],
                                          start=False, stop=True, skip_group_check=True)
                mm.then_inc(pv_full, 1)

            def project(pair, g, u):
                if u == 0:
                    layer_loaded(pe, w_wo, N_WO, pair, 1)
                wait(pe, o_done, 2 * g + 2)
                wait(pe, m_done, m_read(pair, M_WO[u]))
                if u == 1 and not (isinstance(pair, int) and pair < 2):
                    wait(pe, xa_ready, pair + (PAIRS - 1))
                for j in range(HEADS // 2):
                    mm = nc.tensor.matmul(pm[:, 0:P], wo[:, j, :], ot[:, j, :], start=(j == 0), stop=(j == HEADS // 2 - 1))
                mm.then_inc(m_full, 1)

            def ffn(pair, k):
                if isinstance(pair, int) and pair < 2:
                    return
                wait(pe, m_done, m_read(pair, k))
                if k == M_TURN:
                    wait(pe, xf_ready, pair - 1)
                    for c in range(2):
                        mm = nc.tensor.transpose(pm[:, c * P:(c + 1) * P], xf[:, c * P:(c + 1) * P], t.ident[:])
                elif k == M_BACK:
                    for c in range(2):
                        mm = nc.tensor.transpose(pm[:, c * P:(c + 1) * P], xnt[:, c, :], t.ident[:])
                elif k == M_OUT:
                    for n, (f, m) in enumerate(FPARTS):
                        mm = nc.tensor.matmul(pm[:, 0:2 * P], w2[0:m, n, :], hid[0:m, n, :], start=(n == 0), stop=(n == NF - 1))
                else:
                    n = M_HID.index(k)
                    if n == 0:
                        layer_loaded(pe, w_ffn, N_FFN, pair, 2)
                    f, m = FPARTS[n]
                    nc.tensor.matmul(pm[0:m, 0:2 * P], w1[:, FF + f:FF + f + m], xnf[:], start=True, stop=True)
                    mm = nc.tensor.matmul(pm[0:m, 2 * P:4 * P], w1[:, f:f + m], xnf[:], start=True, stop=True)
                mm.then_inc(m_full, 1)

            def body(pair):
                for u in range(2):
                    g = 2 * pair + u
                    for i in range(4):
                        turn_qk(g, u, i)
                        qkv(pair, g, u, i)
                    ffn(pair, (M_TURN, M_HID1)[u])
                    turn_p(g, u, 0)
                    turn_p(g, u, 1)
                    turn_corner(g, u)
                    scores(g, u, 0)
                    scores(g, u, 1)
                    context(pair, g, u, 0)
                    scores(g, u, 2)
                    scores(g, u, 3)
                    ffn(pair, (M_BACK, M_HID2)[u])
                    turn_p(g, u, 2)
                    turn_p(g, u, 3)
                    scores(g, u, 4)
                    scores(g, u, 5)
                    context(pair, g, u, 1)
                    scores(g, u, 6)
                    scores(g, u, 7)
                    ffn(pair, (M_HID0, M_OUT)[u])
                    qkv(pair, g, u, 4)
                    qkv(pair, g, u, 5)
                    project(pair, g, u)

            over_pairs(pe, body)

        @block.scalar
        def _(act):
            def build_xs(pair, u):
                g = 2 * pair + u
                wait(act, xa_ready, pair + 1)
                wait(act, x_full, 6 * (g - 1))
                at = col0(pair) + u * P
                nc.scalar.copy(xs[u][0:D // 2, :], t.xa[0:D // 2, bass.ds(at, P)])
                nc.scalar.copy(xs[u][D // 2:D, :], t.xa[D // 2:D, bass.ds(at - 1, P)]).then_inc(xs_built, 1)

            def build_xf(pair):
                wait(act, m_done, m_read(pair - 1, M_WO[1]) + 1)
                at = col0(pair - 2 + PAIRS)
                nc.scalar.copy(xf[0:D // 2, :], t.xb[0:D // 2, bass.ds(at, 2 * P)])
                nc.scalar.copy(xf[D // 2:D, :], t.xb[D // 2:D, bass.ds(at - 1, 2 * P)]).then_inc(xf_ready, 1)

            def copy_raw(g, i):
                wait(act, x_full, 6 * g + i + 1)
                wait(act, rope_ready, 4 * g + i + 1)
                nc.scalar.copy(raw[:, i, :], px[i % 2][:]).then_inc(x_done, 1)

            def copy_v(pair, g, u, i):
                wait(act, x_full, 6 * g + i + 1)
                wait(act, pv_full, 2 * g + 2)
                wait(act, vr_ready[u], 128 * pair)
                nc.scalar.copy(v[u][:, (i - 4) * 512:(i - 3) * 512], px[i % 2][:]).then_inc(x_done, 1)

            def t_bank(u, k):
                return pt[(9 * u + k) % 2]

            def copy_qt(g, u, i):
                wait(act, t_full, 9 * g + i + 1)
                wait(act, s_full, 8 * g)
                nc.scalar.copy(qt[:, 4 * i:4 * i + 4, :].rearrange("p j n -> p (j n)"), t_bank(u, i)[:]).then_inc(t_act, 1)

            def copy_pt(g, u, i):
                wait(act, t_full, 9 * g + (4, 5, 7, 8)[i] + 1)
                wait(act, pv_full, 2 * g + i // 2)
                nc.scalar.copy(pts[:, i % 2, :], t_bank(u, (4, 5, 7, 8)[i])[:]).then_inc(t_act, 1)

            def copy_corner(g, u):
                wait(act, t_full, 9 * g + 7)
                wait(act, pv_full, 2 * g)
                for hh in range(4):
                    rows = slice(BAND * hh, BAND * (hh + 1))
                    src = t_bank(u, 6)[rows, 0:P].rearrange("p (s i) -> p s i", s=4)
                    last = nc.scalar.copy(bd[rows, :, hh, :], src)
                last.then_inc(t_act, 1)

            def exps(g, u, q):
                wait(act, s_done, 8 * g + 2 * q + 2)
                for h in range(4 * q, 4 * q + 4):
                    last = nc.scalar.activation(p[1 - u][:, h, :], p[1 - u][:, h, :], ACT.Exp, bias=nb[u][:, h:h + 1],
                                                scale=-1.0, accum_out=rs[u][:, h:h + 1])
                last.then_inc(exp_done, 1)

            def copy_context(pair, g, u, r):
                wait(act, pv_full, 2 * g + r + 1)
                if not isinstance(g, int) or g > 0:
                    wait(act, m_full, m_use(pair - 1 + u, M_WO[1 - u]) + 1)
                nc.scalar.copy(ot[:, 4 * r:4 * r + 4, :].rearrange("p j n -> p (j n)"), po[:]).then_inc(o_done, 1)

            def ffn(pair, k):
                if isinstance(pair, int) and pair < 2:
                    return
                wait(act, m_full, m_use(pair, k) + 1)
                if k == M_BACK:
                    layer_loaded(act, w_ffn, N_FFN, pair, 2)
                    nc.scalar.activation(xnf[:], pm[:, 0:2 * P], ACT.Identity, bias=vecs[:, 1:2], scale=vecs[:, 0:1]
                                         ).then_inc(m_done, 1)
                else:
                    n = M_HID.index(k)
                    m = FPARTS[n][1]
                    nc.scalar.activation(gl[0:m, :], pm[0:m, 0:2 * P], ACT.Gelu, bias=b1[0:m, NF + n:NF + n + 1]
                                         ).then_inc(g_ready, 1)

            def body(pair):
                for u in range(2):
                    g = 2 * pair + u
                    if u == 0 and not (isinstance(pair, int) and pair < 2):
                        build_xf(pair)
                    copy_qt(g, u, 0)
                    copy_raw(g, 0)
                    copy_qt(g, u, 1)
                    for i in range(1, 4):
                        copy_raw(g, i)
                    if u == 1:
                        ffn(pair, M_HID1)
                    copy_pt(g, u, 0)
                    copy_pt(g, u, 1)
                    copy_corner(g, u)
                    exps(g, u, 0)
                    copy_context(pair, g, u, 0)
                    exps(g, u, 1)
                    ffn(pair, (M_BACK, M_HID2)[u])
                    copy_pt(g, u, 2)
                    copy_pt(g, u, 3)
                    exps(g, u, 2)
                    copy_context(pair, g, u, 1)
                    exps(g, u, 3)
                    if u == 0:
                        ffn(pair, M_HID0)
                    build_xs(pair + u, 1 - u)
                    copy_v(pair, g, u, 4)
                    copy_v(pair, g, u, 5)

            build_xs(0, 0)
            over_pairs(act, body)

        @block.gpsimd
        def _(pool):
            def squares(g, i):
                wait(pool, x_done, 6 * g + i + 1)
                wait(pool, red_done, 4 * g + i - 1)
                nc.gpsimd.tensor_tensor(sq[:, i % 2, :], raw[:, i, :], raw[:, i, :], ALU.mult).then_inc(sq_ready, 1)

            def tables(pair, g, u):
                layer_loaded(pool, w_early, N_EARLY, pair, 0)
                wait(pool, rope_ready, 4 * g)
                pos = (pair % PAIRS_B) * 2 + u
                slot = (pair // PAIRS) % 2
                nc.gpsimd.tensor_tensor(tc[u][:], rope_tab[:, bass.ds(pos, 1), :].rearrange("p s n -> p (s n)"),
                                        scales[:, bass.ds(slot, 1), :].rearrange("p s n -> p (s n)"), ALU.mult
                                        ).then_inc(tc_ready, 1)

            def choose_mask(pair, g):
                wait(pool, s_done, 8 * g)
                pos = pair % PAIRS_B
                nc.gpsimd.tensor_copy(mask[:], mask_tab[:, bass.ds(pos, 1), :].rearrange("p s n -> p (s n)")
                                      ).then_inc(mask_ready, 1)

            def rotated(g, u, i):
                if i >= 2:
                    wait(pool, kn_ready, 2 * g + i - 1)
                if i == 0:
                    wait(pool, tc_ready, g + 1)
                wait(pool, rope_ready, 4 * g + i + 1)
                hh = HD // 2
                src = raw[:, i, :].rearrange("p (h d) -> p h d", d=HD)
                dst = rot[:, i, :].rearrange("p (h d) -> p h d", d=HD)
                tab = tc[u][:, (1 + 2 * (i // 2)) * HD:(2 + 2 * (i // 2)) * HD]
                nc.gpsimd.tensor_tensor(dst[:, :, 0:hh], src[:, :, hh:HD], wide(tab[:, 0:hh]), ALU.mult)
                nc.gpsimd.tensor_tensor(dst[:, :, hh:HD], src[:, :, 0:hh], wide(tab[:, hh:HD]), ALU.mult
                                        ).then_inc(rot_ready, 1)

            def normalise(g, u, q):
                wait(pool, rinv_ready, 4 * g + q + 1)
                heads = p[1 - u][:, 4 * q:4 * q + 4, BAND:KEYS]
                nc.gpsimd.tensor_tensor(heads, heads, rinv[u][:, 4 * q:4 * q + 4].unsqueeze(2).broadcast_to([P, 4, P]),
                                        ALU.mult).then_inc(p_ready, 1)
                r, hh = q // 2, 2 * (q % 2)
                corner = pc[1 - u][:, 2 * r:2 * r + 2, hh:hh + 2, :].rearrange("p e h k -> p h e k")
                nc.gpsimd.tensor_tensor(corner, p[1 - u][:, 4 * q:4 * q + 4, 0:BAND].rearrange("p (h e) k -> p h e k", e=2),
                                        rinv[u][:, 4 * q:4 * q + 4].rearrange("p (h e) -> p h e", e=2).unsqueeze(3)
                                        .broadcast_to([P, 2, 2, BAND]), ALU.mult).then_inc(corner_ready, 1)

            pool.sem_inc(p_ready, 4)
            pool.sem_inc(corner_ready, 4)

            def body(pair):
                for u in range(2):
                    g = 2 * pair + u
                    if u == 1:
                        choose_mask(pair, g)
                    for i in range(4):
                        squares(g, i)
                    tables(pair, g, u)
                    rotated(g, u, 0)
                    rotated(g, u, 1)
                    normalise(g, u, 0)
                    normalise(g, u, 1)
                    rotated(g, u, 2)
                    rotated(g, u, 3)
                    normalise(g, u, 2)
                    normalise(g, u, 3)

            over_pairs(pool, body)

        @block.vector
        def _(dve):
            def t_bank(u, k):
                return pt[(9 * u + k) % 2]

            def linked(instruction, value):
                instruction.then_inc(link, 1)
                dve.wait_ge(link, value)

            def carry(pair, g, u):
                wait(dve, s_full, 8 * g)
                flat = kb[:].rearrange("p j e k -> p (j e) k")
                if u == 1:
                    wait(dve, mask_ready, pair + 1)
                    ins = nc.vector.tensor_scalar(flat[:, :, 0:BAND], flat[:, :, P:KEYS], mask[:, KEYS:KEYS + 1], None, ALU.mult)
                else:
                    ins = nc.vector.tensor_copy(flat[:, :, 0:BAND], flat[:, :, P:KEYS])
                linked(ins, 1)

            def copy_kb(g, u, i):
                wait(dve, t_full, 9 * g + i + 1)
                for e in range(2):
                    rows = slice(HD * e, HD * (e + 1))
                    last = nc.vector.tensor_copy(kb[rows, 4 * (i - 2):4 * (i - 1), e, BAND:KEYS],
                                                 t_bank(u, i)[rows, :].rearrange("p (j n) -> p j n", j=4))
                last.then_inc(t_dve, 1)

            def head_norms(g, i):
                wait(dve, sq_ready, 4 * g + i + 1)
                nc.vector.tensor_reduce(ss[:, 8 * i:8 * i + 8], sq[:, i % 2, :].rearrange("p (h d) -> p h d", d=HD),
                                        AX.X, ALU.add).then_inc(red_done, 1)

            def norm_factors(g, u):
                wait(dve, red_done, 4 * g + 4)
                linked(nc.vector.tensor_scalar(ss[:], ss[:], 1e-24, None, ALU.max), 2)
                rsqrt_steps(nc, dve, link, 2, rn[u][:], ss[:], nhalf[:], 2 * HEADS)
                linked(nc.vector.tensor_scalar(rn[u][:, 0:HEADS], rn[u][:, 0:HEADS], -SIM_SCALE, None, ALU.mult), 14)

            def masked_scores(pair, g, u, j):
                wait(dve, s_full, 8 * g + j + 1)
                if j == 0:
                    wait(dve, t_full, 9 * g)
                dve.sem_inc(apart, 1)
                m = mask[:, 0:KEYS] if u == 1 else mask_odd[:]
                for e in range(2):
                    h = 2 * j + e
                    last = nc.vector.tensor_tensor_reduce(p[1 - u][:, h, :], ps[j % 2][:, e * KEYS:(e + 1) * KEYS], m,
                                                          rn[1 - u][:, h:h + 1], 3e38, ALU.add, ALU.min,
                                                          nb[u][:, h:h + 1])
                last.then_inc(s_done, 1)

            def inverse_sums(g, u, q):
                wait(dve, exp_done, 4 * g + q + 1)
                nc.vector.reciprocal(rinv[u][:, 4 * q:4 * q + 4], rs[u][:, 4 * q:4 * q + 4]).then_inc(rinv_ready, 1)

            def k_normalised(g, u, i):
                heads = raw[:, i, :].rearrange("p (h d) -> p h d", d=HD)
                nc.vector.tensor_tensor(heads, heads, rn[u][:, 8 * i:8 * i + 8].unsqueeze(2).broadcast_to([P, 8, HD]),
                                        ALU.mult).then_inc(kn_ready, 1)

            def straight(g, u, i):
                if i == 0:
                    wait(dve, tc_ready, g + 1)
                if i >= 2:
                    wait(dve, kn_ready, 2 * g + i - 1)
                wait(dve, t_full, 9 * g + i + 1)
                nc.vector.tensor_tensor(rope[:, i, :].rearrange("p (h d) -> p h d", d=HD),
                                        raw[:, i, :].rearrange("p (h d) -> p h d", d=HD),
                                        wide(tc[u][:, 2 * (i // 2) * HD:(2 * (i // 2) + 1) * HD]), ALU.mult
                                        ).then_inc(link, 1)

            def add_rotated(g, i):
                dve.wait_ge(link, 14 + i + 1)
                wait(dve, rot_ready, 4 * g + i + 1)
                nc.vector.tensor_tensor(rope[:, i, :], rope[:, i, :], rot[:, i, :], ALU.add).then_inc(rope_ready, 1)

            def add_attention(pair, g, u):
                wait(dve, m_full, m_use(pair, M_WO[u]) + 1)
                at = col0(pair - 1 + PAIRS) + u * P
                nc.vector.tensor_tensor(t.xb[:, bass.ds(at, P)], pm[:, 0:P], t.xa[:, bass.ds(at, P)], ALU.add
                                        ).then_inc(m_done, 1)

            def ffn(pair, k):
                if isinstance(pair, int) and pair < 2:
                    return
                wait(dve, m_full, m_use(pair, k) + 1)
                if k == M_TURN:
                    at = 18
                    for c in range(2):
                        nc.vector.bn_stats(st[:, c, :], pm[:, c * P:(c + 1) * P]).then_inc(ffn_link, 1)
                    for c in range(2):
                        dve.wait_ge(ffn_link, c + 1)
                        nc.vector.bn_aggr(mv[:, c, :], st[:, c, :]).then_inc(ffn_link, 1)
                    dve.wait_ge(ffn_link, 4)
                    nc.vector.tensor_scalar(ve[:], mv[:, :, 1], 1e-5, None, ALU.add).then_inc(ffn_link, 1)
                    dve.wait_ge(ffn_link, 5)
                    rsqrt_steps(nc, dve, ffn_link, 5, vr_std[:], ve[:], vh[:], 2)
                    for c in range(2):
                        last = nc.vector.tensor_scalar(xnt[:, c, :], pm[:, c * P:(c + 1) * P], mv[:, c, 0:1],
                                                       vr_std[:, c:c + 1], ALU.subtract, ALU.mult)
                    last.then_inc(m_done, 1)
                elif k == M_OUT:
                    wait(dve, xs_built, 2 * pair - 1)
                    at = col0(pair - 2 + PAIRS)
                    nc.vector.scalar_tensor_tensor(t.xa[:, bass.ds(at, 2 * P)], pm[:, 0:2 * P], vecs[:, 2:3],
                                                   t.xb[:, bass.ds(at, 2 * P)], ALU.add, ALU.add).then_inc(xa_ready, 1)
                else:
                    n = M_HID.index(k)
                    m = FPARTS[n][1]
                    wait(dve, g_ready, NF * pair + (n + 1 - 2 * NF))
                    nc.vector.scalar_tensor_tensor(hid[0:m, n, :], pm[0:m, 2 * P:4 * P], b1[0:m, n:n + 1], gl[0:m, :],
                                                   ALU.add, ALU.mult).then_inc(m_done, 1)

            dve.sem_inc(rope_ready, 4)
            dve.sem_inc(xa_ready, PAIRS)

            def body(pair):
                for u in range(2):
                    g = 2 * pair + u
                    dve.sem_clear(link)
                    if u == 0:
                        dve.sem_clear(ffn_link)
                    carry(pair, g, u)
                    copy_kb(g, u, 2)
                    copy_kb(g, u, 3)
                    ffn(pair, (M_TURN, M_HID1)[u])
                    masked_scores(pair, g, u, 0)
                    masked_scores(pair, g, u, 1)
                    head_norms(g, 0)
                    head_norms(g, 1)
                    masked_scores(pair, g, u, 2)
                    masked_scores(pair, g, u, 3)
                    head_norms(g, 2)
                    head_norms(g, 3)
                    inverse_sums(g, u, 0)
                    if u == 1:
                        ffn(pair, M_HID2)
                    norm_factors(g, u)
                    masked_scores(pair, g, u, 4)
                    masked_scores(pair, g, u, 5)
                    inverse_sums(g, u, 1)
                    k_normalised(g, u, 2)
                    k_normalised(g, u, 3)
                    straight(g, u, 0)
                    straight(g, u, 1)
                    masked_scores(pair, g, u, 6)
                    masked_scores(pair, g, u, 7)
                    inverse_sums(g, u, 2)
                    ffn(pair, (M_HID0, M_OUT)[u])
                    straight(g, u, 2)
                    straight(g, u, 3)
                    inverse_sums(g, u, 3)
                    add_attention(pair, g, u)
                    for i in range(4):
                        add_rotated(g, i)

            over_pairs(dve, body)


def finish(nc, t):
    with ExitStack() as ctx:
        turned = [ctx.enter_context(nc.psum_tensor(f"fin_turned{i}", [P, 512], F32)) for i in range(2)]
        full = ctx.enter_context(nc.semaphore("fin_full"))
        summed = ctx.enter_context(nc.semaphore("fin_summed"))
        stored = ctx.enter_context(nc.semaphore("fin_stored"))
        block = ctx.enter_context(nc.Block())
        out = t.out.rearrange("b (c p) d -> p (b c) d", p=P)

        @block.tensor
        def _(pe):
            for n in range(CHUNKS // 4):
                if n >= 2:
                    pe.wait_ge(summed, n - 1)
                at = 4 * n * P + (4 * n) // (S // P) + 1
                for k in range(4):
                    mm = nc.tensor.transpose(turned[n % 2][:, k * P:(k + 1) * P], t.xa[:, at + k * P:at + (k + 1) * P], t.ident[:])
                mm.then_inc(full, 1)

        @block.vector
        def _(dve):
            for n in range(CHUNKS // 4):
                dve.wait_ge(full, n + 1)
                chunk = t.xtok[:, 4 * n:4 * n + 4, :].rearrange("p c d -> p (c d)")
                nc.vector.tensor_tensor(chunk, turned[n % 2][:], chunk, ALU.add).then_inc(summed, 1)

        @block.sync
        def _(sp):
            for n in range(CHUNKS // 4):
                sp.wait_ge(summed, n + 1)
                sp.dma_start(out[:, 4 * n:4 * n + 4, :], t.xtok[:, 4 * n:4 * n + 4, :]).then_inc(stored, 16)
            sp.wait_ge(stored, 16 * (CHUNKS // 4))


class Tensors:
    pass


def build(nc, t, with_attention=True):
    t.q_parts_d = nc.dram_tensor("q_parts", (3, D, B * S), BF16, kind="Internal").ap()
    t.k_parts_d = nc.dram_tensor("k_parts", (3, D, B * S), BF16, kind="Internal").ap()
    with ExitStack() as ctx:
        def sb(name, shape):
            return ctx.enter_context(nc.sbuf_tensor(name, shape, F32))

        t.xtok = sb("xtok", [P, CHUNKS, D])
        t.xa = sb("xa", [P, COLS])
        t.xb = sb("xb", [P, COLS])
        t.ident = sb("ident", [P, P])
        prepare(nc, t)
        if with_attention:
            attention(nc, t)
        windowed(nc, t)
        finish(nc, t)


def shape_constants():
    f = np.float32
    half = np.arange(0, HD, 2, dtype=f)
    inv_freq = (f(1.0) / f(10000.0) ** (half / f(HD))).astype(f)
    tok = np.arange(S, dtype=f)
    freqs = tok[:, None] * inv_freq[None, :]
    freqs = np.concatenate([freqs, freqs], -1)
    base = (half + f(0.4 * HD)) / f(1.4 * HD)
    power = (tok - f(S // 2)) / f(BAND // 2)
    scale = base[None, :] ** power[:, None]
    scale = np.concatenate([scale, scale], -1).astype(f)
    cos, sin = np.cos(freqs).astype(f), np.sin(freqs).astype(f)
    sign = np.where(np.arange(HD) < HD // 2, -1, 1).astype(f)
    inv = f(1.0) / scale
    tab = np.concatenate([cos * scale, sin * scale * sign, cos * inv, sin * inv * sign], 1)
    rope = np.ascontiguousarray(tab.reshape(S // P, P, 4 * HD).transpose(1, 0, 2)).astype(f)
    i, j = np.arange(P)[:, None], np.arange(KEYS)[None, :] - BAND
    odd = np.where((j <= i) & (i <= j + BAND), 0.0, MASKED).astype(f)
    first = np.where(j < 0, f(MASKED), odd).astype(f)
    masks = np.ones((P, PAIRS_B, KEYS + 1), f)
    masks[:, :, :KEYS] = odd[:, None, :]
    masks[:, 0, :KEYS] = first
    masks[:, 0, KEYS] = 0.0
    later = np.where(np.arange(P)[None, :] > np.arange(P)[:, None], f(MASKED), f(0.0)).astype(f)
    return {"ident": np.eye(P, dtype=f), "rope_tab": rope, "mask_tab": masks, "mask_odd": odd,
            "a_masks": np.ascontiguousarray(np.stack([later, later.T], 1))}


_INS = {"L0_attn_x": "x", "L0_attn_W_qkv": "awqkv_d", "L0_attn_q_scale": "aqs_d", "L0_attn_k_scale": "aks_d",
        "L0_attn_W_out": "awout_d", "L0_ffn_Wqkv": "wqkv_d", "L0_ffn_q_scale": "qs_d", "L0_ffn_k_scale": "ks_d",
        "L0_ffn_Wo": "wo_d", "L0_ffn_ln_g": "g_d", "L0_ffn_ln_b": "b_d", "L0_ffn_W1": "w1_d", "L0_ffn_b1": "b1_d",
        "L0_ffn_W2": "w2_d", "L0_ffn_b2": "b2_d"}
_CONSTS = {"ident": "ident_d", "rope_tab": "rope_d", "mask_tab": "mask_d", "mask_odd": "mask_odd_d",
           "a_masks": "amasks_d"}


def kernel(**inputs):
    import concourse.bacc as bacc
    from concourse.bass_utils import run_bass_kernel_spmd

    nc = bacc.Bacc("TRN2", target_bir_lowering=False, num_devices=1)
    t = Tensors()
    arrays = {}

    def dram_in(name, a):
        arrays[name] = a
        return nc.dram_tensor(name, a.shape, mybir.dt.from_np(a.dtype), kind="ExternalInput").ap()

    d = {}
    for name in _INS:
        d[_INS[name]] = dram_in("in_" + name, np.ascontiguousarray(inputs[name]))
    for name, a in shape_constants().items():
        d[_CONSTS[name]] = dram_in("const_" + name, a)
    t.__dict__.update(d)
    t.out = nc.dram_tensor("out", (B, S, D), F32, kind="ExternalOutput").ap()
    build(nc, t)
    r = run_bass_kernel_spmd(nc, [arrays], core_ids=[0])
    return r.results[0]["out"]
```

```python
from contextlib import ExitStack

import numpy as np
import concourse.bass as bass
from concourse import mybir

F32 = mybir.dt.float32
BF16 = mybir.dt.bfloat16
I32 = mybir.dt.int32
ALU = mybir.AluOpType
ACT = mybir.ActivationFunctionType
AX = mybir.AxisListType

P = 128
B, S, D = 4, 1024, 128
CHUNKS = B * S // P
PAIRS = CHUNKS // 2
PAIRS_B = PAIRS // B
COLS = B * (S + 1)

AHD = 8
AG = 4
GROUPS = D // AHD // AG

LAYERS = 6
HEADS, HD = 16, 64
INNER = HEADS * HD
BAND = 32
KEYS = BAND + P
SIM_SCALE = 8.0
FF = int(D * 4 * 2 / 3)
FPARTS = [(f, min(P, FF - f)) for f in range(0, FF, P)]
NF = len(FPARTS)
MASKED = -1e30
RSQRT_MAGIC = float(0x5F3759DF)


def wait(engine, semaphore, value):
    if isinstance(value, int) and value <= 0:
        return
    engine.wait_ge(semaphore, value)


RSQRT_STEPS = 2 + 3 * 3


def rsqrt_step(nc, n, y, x, half):
    v = nc.vector
    if n == 0:
        return v.tensor_scalar(y.bitcast(I32), x.bitcast(I32), 1, None, ALU.logical_shift_right)
    if n == 1:
        return v.tensor_scalar(y.bitcast(I32), y.bitcast(I32), -1.0, RSQRT_MAGIC, ALU.mult, ALU.add)
    if n % 3 == 2:
        return v.tensor_tensor(half, y, y, ALU.mult)
    if n % 3 == 0:
        return v.scalar_tensor_tensor(half, half, -0.5, x, ALU.mult, ALU.mult)
    return v.scalar_tensor_tensor(y, half, 1.5, y, ALU.add, ALU.mult)


def rsqrt_steps(nc, dve, link, link_from, y, x, half):
    for n in range(RSQRT_STEPS):
        rsqrt_step(nc, n, y, x, half).then_inc(link, 1)
        dve.wait_ge(link, link_from + n + 1)


def prepare(nc, t):
    with ExitStack() as ctx:
        stats = ctx.enter_context(nc.sbuf_tensor("pre_stats", [P, CHUNKS, 6], F32))
        mean_var = ctx.enter_context(nc.sbuf_tensor("pre_mean_var", [P, CHUNKS, 2], F32))
        var = ctx.enter_context(nc.sbuf_tensor("pre_var", [P, CHUNKS], F32))
        rstd = ctx.enter_context(nc.sbuf_tensor("pre_rstd", [P, CHUNKS], F32))
        half = ctx.enter_context(nc.sbuf_tensor("pre_half", [P, CHUNKS], F32))
        xn = ctx.enter_context(nc.sbuf_tensor("pre_xn", [P, CHUNKS, D], F32))
        turned = [ctx.enter_context(nc.psum_tensor(f"pre_turned{i}", [P, 512], F32)) for i in range(2)]
        x_loaded = ctx.enter_context(nc.semaphore("pre_x_loaded"))
        stats_done = ctx.enter_context(nc.semaphore("pre_stats_done"))
        link = ctx.enter_context(nc.semaphore("pre_link"))
        xn_done = ctx.enter_context(nc.semaphore("pre_xn_done"))
        turned_full = ctx.enter_context(nc.semaphore("pre_turned_full"))
        turned_read = ctx.enter_context(nc.semaphore("pre_turned_read"))
        padded = ctx.enter_context(nc.semaphore("pre_padded"))
        block = ctx.enter_context(nc.Block())

        @block.sync
        def _(sp):
            sp.dma_start(t.xtok[:], t.x.rearrange("b (c p) d -> p (b c) d", p=P)).then_inc(x_loaded, 16)
            sp.dma_start(t.ident[:], t.ident_d).then_inc(x_loaded, 16)
            sp.wait_ge(x_loaded, 32)

        @block.vector
        def _(dve):
            dve.wait_ge(x_loaded, 32)
            for c in range(CHUNKS):
                nc.vector.bn_stats(stats[:, c, :], t.xtok[:, c, :]).then_inc(stats_done, 1)
            for c in range(CHUNKS):
                dve.wait_ge(stats_done, c + 1)
                nc.vector.bn_aggr(mean_var[:, c, :], stats[:, c, :]).then_inc(stats_done, 1)
            dve.wait_ge(stats_done, 2 * CHUNKS)
            nc.vector.tensor_scalar(var[:], mean_var[:, :, 1], 1e-5, None, ALU.add).then_inc(link, 1)
            dve.wait_ge(link, 1)
            rsqrt_steps(nc, dve, link, 1, rstd[:], var[:], half[:])
            for c in range(CHUNKS):
                nc.vector.tensor_scalar(xn[:, c, :], t.xtok[:, c, :], mean_var[:, c, 0:1], rstd[:, c:c + 1],
                                        ALU.subtract, ALU.mult).then_inc(xn_done, 1)

        @block.tensor
        def _(pe):
            for n in range(CHUNKS // 4):
                pe.wait_ge(xn_done, 4 * n + 4)
                if n >= 2:
                    pe.wait_ge(turned_read, n - 1)
                for k in range(4):
                    mm = nc.tensor.transpose(turned[n % 2][:, k * P:(k + 1) * P], xn[:, 4 * n + k, :], t.ident[:])
                mm.then_inc(turned_full, 1)

        @block.scalar
        def _(act):
            act.wait_ge(padded, 1)
            for n in range(CHUNKS // 4):
                at = 4 * n * P + (4 * n) // (S // P) + 1
                act.wait_ge(turned_full, n + 1)
                nc.scalar.copy(t.xa[:, at:at + 512], turned[n % 2][:]).then_inc(turned_read, 1)

        @block.gpsimd
        def _(pool):
            nc.gpsimd.memset(t.xa[:], 0.0).then_inc(padded, 1)
            nc.gpsimd.memset(t.xb[:], 0.0).then_inc(padded, 1)


def attention(nc, t):
    N_TURNS = 2 * B * S // 512
    with ExitStack() as ctx:
        def sb(name, shape, dt=F32):
            return ctx.enter_context(nc.sbuf_tensor("a_" + name, shape, dt))

        def sem(name):
            return ctx.enter_context(nc.semaphore("a_" + name))

        v_all = sb("v_all", [P, CHUNKS, D])
        w_out = sb("w_out", [P, D])
        ident_bf = sb("ident_bf", [P, P], BF16)
        mask_qk = sb("mask_qk", [P, P], BF16)
        mask_kq = sb("mask_kq", [P, P], BF16)
        q_stack = [sb(f"q_stack{n}", [P, AG, S], BF16) for n in range(GROUPS)]
        k_stack = [sb(f"k_stack{n}", [P, AG, S], BF16) for n in range(GROUPS)]
        v_pad = [sb(f"v_pad{n}", [P, S // P, AG, BAND]) for n in range(2)]
        neg_max = sb("neg_max", [P, S // P, AG, BAND], BF16)

        with ExitStack() as pre:
            def psb(name, shape, dt=F32):
                return pre.enter_context(nc.sbuf_tensor("ap_" + name, shape, dt))

            def psem(name):
                return pre.enter_context(nc.semaphore("ap_" + name))

            wqkv = psb("wqkv", [P, 3 * D])
            masks = psb("masks", [P, 2, P])
            qk = psb("qk", [P, 2, CHUNKS, D])
            stats = psb("stats", [P, 2 * CHUNKS, 6])
            mean_var = psb("mean_var", [P, 2 * CHUNKS, 2])
            var = psb("var", [P, 2 * CHUNKS])
            rstd = psb("rstd", [P, 2 * CHUNKS])
            half = psb("half", [P, 2 * CHUNKS])
            cols = psb("cols", [P, 2])
            full = [psb(f"full{n}", [P, 512]) for n in range(2)]
            parts = [psb(f"parts{n}", [P, 3, 512], BF16) for n in range(2)]
            rest = [psb(f"rest{n}", [P, 512]) for n in range(2)]
            bank = [pre.enter_context(nc.psum_tensor(f"ap_bank{n}", [P, 512], F32)) for n in range(4)]
            loaded, proj_full, proj_read, stats_done = psem("loaded"), psem("proj_full"), psem("proj_read"), psem("stats_done")
            link, normal, cols_ready, filled = psem("link"), psem("normal"), psem("cols_ready"), psem("filled")
            turned, scaled, rested, parted, last_part = (psem("turned"), psem("scaled"), psem("rested"), psem("parted"),
                                                         psem("last_part"))
            stored = [psem(f"stored{n}") for n in range(2)]
            LOADED = 16 * 5
            block = pre.enter_context(nc.Block())

            @block.sync
            def _(sp):
                sp.dma_start(wqkv[:], t.awqkv_d).then_inc(loaded, 16)
                sp.dma_start(w_out[:], t.awout_d).then_inc(loaded, 16)
                sp.dma_start(cols[:, 0:1], t.aqs_d.unsqueeze(1)).then_inc(loaded, 16)
                sp.dma_start(cols[:, 1:2], t.aks_d.unsqueeze(1)).then_inc(loaded, 16)
                sp.dma_start(masks[:], t.amasks_d).then_inc(loaded, 16)
                for n in range(N_TURNS):
                    sp.wait_ge(last_part, n + 1)
                    dst = (t.q_parts_d, t.k_parts_d)[n % 2][:, :, (n // 2) * 512:(n // 2 + 1) * 512]
                    sp.dma_start(dst.rearrange("a f t -> f a t"), parts[n % 2][:]).then_inc(stored[n % 2], 16)
                for n in range(2):
                    sp.wait_ge(stored[n], 16 * (N_TURNS // 2))

            @block.tensor
            def _(pe):
                pe.wait_ge(loaded, LOADED)
                for c in range(CHUNKS):
                    if c >= 4:
                        pe.wait_ge(stats_done, 2 * (c - 3))
                    at = c * P + c // (S // P) + 1
                    nc.tensor.matmul(bank[c % 4][:, 0:3 * D], t.xa[:, at:at + P], wqkv[:], start=True, stop=True
                                     ).then_inc(proj_full, 1)
                pe.wait_ge(stats_done, 2 * CHUNKS)
                for n in range(N_TURNS):
                    if n >= 4:
                        pe.wait_ge(scaled, n - 3)
                    pe.wait_ge(normal, 4 * n + 4)
                    for k in range(4):
                        mm = nc.tensor.transpose(bank[n % 4][:, k * P:(k + 1) * P], qk[:, n % 2, 4 * (n // 2) + k, :], t.ident[:])
                    mm.then_inc(turned, 1)

            @block.vector
            def _(dve):
                for c in range(CHUNKS):
                    dve.wait_ge(proj_full, c + 1)
                    dve.wait_ge(proj_read, c + 1)
                    for w in range(2):
                        nc.vector.bn_stats(stats[:, 2 * c + w, :], bank[c % 4][:, w * D:(w + 1) * D]).then_inc(stats_done, 1)
                for c in range(2 * CHUNKS):
                    dve.wait_ge(stats_done, c + 1)
                    nc.vector.bn_aggr(mean_var[:, c, :], stats[:, c, :]).then_inc(link, 1)
                dve.wait_ge(link, 2 * CHUNKS)
                nc.vector.tensor_scalar(var[:], mean_var[:, :, 1], 1e-6, None, ALU.add).then_inc(link, 1)
                dve.wait_ge(link, 2 * CHUNKS + 1)
                rsqrt_steps(nc, dve, link, 2 * CHUNKS + 1, rstd[:], var[:], half[:])
                dve.wait_ge(loaded, LOADED)
                nc.vector.tensor_scalar(cols[:, 0:1], cols[:, 0:1], float(AHD) ** -0.5, None, ALU.mult).then_inc(cols_ready, 1)
                for n in range(N_TURNS):
                    for k in range(4):
                        c, w = 4 * (n // 2) + k, n % 2
                        m = 2 * c + w
                        nc.vector.tensor_scalar(qk[:, w, c, :], qk[:, w, c, :], mean_var[:, m, 0:1], rstd[:, m:m + 1],
                                                ALU.subtract, ALU.mult).then_inc(normal, 1)
                dve.wait_ge(filled, 1)
                for n in range(GROUPS):
                    nc.vector.memset(k_stack[n][96:99, :, :], 1.0)
                for n in range(2):
                    nc.vector.memset(v_pad[n][:, :, :, AHD:AHD + 1], 1.0)

            @block.scalar
            def _(act):
                act.wait_ge(loaded, LOADED)
                nc.scalar.copy(ident_bf[:], t.ident[:])
                nc.scalar.copy(mask_qk[:], masks[:, 0, :])
                nc.scalar.copy(mask_kq[:], masks[:, 1, :])
                for c in range(CHUNKS):
                    act.wait_ge(proj_full, c + 1)
                    nc.scalar.copy(qk[:, :, c, :], bank[c % 4][:, 0:2 * D].rearrange("p (w d) -> p w d", w=2))
                    nc.scalar.copy(v_all[:, c, :], bank[c % 4][:, 2 * D:3 * D]).then_inc(proj_read, 1)
                act.wait_ge(cols_ready, 1)
                for n in range(N_TURNS):
                    s = n % 2
                    act.wait_ge(turned, n + 1)
                    if n >= 2:
                        act.wait_ge(rested, n - 1)
                        act.wait_ge(stored[s], 16 * (n // 2))
                    nc.scalar.activation(full[s][:], bank[n % 4][:], ACT.Copy, scale=cols[:, s:s + 1]).then_inc(scaled, 1)
                    act.wait_ge(scaled, n + 1)
                    nc.scalar.copy(parts[s][:, 0, :], full[s][:]).then_inc(parted, 1)
                    if n >= 1:
                        act.wait_ge(rested, n)
                        nc.scalar.copy(parts[1 - s][:, 1, :], rest[1 - s][:]).then_inc(parted, 1)
                act.wait_ge(rested, N_TURNS)
                nc.scalar.copy(parts[1][:, 1, :], rest[1][:]).then_inc(parted, 1)

            @block.gpsimd
            def _(pool):
                for buf in (*k_stack, *v_pad, *q_stack, neg_max):
                    last = nc.gpsimd.memset(buf[:], 0.0)
                last.then_inc(filled, 1)
                for n in range(N_TURNS + 1):
                    if n < N_TURNS:
                        s = n % 2
                        pool.wait_ge(parted, max(2 * n, 1))
                        nc.gpsimd.tensor_tensor(rest[s][:], full[s][:], parts[s][:, 0, :], ALU.subtract).then_inc(rested, 1)
                    if n >= 1:
                        s = (n - 1) % 2
                        pool.wait_ge(parted, min(2 * n + 1, 2 * N_TURNS))
                        nc.gpsimd.tensor_tensor(parts[s][:, 2, :], rest[s][:], parts[s][:, 1, :], ALU.subtract
                                                ).then_inc(last_part, 1)

        probs = [sb(f"probs{n}", [P, AG, S]) for n in range(2)]
        row_max = sb("row_max", [P, AG, S // P])
        max_b = sb("max_b", [P, AG, S // P])
        max_rest = sb("max_rest", [P, AG, S // P])
        ctx_t = sb("ctx_t", [P, S])
        inv = sb("inv", [P, 2, 4, AG])
        ctx_tok = sb("ctx_tok", [P, S // P, D])
        ctx_f = sb("ctx_f", [P, S])

        ring = [ctx.enter_context(nc.psum_tensor(f"a_ring{n}", [P, 512], F32)) for n in range(2)]
        wide_bank = [ctx.enter_context(nc.psum_tensor(f"a_wide{n}", [P, S], F32)) for n in range(2)]
        out_bank = ctx.enter_context(nc.psum_tensor("a_out", [P, S], F32))

        stacked = [sem(f"stacked{n}") for n in range(GROUPS)]
        r_full, r_done = sem("r_full"), sem("r_done")
        split_done, max_placed = sem("split_done"), sem("max_placed")
        wide_full, exp_done, pv_done, pv_read = sem("wide_full"), sem("exp_done"), sem("pv_done"), sem("pv_read")
        v_ready, link = sem("v_ready"), sem("link")

        units = [(c, k0, min(512, (c + 1) * P - k0)) for c in range(S // P) for k0 in range(0, (c + 1) * P, 512)]
        KC = S // P
        NMAX = AG * len(units)
        TURN_MAX, TURN_CTX, PROJECT = NMAX, NMAX + 1, NMAX + 3
        STEP, BATCH = NMAX + 3, GROUPS * (NMAX + 3) + 4

        def ring_at(b, hg, n):
            if isinstance(b, int) and b == 0 and hg == 0:
                return n
            return BATCH * b + (STEP * hg + (4 if hg > 0 else 0) - 6 + n)

        def bank_at(hg, n):
            return ring[(STEP * hg + n) % 2]

        def is_first(b, hg):
            return isinstance(b, int) and b == 0 and hg == 0

        def over_batches(engine, step, last):
            for hg in range(GROUPS):
                step(0, hg)
            with engine.Fori(1, B) as b:
                for hg in range(GROUPS):
                    step(b, hg)
            last()

        block = ctx.enter_context(nc.Block())

        @block.sync
        def _(sp):
            def stacks(b, hg):
                toks = bass.ds(b * S, S)
                rows = slice(AG * AHD * hg, AG * AHD * (hg + 1))
                for a in range(3):
                    for j in range(3):
                        at = AHD * (3 * a + j)
                        for stack, src in ((q_stack, t.q_parts_d[a]), (k_stack, t.k_parts_d[j])):
                            sp.dma_start(stack[hg][at:at + AHD, :, :], src[rows, toks].rearrange("(h r) t -> r h t", h=AG)
                                         ).then_inc(stacked[hg], 16)

            for hg in range(GROUPS):
                stacks(0, hg)
            with sp.Fori(1, B) as b:
                for hg in range(GROUPS):
                    sp.wait_ge(wide_full, AG * KC * GROUPS * b + (AG * KC * (hg + 1 - GROUPS)))
                    stacks(b, hg)
            for hg in range(GROUPS):
                sp.wait_ge(stacked[hg], 16 * 18 * B)

        @block.tensor
        def _(pe):
            def maxima(b, hg, n):
                hh, (c, k0, width) = n // len(units), units[n % len(units)]
                wait(pe, r_done, ring_at(b, hg, n) - 1)
                bank = bank_at(hg, n)
                diagonal = k0 + width == (c + 1) * P
                mm = nc.tensor.matmul(bank[:, 0:width], q_stack[hg][0:96, hh, c * P:(c + 1) * P],
                                      k_stack[hg][0:96, hh, k0:k0 + width], start=True, stop=True)
                if diagonal:
                    mm = nc.tensor.matmul(bank[:, width - P:width], ident_bf[:], mask_qk[:], start=False, stop=True,
                                          skip_group_check=True)
                mm.then_inc(r_full, 1)

            def turn_maxima(b, hg):
                wait(pe, r_done, ring_at(b, hg, TURN_MAX) - 1)
                wait(pe, split_done, GROUPS * b + (hg + 1))
                bank = bank_at(hg, TURN_MAX)[:].bitcast(BF16)
                for c in range(KC):
                    mm = nc.tensor.transpose(bank[:, c * P:(c + 1) * P], neg_max[:, c, :, :].rearrange("p h k -> p (h k)"),
                                             ident_bf[:])
                mm.then_inc(r_full, 1)

            def scores(n2, hg, kc, hh):
                width = S - kc * P
                if kc == 0 and hh == 0:
                    wait(pe, max_placed, n2 + 1)
                w = AG * kc + hh
                wait(pe, exp_done, n2 * (AG * KC) + (w - 1))
                bank = wide_bank[w % 2]
                for at in range(0, width, 512):
                    n = min(512, width - at)
                    mm = nc.tensor.matmul(bank[:, at:at + n], k_stack[hg][:, hh, kc * P:(kc + 1) * P],
                                          q_stack[hg][:, hh, kc * P + at:kc * P + at + n], start=True, stop=True)
                mm = nc.tensor.matmul(bank[:, 0:P], ident_bf[:], mask_kq[:], start=False, stop=True, skip_group_check=True)
                mm.then_inc(wide_full, 1)

            def values(n2, hg, kc):
                wait(pe, exp_done, n2 * (AG * KC) + AG * (kc + 1))
                if kc == 0:
                    wait(pe, pv_read, n2)
                    wait(pe, v_ready, n2 + 1)
                for q0 in range(0, S, 512):
                    lo = max(q0, kc * P)
                    if lo >= q0 + 512:
                        continue
                    for hh in range(AG):
                        mm = nc.tensor.matmul(out_bank[BAND * hh:BAND * (hh + 1), lo:q0 + 512], v_pad[hg % 2][:, kc, hh, :],
                                              probs[kc % 2][:, hh, lo - kc * P:q0 + 512 - kc * P],
                                              start=(kc == 0), stop=(kc == KC - 1), skip_group_check=True)
                mm.then_inc(pv_done, 1)

            def turn_context(n2, b, hg, n0):
                wait(pe, pv_read, n2 + 1)
                for n in range(2):
                    wait(pe, r_done, ring_at(b, hg, n0 + n) - 1)
                    for k in range(4):
                        c = 4 * n + k
                        mm = nc.tensor.transpose(bank_at(hg, n0 + n)[:, k * P:(k + 1) * P], ctx_t[:, c * P:(c + 1) * P], t.ident[:])
                    mm.then_inc(r_full, 1)

            def project(b, hg, n0):
                for n in range(2):
                    wait(pe, r_done, ring_at(b, hg, n0))
                    if n == 1:
                        wait(pe, r_done, ring_at(b, hg, n0 + n) - 1)
                    for k in range(4):
                        mm = nc.tensor.transpose(bank_at(hg, n0 + n)[:, k * P:(k + 1) * P], ctx_tok[:, 4 * n + k, :], t.ident[:])
                    mm.then_inc(r_full, 1)
                for n in range(2):
                    wait(pe, r_done, ring_at(b, hg, n0 + 2))
                    for k in range(4):
                        c = 4 * n + k
                        mm = nc.tensor.matmul(bank_at(hg, n0 + 2 + n)[:, k * P:(k + 1) * P], ctx_f[:, c * P:(c + 1) * P],
                                              w_out[:], start=True, stop=True)
                    mm.then_inc(r_full, 1)

            def step(b, hg):
                wait(pe, stacked[hg], 16 * 18 * (b + 1))
                n2, before = GROUPS * b + (hg - 1), (hg - 1) % GROUPS
                share = NMAX // KC
                for kc in range(KC):
                    for m in range(share):
                        maxima(b, hg, kc * share + m)
                        if not is_first(b, hg) and m < AG:
                            scores(n2, before, kc, m)
                    if not is_first(b, hg) and kc >= 1:
                        values(n2, before, kc - 1)
                turn_maxima(b, hg)
                if not is_first(b, hg):
                    values(n2, before, KC - 1)
                    turn_context(n2, b, hg, TURN_CTX)
                    if hg == 0:
                        project(b, hg, PROJECT)

            def last():
                n2, before = GROUPS * B - 1, GROUPS - 1
                for kc in range(KC):
                    for hh in range(AG):
                        scores(n2, before, kc, hh)
                    if kc >= 1:
                        values(n2, before, kc - 1)
                values(n2, before, KC - 1)
                turn_context(n2, B, 0, 0)
                project(B, 0, 2)

            over_batches(pe, step, last)

        @block.scalar
        def _(act):
            def exps(n2):
                for kc in range(KC):
                    for hh in range(AG):
                        w = AG * kc + hh
                        width = S - kc * P
                        wait(act, wide_full, n2 * (AG * KC) + (w + 1))
                        if hh == 0:
                            wait(act, pv_done, n2 * KC + (kc - 1))
                        nc.scalar.activation(probs[kc % 2][:, hh, 0:width], wide_bank[w % 2][:, 0:width], ACT.Exp
                                             ).then_inc(exp_done, 1)

            def copy_context(n2, b, hg):
                wait(act, pv_done, n2 * KC + KC)
                nc.scalar.copy(ctx_t[:], out_bank[:]).then_inc(pv_read, 1)

            def step(b, hg):
                if is_first(b, hg):
                    return
                n2 = GROUPS * b + (hg - 1)
                exps(n2)
                copy_context(n2, b, hg)

            def last():
                exps(GROUPS * B - 1)
                copy_context(GROUPS * B - 1, B, 0)

            over_batches(act, step, last)

        @block.gpsimd
        def _(pool):
            def step(b, hg):
                wait(pool, pv_done, KC * GROUPS * b + KC * (hg - 1))
                src = v_all[:, bass.ds(b * KC, KC), AG * AHD * hg:AG * AHD * (hg + 1)]
                nc.gpsimd.tensor_copy(v_pad[hg % 2][:, :, :, 0:AHD], src.rearrange("p c (h d) -> p c h d", h=AG)
                                      ).then_inc(v_ready, 1)

            over_batches(pool, step, lambda: None)

        @block.vector
        def _(dve):
            def maxima(b, hg, n):
                hh, (c, k0, width) = n // len(units), units[n % len(units)]
                wait(dve, r_full, ring_at(b, hg, n) + 1)
                into = (max_b if k0 > 0 else row_max)[:, hh, c:c + 1]
                nc.vector.tensor_reduce(into, bank_at(hg, n)[:, 0:width], AX.X, ALU.max).then_inc(r_done, 1)

            def split_maxima(b, hg):
                dve.sem_clear(link)
                wait(dve, r_done, ring_at(b, hg, NMAX))
                part = [neg_max[:, :, :, n].rearrange("p c h -> p h c") for n in range(3)]
                half = KC // 2
                at = 0

                def linked(instruction):
                    nonlocal at
                    at += 1
                    instruction.then_inc(link, 1)
                    dve.wait_ge(link, at)

                linked(nc.vector.tensor_tensor(row_max[:, :, half:KC], row_max[:, :, half:KC], max_b[:, :, half:KC], ALU.max))
                linked(nc.vector.tensor_scalar(part[0], row_max[:], -1.0, None, ALU.mult))
                linked(nc.vector.scalar_tensor_tensor(max_rest[:], row_max[:], -1.0, part[0], ALU.mult, ALU.subtract))
                linked(nc.vector.tensor_copy(part[1], max_rest[:]))
                nc.vector.tensor_tensor(part[2], max_rest[:], part[1], ALU.subtract).then_inc(split_done, 1)

            def place_maxima(b, hg):
                wait(dve, r_full, ring_at(b, hg, TURN_MAX) + 1)
                bank = bank_at(hg, TURN_MAX)[:].bitcast(BF16)
                for hh in range(AG):
                    last = nc.vector.tensor_copy(q_stack[hg][96:P, hh, :], bank[BAND * hh:BAND * (hh + 1), :])
                    if hh < AG - 1:
                        last.then_inc(max_placed_parts, 1)
                last.then_inc(max_placed, 1)
                dve.wait_ge(max_placed, GROUPS * b + (hg + 1))
                dve.sem_inc(r_done, 1)

            def normalise(b, hg, n0, before):
                dve.sem_clear(link)
                for n in range(2):
                    wait(dve, r_full, ring_at(b, hg, n0 + n) + 1)
                    bank = bank_at(hg, n0 + n)[:].rearrange("p (c h d) -> p c h d", c=4, h=AG)
                    nc.vector.reciprocal(inv[:, n], bank[:, :, :, AHD]).then_inc(link, 1)
                    dve.wait_ge(link, n + 1)
                    out = ctx_tok[:, 4 * n:4 * n + 4, AG * AHD * before:AG * AHD * (before + 1)]
                    nc.vector.tensor_tensor(out.rearrange("p c (h d) -> p c h d", h=AG), bank[:, :, :, 0:AHD],
                                            inv[:, n].unsqueeze(3).broadcast_to([P, 4, AG, AHD]), ALU.mult).then_inc(r_done, 1)

            def project(b, hg, n0):
                for n in range(2):
                    wait(dve, r_full, ring_at(b, hg, n0 + n) + 1)
                    nc.vector.tensor_copy(ctx_f[:, 512 * n:512 * (n + 1)], bank_at(hg, n0 + n)[:]).then_inc(r_done, 1)
                for n in range(2):
                    wait(dve, r_full, ring_at(b, hg, n0 + 2 + n) + 1)
                    chunk = t.xtok[:, bass.ds((b - 1) * KC + 4 * n, 4), :].rearrange("p c d -> p (c d)")
                    nc.vector.tensor_tensor(chunk, bank_at(hg, n0 + 2 + n)[:], chunk, ALU.add).then_inc(r_done, 1)

            max_placed_parts = sem("max_placed_parts")

            def step(b, hg):
                for n in range(NMAX):
                    maxima(b, hg, n)
                split_maxima(b, hg)
                place_maxima(b, hg)
                if not is_first(b, hg):
                    normalise(b, hg, TURN_CTX, (hg - 1) % GROUPS)
                    if hg == 0:
                        project(b, hg, PROJECT)

            def last():
                normalise(B, 0, 0, GROUPS - 1)
                project(B, 0, 2)

            over_batches(dve, step, last)


def windowed(nc, t):
    with ExitStack() as ctx:
        def sb(name, shape, dt=F32):
            return ctx.enter_context(nc.sbuf_tensor("w_" + name, shape, dt))

        def sem(name):
            return ctx.enter_context(nc.semaphore("w_" + name))

        wqkv = sb("wqkv", [P, 2, 3 * INNER])
        scales = sb("scales", [P, 2, 4 * HD])
        wo = sb("wo", [P, HEADS // 2, D])
        w1 = sb("w1", [P, 2 * FF])
        w2 = sb("w2", [P, NF, D])
        b1 = sb("b1", [P, 2 * NF])
        vecs = sb("vecs", [P, 3])
        rope_tab = sb("rope_tab", [P, S // P, 4 * HD])
        mask_tab = sb("mask_tab", [P, PAIRS_B, KEYS + 1])
        mask_odd = sb("mask_odd", [P, KEYS])
        xs = [sb(f"xs{u}", [P, P]) for u in range(2)]
        raw = sb("raw", [P, 4, 512])
        sq = sb("sq", [P, 2, 512])
        rot = sb("rot", [P, 4, 512])
        rope = sb("rope", [P, 4, 512])
        tc = [sb(f"tc{u}", [P, 4 * HD]) for u in range(2)]
        ss = sb("ss", [P, 2 * HEADS])
        rn = [sb(f"rn{u}", [P, 2 * HEADS]) for u in range(2)]
        nhalf = sb("nhalf", [P, 2 * HEADS])
        qt = sb("qt", [P, HEADS // 2, P])
        kb = sb("kb", [P, HEADS // 2, 2, KEYS])
        mask = sb("mask", [P, KEYS + 1])
        v = [sb(f"v{u}", [P, INNER]) for u in range(2)]
        vr = [sb(f"vr{u}", [P, 4, HD]) for u in range(2)]
        p = [sb(f"p{u}", [P, HEADS, KEYS]) for u in range(2)]
        pc = [sb(f"pc{u}", [P, 4, 4, BAND]) for u in range(2)]
        nb = [sb(f"nb{u}", [P, HEADS]) for u in range(2)]
        rs = [sb(f"rs{u}", [P, HEADS]) for u in range(2)]
        rinv = [sb(f"rinv{u}", [P, HEADS]) for u in range(2)]
        pts = sb("pts", [P, 2, 512])
        bd = sb("bd", [P, 4, 4, BAND])
        ot = sb("ot", [P, HEADS // 2, P])
        xf = sb("xf", [P, 2 * P])
        st = sb("st", [P, 2, 6])
        mv = sb("mv", [P, 2, 2])
        ve = sb("ve", [P, 2])
        vh = sb("vh", [P, 2])
        vr_std = sb("vr_std", [P, 2])
        xnt = sb("xnt", [P, 2, P])
        xnf = sb("xnf", [P, 2 * P])
        gl = sb("gl", [P, 2 * P])
        hid = sb("hid", [P, NF, 2 * P])

        def banks(name, n):
            return [ctx.enter_context(nc.psum_tensor(f"w_{name}{i}", [P, 512], F32)) for i in range(n)]

        px, pt, ps = banks("px", 2), banks("pt", 2), banks("ps", 2)
        po, pm = banks("po", 1)[0], banks("pm", 1)[0]

        w_early = sem("w_early")
        w_wo = sem("w_wo")
        w_ffn = sem("w_ffn")
        consts = sem("consts")
        xs_built = sem("xs_built")
        x_full, x_done = sem("x_full"), sem("x_done")
        sq_ready, red_done = sem("sq_ready"), sem("red_done")
        kn_ready, tc_ready, rot_ready, rope_ready = sem("kn_ready"), sem("tc_ready"), sem("rot_ready"), sem("rope_ready")
        t_full, t_act, t_dve = sem("t_full"), sem("t_act"), sem("t_dve")
        s_full, s_done = sem("s_full"), sem("s_done")
        mask_ready = sem("mask_ready")
        corner_ready = sem("corner_ready")
        exp_done, rinv_ready, p_ready = sem("exp_done"), sem("rinv_ready"), sem("p_ready")
        pv_full, o_done = sem("pv_full"), sem("o_done")
        vr_ready = [sem(f"vr_ready{u}") for u in range(2)]
        m_full, m_done, g_ready = sem("m_full"), sem("m_done"), sem("g_ready")
        xf_ready, xa_ready = sem("xf_ready"), sem("xa_ready")
        link, ffn_link = sem("link"), sem("ffn_link")
        mult_done = sem("mult_done")
        apart = sem("apart")
        CONSTS = 3 * 16

        with nc.Block() as block:
            @block.sync
            def _(sp):
                sp.dma_start(rope_tab[:], t.rope_d).then_inc(consts, 16)
                sp.dma_start(mask_tab[:], t.mask_d).then_inc(consts, 16)
                sp.dma_start(mask_odd[:], t.mask_odd_d).then_inc(consts, 16)
                sp.wait_ge(consts, CONSTS)

            @block.gpsimd
            def _(pool):
                for buf in (rope, kb, v[0], v[1], vr[0], vr[1], p[0], p[1], pc[0], pc[1], bd, rn[0], rn[1], qt, raw):
                    nc.gpsimd.memset(buf[:], 0.0)

        def m_use(pp, k):
            if isinstance(pp, int) and pp < 2:
                return 2 * pp + (k == M_WO[1])
            return 8 * pp + (k - 12)

        def m_read(pp, k):
            if isinstance(pp, int) and pp < 2:
                return 2 * pp + (k == M_WO[1])
            return 7 * pp + (min(k, M_OUT) - 10)

        M_TURN, M_BACK, M_HID0, M_HID1, M_HID2, M_OUT = 0, 1, 3, 4, 5, 6
        M_WO = (2, 7)
        M_HID = (M_HID0, M_HID1, M_HID2)

        UNIT_AT = (2, 3, 0, 1, 4, 5)
        T_UNIT = (0, 2, 1, 3)
        T_P, T_CORNER, T_USES = (4, 5, 7, 8), 6, 9

        def wide(ap, heads=8):
            return ap.unsqueeze(1).broadcast_to([P, heads, ap.shape[-1]])

        def col0(pair):
            q = pair % PAIRS
            return q * (2 * P) + q // PAIRS_B + 1

        block = ctx.enter_context(nc.Block())

        @block.sync
        def _(sp):
            def load_early(layer, slot):
                sp.dma_start(wqkv[:, bass.ds(slot, 1), :].rearrange("p s n -> p (s n)"), t.wqkv_d[bass.ds(layer, 1)].rearrange("l p n -> (l p) n")
                             ).then_inc(w_early, 16)
                for which, scale in ((0, t.qs_d), (2, t.ks_d)):
                    row = scale[bass.ds(layer, 1)]
                    for n, half in enumerate((row, row[:, HD // 2:HD], row[:, 0:HD // 2])):
                        at = which * HD + (0, HD, HD + HD // 2)[n]
                        width = half.shape[-1]
                        sp.dma_start(scales[:, bass.ds(slot, 1), at:at + width].rearrange("p s n -> p (s n)"), half.broadcast_to([P, width])
                                     ).then_inc(w_early, 16)

            def load_wo(layer):
                sp.dma_start(wo[:], t.wo_d[bass.ds(layer, 1)].rearrange("l (j p) n -> p (l j) n", p=P)
                             ).then_inc(w_wo, 16)

            def load_ffn(layer):
                one = bass.ds(layer, 1)
                sp.dma_start(w1[:], t.w1_d[one].rearrange("l p n -> (l p) n")).then_inc(w_ffn, 16)
                for n, (f, m) in enumerate(FPARTS):
                    sp.dma_start(w2[0:m, n, :], t.w2_d[one, f:f + m].rearrange("l p n -> (l p) n")).then_inc(w_ffn, 16)
                    for half in range(2):
                        src = t.b1_d[one, half * FF + f:half * FF + f + m].rearrange("l p -> p l")
                        at = half * NF + n
                        sp.dma_start(b1[0:m, at:at + 1], src).then_inc(w_ffn, 16)
                for n, vec in enumerate((t.g_d, t.b_d, t.b2_d)):
                    sp.dma_start(vecs[:, n:n + 1], vec[one].rearrange("l p -> p l")).then_inc(w_ffn, 16)

            def v_tail(pair, u):
                g = 2 * pair + u
                wait(sp, x_done, 6 * g + 6)
                wait(sp, pv_full, 2 * g + 4)
                src = v[u][P - BAND:P, :].rearrange("p (r h e d) -> p h r e d", r=2, h=4, e=2)
                for hh in range(4):
                    for r in range(2):
                        sp.dma_start(vr[u][BAND * hh:BAND * (hh + 1), 2 * r:2 * r + 2, :], src[:, hh, r]
                                     ).then_inc(vr_ready[u], 16)

            load_early(0, 0)
            load_wo(0)
            load_ffn(0)
            v_tail(0, 0)
            v_tail(0, 1)
            load_early(1, 1)
            with sp.Fori(1, PAIRS) as q:
                v_tail(q, 0)
                v_tail(q, 1)

            def layer_loads(layer, more):
                first = layer * PAIRS
                v_tail(first, 0)
                sp.wait_ge(m_full, m_use(first, M_WO[1]) + 1)
                load_wo(layer)
                v_tail(first, 1)
                v_tail(first + 1, 0)
                sp.wait_ge(xa_ready, first + PAIRS)
                load_ffn(layer)
                v_tail(first + 1, 1)
                if more:
                    load_early(layer + 1, (layer + 1) % 2)
                with sp.Fori(2, PAIRS) as q:
                    v_tail(first + q, 0)
                    v_tail(first + q, 1)

            if LAYERS > 2:
                with sp.Fori(1, LAYERS - 1) as layer:
                    layer_loads(layer, True)
            layer_loads(LAYERS - 1, False)
            v_tail(LAYERS * PAIRS, 0)
            v_tail(LAYERS * PAIRS, 1)
            for u in range(2):
                sp.wait_ge(vr_ready[u], 128 * (LAYERS * PAIRS + 1))

        steps = LAYERS * PAIRS + 2

        def over_pairs(engine, body):
            body(0)
            body(1)
            with engine.Fori(2, steps - 2) as pair:
                body(pair)
            body(steps - 2)
            body(steps - 1)

        def layer_loaded(engine, semaphore, per_layer, pair, lag):
            if isinstance(pair, int):
                layer = min(max(pair - lag, 0) // PAIRS, LAYERS - 1)
                engine.wait_ge(semaphore, per_layer * (layer + 1))
            else:
                engine.wait_ge(semaphore, ((pair + (PAIRS - lag)) // PAIRS) * per_layer)

        N_EARLY, N_WO, N_FFN = 16 * 7, 16, 16 * (1 + 3 * NF + 3)

        @block.tensor
        def _(pe):
            def qkv(pair, g, u, i):
                if i == 0:
                    layer_loaded(pe, w_early, N_EARLY, pair, 0)
                    wait(pe, xs_built, g + 1)
                wait(pe, x_done, 6 * g + i - 1)
                slot = (pair // PAIRS) % 2
                at = UNIT_AT[i] * 512
                rhs = wqkv[:, bass.ds(slot, 1), at:at + 512].rearrange("p s n -> p (s n)")
                nc.tensor.matmul(px[i % 2][:], xs[u][:], rhs, start=True, stop=True).then_inc(x_full, 1)

            def t_bank(u, k):
                return pt[(9 * u + k) % 2]

            def turn_qk(g, u, i):
                unit = T_UNIT[i]
                if unit < 2:
                    wait(pe, kn_ready, 2 * g + unit + 1)
                else:
                    wait(pe, rope_ready, 4 * g + unit + 1)
                if i == 0:
                    wait(pe, t_act, 7 * g - 1)
                if i == 1:
                    wait(pe, t_act, 7 * g)
                if i == 2:
                    wait(pe, t_dve, 2 * g + 1)
                if i == 3:
                    wait(pe, t_act, 7 * g + 1)
                for j in range(4):
                    mm = nc.tensor.transpose(t_bank(u, i)[:, j * P:(j + 1) * P], rope[:, unit, j * P:(j + 1) * P], t.ident[:])
                mm.then_inc(t_full, 1)

            def turn_p(g, u, i):
                k = T_P[i]
                wait(pe, p_ready, 4 * g + i + 1)
                if i == 0:
                    wait(pe, t_dve, 2 * g + 2)
                if i == 1:
                    wait(pe, t_act, 7 * g + 2)
                if i >= 2:
                    wait(pe, t_act, 7 * g + i + 2)
                for j in range(4):
                    mm = nc.tensor.transpose(t_bank(u, k)[:, j * P:(j + 1) * P], p[u][:, 4 * i + j, BAND:KEYS], t.ident[:])
                mm.then_inc(t_full, 1)

            def turn_corner(g, u):
                wait(pe, corner_ready, 4 * g + 4)
                wait(pe, t_act, 7 * g + 3)
                pe.sem_inc(apart, 1)
                for s in range(4):
                    src = pc[u][0:BAND, s, :, :].rearrange("p h k -> p (h k)")
                    mm = nc.tensor.transpose(t_bank(u, 6)[:, s * BAND:(s + 1) * BAND], src, t.ident[0:BAND, 0:BAND])
                mm.then_inc(t_full, 1)

            def scores(g, u, j):
                if j == 0:
                    wait(pe, t_act, 7 * g + 2)
                    wait(pe, t_dve, 2 * g + 2)
                wait(pe, s_done, 8 * g + j - 1)
                nc.tensor.matmul(ps[j % 2][:, 0:2 * KEYS], qt[:, j, :], kb[:, j, :, :].rearrange("p e k -> p (e k)"),
                                 start=True, stop=True).then_inc(s_full, 1)

            def context(pair, g, u, r):
                wait(pe, t_act, 7 * g + (5, 7)[r])
                wait(pe, o_done, 2 * g + r)
                if r == 0:
                    wait(pe, x_done, 6 * (g - 2) + 6)
                    wait(pe, vr_ready[1 - u], 128 * (pair - 1 + u))
                for j in range(4):
                    for e in range(2):
                        h = 2 * (4 * r + j) + e
                        nc.tensor.matmul(po[HD * e:HD * (e + 1), j * P:(j + 1) * P], v[u][:, h * HD:(h + 1) * HD],
                                         pts[:, (h // 4) % 2, (h % 4) * P:(h % 4 + 1) * P],
                                         start=(j == 0), stop=False, skip_group_check=True)
                for e in range(2):
                    out = po[HD * e:HD * (e + 1), :].rearrange("p (j i) -> p j i", j=4)[:, :, 0:BAND]
                    mm = nc.tensor.matmul(out, vr[1 - u][:, 2 * r + e, :], bd[:, 2 * r + e, :, :],
                                          start=False, stop=True, skip_group_check=True)
                mm.then_inc(pv_full, 1)

            def project(pair, g, u):
                if u == 0:
                    layer_loaded(pe, w_wo, N_WO, pair, 1)
                wait(pe, o_done, 2 * g + 2)
                wait(pe, m_done, m_read(pair, M_WO[u]))
                if u == 1 and not (isinstance(pair, int) and pair < 2):
                    wait(pe, xa_ready, pair + (PAIRS - 1))
                for j in range(HEADS // 2):
                    mm = nc.tensor.matmul(pm[:, 0:P], wo[:, j, :], ot[:, j, :], start=(j == 0), stop=(j == HEADS // 2 - 1))
                mm.then_inc(m_full, 1)

            def ffn(pair, k):
                if isinstance(pair, int) and pair < 2:
                    return
                wait(pe, m_done, m_read(pair, k))
                if k == M_TURN:
                    wait(pe, xf_ready, pair - 1)
                    for c in range(2):
                        mm = nc.tensor.transpose(pm[:, c * P:(c + 1) * P], xf[:, c * P:(c + 1) * P], t.ident[:])
                elif k == M_BACK:
                    for c in range(2):
                        mm = nc.tensor.transpose(pm[:, c * P:(c + 1) * P], xnt[:, c, :], t.ident[:])
                elif k == M_OUT:
                    for n, (f, m) in enumerate(FPARTS):
                        mm = nc.tensor.matmul(pm[:, 0:2 * P], w2[0:m, n, :], hid[0:m, n, :], start=(n == 0), stop=(n == NF - 1))
                else:
                    n = M_HID.index(k)
                    if n == 0:
                        layer_loaded(pe, w_ffn, N_FFN, pair, 2)
                    f, m = FPARTS[n]
                    nc.tensor.matmul(pm[0:m, 0:2 * P], w1[:, FF + f:FF + f + m], xnf[:], start=True, stop=True)
                    mm = nc.tensor.matmul(pm[0:m, 2 * P:4 * P], w1[:, f:f + m], xnf[:], start=True, stop=True)
                mm.then_inc(m_full, 1)

            def body(pair):
                for u in range(2):
                    g = 2 * pair + u
                    turn_qk(g, u, 0)
                    turn_qk(g, u, 1)
                    qkv(pair, g, u, 0)
                    if u == 1:
                        ffn(pair, M_HID0)
                    turn_qk(g, u, 2)
                    turn_qk(g, u, 3)
                    qkv(pair, g, u, 1)
                    qkv(pair, g, u, 2)
                    scores(g, u, 0)
                    scores(g, u, 1)
                    ffn(pair, (M_TURN, M_HID1)[u])
                    qkv(pair, g, u, 3)
                    turn_p(g, u, 0)
                    turn_p(g, u, 1)
                    scores(g, u, 2)
                    scores(g, u, 3)
                    turn_corner(g, u)
                    if u == 1:
                        ffn(pair, M_HID2)
                    context(pair, g, u, 0)
                    turn_p(g, u, 2)
                    scores(g, u, 4)
                    turn_p(g, u, 3)
                    scores(g, u, 5)
                    scores(g, u, 6)
                    scores(g, u, 7)
                    context(pair, g, u, 1)
                    ffn(pair, (M_BACK, M_OUT)[u])
                    qkv(pair, g, u, 4)
                    qkv(pair, g, u, 5)
                    project(pair, g, u)

            over_pairs(pe, body)

        @block.scalar
        def _(act):
            def build_xs(pair, u):
                g = 2 * pair + u
                wait(act, xa_ready, pair + 1)
                wait(act, x_full, 6 * (g - 1))
                at = col0(pair) + u * P
                nc.scalar.copy(xs[u][0:D // 2, :], t.xa[0:D // 2, bass.ds(at, P)])
                nc.scalar.copy(xs[u][D // 2:D, :], t.xa[D // 2:D, bass.ds(at - 1, P)]).then_inc(xs_built, 1)

            def build_xf(pair):
                wait(act, m_done, m_read(pair - 1, M_WO[1]) + 1)
                at = col0(pair - 2 + PAIRS)
                nc.scalar.copy(xf[0:D // 2, :], t.xb[0:D // 2, bass.ds(at, 2 * P)])
                nc.scalar.copy(xf[D // 2:D, :], t.xb[D // 2:D, bass.ds(at - 1, 2 * P)]).then_inc(xf_ready, 1)

            def copy_raw(g, i):
                wait(act, x_full, 6 * g + i + 1)
                wait(act, rope_ready, 4 * g + i + 1)
                nc.scalar.copy(raw[:, i, :], px[i % 2][:]).then_inc(x_done, 1)

            def copy_v(pair, g, u, i):
                wait(act, x_full, 6 * g + i + 1)
                wait(act, pv_full, 2 * g + 2)
                wait(act, vr_ready[u], 128 * pair)
                nc.scalar.copy(v[u][:, (i - 4) * 512:(i - 3) * 512], px[i % 2][:]).then_inc(x_done, 1)

            def t_bank(u, k):
                return pt[(9 * u + k) % 2]

            def copy_qt(g, u, i):
                k = 2 * i + 1
                wait(act, t_full, 9 * g + k + 1)
                wait(act, s_full, 8 * g)
                nc.scalar.copy(qt[:, 4 * i:4 * i + 4, :].rearrange("p j n -> p (j n)"), t_bank(u, k)[:]).then_inc(t_act, 1)

            def copy_pt(g, u, i):
                wait(act, t_full, 9 * g + T_P[i] + 1)
                wait(act, pv_full, 2 * g + i // 2)
                nc.scalar.copy(pts[:, i % 2, :], t_bank(u, T_P[i])[:]).then_inc(t_act, 1)

            def copy_corner(g, u):
                wait(act, t_full, 9 * g + T_CORNER + 1)
                wait(act, pv_full, 2 * g)
                for hh in range(4):
                    rows = slice(BAND * hh, BAND * (hh + 1))
                    src = t_bank(u, 6)[rows, 0:P].rearrange("p (s i) -> p s i", s=4)
                    last = nc.scalar.copy(bd[rows, :, hh, :], src)
                last.then_inc(t_act, 1)

            def exps(g, u, q):
                wait(act, s_done, 8 * g + 2 * q + 2)
                for h in range(4 * q, 4 * q + 4):
                    last = nc.scalar.activation(p[1 - u][:, h, :], p[1 - u][:, h, :], ACT.Exp, bias=nb[u][:, h:h + 1],
                                                scale=-1.0, accum_out=rs[u][:, h:h + 1])
                last.then_inc(exp_done, 1)

            def copy_context(pair, g, u, r):
                wait(act, pv_full, 2 * g + r + 1)
                if not isinstance(g, int) or g > 0:
                    wait(act, m_full, m_use(pair - 1 + u, M_WO[1 - u]) + 1)
                nc.scalar.copy(ot[:, 4 * r:4 * r + 4, :].rearrange("p j n -> p (j n)"), po[:]).then_inc(o_done, 1)

            def ffn(pair, k):
                if isinstance(pair, int) and pair < 2:
                    return
                wait(act, m_full, m_use(pair, k) + 1)
                if k == M_BACK:
                    layer_loaded(act, w_ffn, N_FFN, pair, 2)
                    nc.scalar.activation(xnf[:], pm[:, 0:2 * P], ACT.Identity, bias=vecs[:, 1:2], scale=vecs[:, 0:1]
                                         ).then_inc(m_done, 1)
                else:
                    n = M_HID.index(k)
                    m = FPARTS[n][1]
                    nc.scalar.activation(gl[0:m, :], pm[0:m, 0:2 * P], ACT.Gelu, bias=b1[0:m, NF + n:NF + n + 1]
                                         ).then_inc(g_ready, 1)

            def body(pair):
                for u in range(2):
                    g = 2 * pair + u
                    copy_qt(g, u, 0)
                    copy_raw(g, 0)
                    if u == 1:
                        ffn(pair, M_HID0)
                    copy_qt(g, u, 1)
                    copy_raw(g, 1)
                    if u == 0 and not (isinstance(pair, int) and pair < 2):
                        build_xf(pair)
                    copy_raw(g, 2)
                    if u == 1:
                        ffn(pair, M_HID1)
                    copy_raw(g, 3)
                    copy_pt(g, u, 0)
                    copy_pt(g, u, 1)
                    copy_corner(g, u)
                    if u == 1:
                        ffn(pair, M_HID2)
                    exps(g, u, 0)
                    copy_pt(g, u, 2)
                    copy_context(pair, g, u, 0)
                    copy_pt(g, u, 3)
                    exps(g, u, 1)
                    exps(g, u, 2)
                    copy_context(pair, g, u, 1)
                    if u == 0:
                        ffn(pair, M_BACK)
                    build_xs(pair + u, 1 - u)
                    exps(g, u, 3)
                    copy_v(pair, g, u, 4)
                    copy_v(pair, g, u, 5)

            build_xs(0, 0)
            over_pairs(act, body)

        @block.gpsimd
        def _(pool):
            def squares(g, i):
                wait(pool, x_done, 6 * g + i + 1)
                wait(pool, red_done, 4 * g + i - 1)
                nc.gpsimd.tensor_tensor(sq[:, i % 2, :], raw[:, i, :], raw[:, i, :], ALU.mult).then_inc(sq_ready, 1)

            def tables(pair, g, u):
                layer_loaded(pool, w_early, N_EARLY, pair, 0)
                wait(pool, rope_ready, 4 * g)
                pos = (pair % PAIRS_B) * 2 + u
                slot = (pair // PAIRS) % 2
                nc.gpsimd.tensor_tensor(tc[u][:], rope_tab[:, bass.ds(pos, 1), :].rearrange("p s n -> p (s n)"),
                                        scales[:, bass.ds(slot, 1), :].rearrange("p s n -> p (s n)"), ALU.mult
                                        ).then_inc(tc_ready, 1)

            def choose_mask(pair, g):
                wait(pool, s_done, 8 * g)
                pos = pair % PAIRS_B
                nc.gpsimd.tensor_copy(mask[:], mask_tab[:, bass.ds(pos, 1), :].rearrange("p s n -> p (s n)")
                                      ).then_inc(mask_ready, 1)

            def rotated(g, u, i):
                if i == 0:
                    wait(pool, tc_ready, g + 1)
                wait(pool, rope_ready, 4 * g + i + 1)
                hh = HD // 2
                src = raw[:, i, :].rearrange("p (h d) -> p h d", d=HD)
                dst = rot[:, i, :].rearrange("p (h d) -> p h d", d=HD)
                which = 1 - i // 2
                tab = tc[u][:, (1 + 2 * which) * HD:(2 + 2 * which) * HD]
                nc.gpsimd.tensor_tensor(dst[:, :, 0:hh], src[:, :, hh:HD], wide(tab[:, 0:hh]), ALU.mult)
                nc.gpsimd.tensor_tensor(dst[:, :, hh:HD], src[:, :, 0:hh], wide(tab[:, hh:HD]), ALU.mult
                                        ).then_inc(rot_ready, 1)

            def normalise(g, u, q):
                wait(pool, rinv_ready, 4 * g + q + 1)
                heads = p[1 - u][:, 4 * q:4 * q + 4, BAND:KEYS]
                nc.gpsimd.tensor_tensor(heads, heads, rinv[u][:, 4 * q:4 * q + 4].unsqueeze(2).broadcast_to([P, 4, P]),
                                        ALU.mult).then_inc(p_ready, 1)
                r, hh = q // 2, 2 * (q % 2)
                corner = pc[1 - u][:, 2 * r:2 * r + 2, hh:hh + 2, :].rearrange("p e h k -> p h e k")
                nc.gpsimd.tensor_tensor(corner, p[1 - u][:, 4 * q:4 * q + 4, 0:BAND].rearrange("p (h e) k -> p h e k", e=2),
                                        rinv[u][:, 4 * q:4 * q + 4].rearrange("p (h e) -> p h e", e=2).unsqueeze(3)
                                        .broadcast_to([P, 2, 2, BAND]), ALU.mult).then_inc(corner_ready, 1)

            pool.sem_inc(p_ready, 4)
            pool.sem_inc(corner_ready, 4)

            def body(pair):
                for u in range(2):
                    g = 2 * pair + u
                    tables(pair, g, u)
                    if not isinstance(g, int) or g > 0:
                        normalise(g - 1, 1 - u, 3)
                    for i in range(4):
                        squares(g, i)
                    if u == 0:
                        choose_mask(pair, g)
                    rotated(g, u, 0)
                    rotated(g, u, 1)
                    rotated(g, u, 2)
                    normalise(g, u, 0)
                    rotated(g, u, 3)
                    normalise(g, u, 1)
                    normalise(g, u, 2)

            over_pairs(pool, body)

        @block.vector
        def _(dve):
            def t_bank(u, k):
                return pt[(9 * u + k) % 2]

            def linked(instruction, value):
                instruction.then_inc(link, 1)
                dve.wait_ge(link, value)

            def carry(pair, g, u):
                wait(dve, s_full, 8 * g)
                flat = kb[:].rearrange("p j e k -> p (j e) k")
                if u == 1:
                    wait(dve, mask_ready, pair + 1)
                    ins = nc.vector.tensor_scalar(flat[:, :, 0:BAND], flat[:, :, P:KEYS], mask[:, KEYS:KEYS + 1], None, ALU.mult)
                else:
                    ins = nc.vector.tensor_copy(flat[:, :, 0:BAND], flat[:, :, P:KEYS])
                ins.then_inc(link, 1)
                dve.wait_ge(link, 1)

            def copy_kb(g, u, i):
                k = 2 * i
                wait(dve, t_full, 9 * g + k + 1)
                for e in range(2):
                    rows = slice(HD * e, HD * (e + 1))
                    last = nc.vector.tensor_copy(kb[rows, 4 * i:4 * (i + 1), e, BAND:KEYS],
                                                 t_bank(u, k)[rows, :].rearrange("p (j n) -> p j n", j=4))
                last.then_inc(t_dve, 1)

            def head_norms(g, i):
                wait(dve, sq_ready, 4 * g + i + 1)
                nc.vector.tensor_reduce(ss[:, 8 * i:8 * i + 8], sq[:, i % 2, :].rearrange("p (h d) -> p h d", d=HD),
                                        AX.X, ALU.add).then_inc(red_done, 1)

            FACTORS = RSQRT_STEPS + 2
            Q_HEADS = slice(HEADS, 2 * HEADS)

            def factors(g, u, n):
                if n == 0:
                    wait(dve, red_done, 4 * g + 4)
                    ins = nc.vector.tensor_scalar(ss[:], ss[:], 1e-24, None, ALU.max)
                elif n <= RSQRT_STEPS:
                    dve.wait_ge(link, 1 + n)
                    ins = rsqrt_step(nc, n - 1, rn[u][:], ss[:], nhalf[:])
                else:
                    dve.wait_ge(link, 1 + n)
                    ins = nc.vector.tensor_scalar(rn[u][:, Q_HEADS], rn[u][:, Q_HEADS], -SIM_SCALE, None, ALU.mult)
                ins.then_inc(link, 1)

            def masked_scores(pair, g, u, j, e):
                if e == 0:
                    wait(dve, s_full, 8 * g + j + 1)
                    if j == 0:
                        wait(dve, t_full, 9 * g)
                    dve.sem_inc(apart, 1)
                m = mask[:, 0:KEYS] if u == 1 else mask_odd[:]
                h = 2 * j + e
                factor = rn[1 - u][:, HEADS + h:HEADS + h + 1]
                ins = nc.vector.tensor_tensor_reduce(p[1 - u][:, h, :], ps[j % 2][:, e * KEYS:(e + 1) * KEYS], m,
                                                     factor, 3e38, ALU.add, ALU.min, nb[u][:, h:h + 1])
                if e == 1:
                    ins.then_inc(s_done, 1)

            def inverse_sums(g, u, q):
                wait(dve, exp_done, 4 * g + q + 1)
                nc.vector.reciprocal(rinv[u][:, 4 * q:4 * q + 4], rs[u][:, 4 * q:4 * q + 4]).then_inc(rinv_ready, 1)

            def straight(g, u, i):
                if i == 0:
                    wait(dve, tc_ready, g + 1)
                wait(dve, x_done, 6 * g + i + 1)
                wait(dve, t_full, 9 * g + T_UNIT.index(i) + 1)
                which = 1 - i // 2
                nc.vector.tensor_tensor(rope[:, i, :].rearrange("p (h d) -> p h d", d=HD),
                                        raw[:, i, :].rearrange("p (h d) -> p h d", d=HD),
                                        wide(tc[u][:, 2 * which * HD:(2 * which + 1) * HD]), ALU.mult
                                        ).then_inc(mult_done, 1)

            def add_rotated(g, i):
                dve.wait_ge(mult_done, i + 1)
                wait(dve, rot_ready, 4 * g + i + 1)
                nc.vector.tensor_tensor(rope[:, i, :], rope[:, i, :], rot[:, i, :], ALU.add).then_inc(rope_ready, 1)

            def k_normalised(g, u, i):
                if i == 0:
                    dve.wait_ge(link, 1 + 1 + RSQRT_STEPS)
                wait(dve, rope_ready, 4 * g + 4 + i + 1)
                heads = rope[:, i, :].rearrange("p (h d) -> p h d", d=HD)
                nc.vector.tensor_tensor(heads, heads, rn[u][:, 8 * i:8 * i + 8].unsqueeze(2).broadcast_to([P, 8, HD]),
                                        ALU.mult).then_inc(kn_ready, 1)

            def add_attention(pair, g, u):
                wait(dve, m_full, m_use(pair, M_WO[u]) + 1)
                at = col0(pair - 1 + PAIRS) + u * P
                nc.vector.tensor_tensor(t.xb[:, bass.ds(at, P)], pm[:, 0:P], t.xa[:, bass.ds(at, P)], ALU.add
                                        ).then_inc(m_done, 1)

            LN_STEPS = RSQRT_STEPS + 4

            def layer_norm(pair, n):
                if isinstance(pair, int) and pair < 2:
                    return
                if n == 0:
                    wait(dve, m_full, m_use(pair, M_TURN) + 1)
                    for c in range(2):
                        nc.vector.bn_stats(st[:, c, :], pm[:, c * P:(c + 1) * P]).then_inc(ffn_link, 1)
                elif n == 1:
                    for c in range(2):
                        dve.wait_ge(ffn_link, c + 1)
                        nc.vector.bn_aggr(mv[:, c, :], st[:, c, :]).then_inc(ffn_link, 1)
                elif n == 2:
                    dve.wait_ge(ffn_link, 4)
                    nc.vector.tensor_scalar(ve[:], mv[:, :, 1], 1e-5, None, ALU.add).then_inc(ffn_link, 1)
                elif n < LN_STEPS - 1:
                    dve.wait_ge(ffn_link, 2 + n)
                    rsqrt_step(nc, n - 3, vr_std[:], ve[:], vh[:]).then_inc(ffn_link, 1)
                else:
                    dve.wait_ge(ffn_link, 2 + n)
                    for c in range(2):
                        last = nc.vector.tensor_scalar(xnt[:, c, :], pm[:, c * P:(c + 1) * P], mv[:, c, 0:1],
                                                       vr_std[:, c:c + 1], ALU.subtract, ALU.mult)
                    last.then_inc(m_done, 1)

            def ffn(pair, k):
                if isinstance(pair, int) and pair < 2:
                    return
                wait(dve, m_full, m_use(pair, k) + 1)
                if k == M_OUT:
                    wait(dve, xs_built, 2 * pair - 1)
                    at = col0(pair - 2 + PAIRS)
                    nc.vector.scalar_tensor_tensor(t.xa[:, bass.ds(at, 2 * P)], pm[:, 0:2 * P], vecs[:, 2:3],
                                                   t.xb[:, bass.ds(at, 2 * P)], ALU.add, ALU.add).then_inc(xa_ready, 1)
                else:
                    n = M_HID.index(k)
                    m = FPARTS[n][1]
                    wait(dve, g_ready, NF * pair + (n + 1 - 2 * NF))
                    nc.vector.scalar_tensor_tensor(hid[0:m, n, :], pm[0:m, 2 * P:4 * P], b1[0:m, n:n + 1], gl[0:m, :],
                                                   ALU.add, ALU.mult).then_inc(m_done, 1)

            dve.sem_inc(rope_ready, 4)
            dve.sem_inc(kn_ready, 2)
            dve.sem_inc(xa_ready, PAIRS)

            def between(pair, u, n):
                if u == 0:
                    layer_norm(pair, n)

            def body(pair):
                for u in range(2):
                    g = 2 * pair + u
                    if not isinstance(g, int) or g > 0:
                        dve.wait_ge(link, 1 + FACTORS)
                    dve.sem_clear(link)
                    dve.sem_clear(mult_done)
                    if u == 0:
                        dve.sem_clear(ffn_link)
                    carry(pair, g, u)
                    if not isinstance(g, int) or g > 0:
                        add_attention(pair - 1 + u, g - 1, 1 - u)
                    copy_kb(g, u, 0)
                    if not isinstance(g, int) or g > 0:
                        inverse_sums(g - 1, 1 - u, 3)
                    copy_kb(g, u, 1)
                    straight(g, u, 0)
                    if u == 1:
                        ffn(pair, M_HID0)
                    straight(g, u, 1)
                    head_norms(g, 0)
                    masked_scores(pair, g, u, 0, 0)
                    masked_scores(pair, g, u, 0, 1)
                    between(pair, u, 0)
                    masked_scores(pair, g, u, 1, 0)
                    between(pair, u, 1)
                    masked_scores(pair, g, u, 1, 1)
                    between(pair, u, 2)
                    if u == 1:
                        ffn(pair, M_HID1)
                    head_norms(g, 1)
                    between(pair, u, 3)
                    straight(g, u, 2)
                    between(pair, u, 4)
                    masked_scores(pair, g, u, 2, 0)
                    between(pair, u, 5)
                    masked_scores(pair, g, u, 2, 1)
                    between(pair, u, 6)
                    masked_scores(pair, g, u, 3, 0)
                    between(pair, u, 7)
                    masked_scores(pair, g, u, 3, 1)
                    between(pair, u, 8)
                    straight(g, u, 3)
                    between(pair, u, 9)
                    head_norms(g, 2)
                    head_norms(g, 3)
                    between(pair, u, 10)
                    factors(g, u, 0)
                    masked_scores(pair, g, u, 4, 0)
                    between(pair, u, 11)
                    factors(g, u, 1)
                    masked_scores(pair, g, u, 4, 1)
                    between(pair, u, 12)
                    factors(g, u, 2)
                    masked_scores(pair, g, u, 5, 0)
                    between(pair, u, 13)
                    factors(g, u, 3)
                    masked_scores(pair, g, u, 5, 1)
                    between(pair, u, 14)
                    factors(g, u, 4)
                    if u == 1:
                        ffn(pair, M_HID2)
                    add_rotated(g, 0)
                    factors(g, u, 5)
                    add_rotated(g, 1)
                    factors(g, u, 6)
                    inverse_sums(g, u, 0)
                    masked_scores(pair, g, u, 6, 0)
                    factors(g, u, 7)
                    masked_scores(pair, g, u, 6, 1)
                    factors(g, u, 8)
                    inverse_sums(g, u, 1)
                    masked_scores(pair, g, u, 7, 0)
                    factors(g, u, 9)
                    masked_scores(pair, g, u, 7, 1)
                    factors(g, u, 10)
                    if u == 1:
                        ffn(pair, M_OUT)
                    add_rotated(g, 2)
                    factors(g, u, 11)
                    add_rotated(g, 3)
                    factors(g, u, 12)
                    k_normalised(g, u, 0)
                    k_normalised(g, u, 1)
                    inverse_sums(g, u, 2)

            over_pairs(dve, body)
            add_attention(steps - 1, 2 * steps - 1, 1)


def finish(nc, t):
    with ExitStack() as ctx:
        turned = [ctx.enter_context(nc.psum_tensor(f"fin_turned{i}", [P, 512], F32)) for i in range(2)]
        full = ctx.enter_context(nc.semaphore("fin_full"))
        summed = ctx.enter_context(nc.semaphore("fin_summed"))
        stored = ctx.enter_context(nc.semaphore("fin_stored"))
        block = ctx.enter_context(nc.Block())
        out = t.out.rearrange("b (c p) d -> p (b c) d", p=P)

        @block.tensor
        def _(pe):
            for n in range(CHUNKS // 4):
                if n >= 2:
                    pe.wait_ge(summed, n - 1)
                at = 4 * n * P + (4 * n) // (S // P) + 1
                for k in range(4):
                    mm = nc.tensor.transpose(turned[n % 2][:, k * P:(k + 1) * P], t.xa[:, at + k * P:at + (k + 1) * P], t.ident[:])
                mm.then_inc(full, 1)

        @block.vector
        def _(dve):
            for n in range(CHUNKS // 4):
                dve.wait_ge(full, n + 1)
                chunk = t.xtok[:, 4 * n:4 * n + 4, :].rearrange("p c d -> p (c d)")
                nc.vector.tensor_tensor(chunk, turned[n % 2][:], chunk, ALU.add).then_inc(summed, 1)

        @block.sync
        def _(sp):
            for n in range(CHUNKS // 4):
                sp.wait_ge(summed, n + 1)
                sp.dma_start(out[:, 4 * n:4 * n + 4, :], t.xtok[:, 4 * n:4 * n + 4, :]).then_inc(stored, 16)
            sp.wait_ge(stored, 16 * (CHUNKS // 4))


class Tensors:
    pass


def build(nc, t, with_attention=True):
    t.q_parts_d = nc.dram_tensor("q_parts", (3, D, B * S), BF16, kind="Internal").ap()
    t.k_parts_d = nc.dram_tensor("k_parts", (3, D, B * S), BF16, kind="Internal").ap()
    with ExitStack() as ctx:
        def sb(name, shape):
            return ctx.enter_context(nc.sbuf_tensor(name, shape, F32))

        t.xtok = sb("xtok", [P, CHUNKS, D])
        t.xa = sb("xa", [P, COLS])
        t.xb = sb("xb", [P, COLS])
        t.ident = sb("ident", [P, P])
        prepare(nc, t)
        if with_attention:
            attention(nc, t)
        windowed(nc, t)
        finish(nc, t)


def shape_constants():
    f = np.float32
    half = np.arange(0, HD, 2, dtype=f)
    inv_freq = (f(1.0) / f(10000.0) ** (half / f(HD))).astype(f)
    tok = np.arange(S, dtype=f)
    freqs = tok[:, None] * inv_freq[None, :]
    freqs = np.concatenate([freqs, freqs], -1)
    base = (half + f(0.4 * HD)) / f(1.4 * HD)
    power = (tok - f(S // 2)) / f(BAND // 2)
    scale = base[None, :] ** power[:, None]
    scale = np.concatenate([scale, scale], -1).astype(f)
    cos, sin = np.cos(freqs).astype(f), np.sin(freqs).astype(f)
    sign = np.where(np.arange(HD) < HD // 2, -1, 1).astype(f)
    inv = f(1.0) / scale
    tab = np.concatenate([cos * scale, sin * scale * sign, cos * inv, sin * inv * sign], 1)
    rope = np.ascontiguousarray(tab.reshape(S // P, P, 4 * HD).transpose(1, 0, 2)).astype(f)
    i, j = np.arange(P)[:, None], np.arange(KEYS)[None, :] - BAND
    odd = np.where((j <= i) & (i <= j + BAND), 0.0, MASKED).astype(f)
    first = np.where(j < 0, f(MASKED), odd).astype(f)
    masks = np.ones((P, PAIRS_B, KEYS + 1), f)
    masks[:, :, :KEYS] = odd[:, None, :]
    masks[:, 0, :KEYS] = first
    masks[:, 0, KEYS] = 0.0
    later = np.where(np.arange(P)[None, :] > np.arange(P)[:, None], f(MASKED), f(0.0)).astype(f)
    return {"ident": np.eye(P, dtype=f), "rope_tab": rope, "mask_tab": masks, "mask_odd": odd,
            "a_masks": np.ascontiguousarray(np.stack([later, later.T], 1))}


_INS = {"L0_attn_x": "x", "L0_attn_W_qkv": "awqkv_d", "L0_attn_q_scale": "aqs_d", "L0_attn_k_scale": "aks_d",
        "L0_attn_W_out": "awout_d", "L0_ffn_Wqkv": "wqkv_d", "L0_ffn_q_scale": "qs_d", "L0_ffn_k_scale": "ks_d",
        "L0_ffn_Wo": "wo_d", "L0_ffn_ln_g": "g_d", "L0_ffn_ln_b": "b_d", "L0_ffn_W1": "w1_d", "L0_ffn_b1": "b1_d",
        "L0_ffn_W2": "w2_d", "L0_ffn_b2": "b2_d"}
_CONSTS = {"ident": "ident_d", "rope_tab": "rope_d", "mask_tab": "mask_d", "mask_odd": "mask_odd_d",
           "a_masks": "amasks_d"}


def kernel(**inputs):
    import concourse.bacc as bacc
    from concourse.bass_utils import run_bass_kernel_spmd

    nc = bacc.Bacc("TRN2", target_bir_lowering=False, num_devices=1)
    t = Tensors()
    arrays = {}

    def dram_in(name, a):
        arrays[name] = a
        return nc.dram_tensor(name, a.shape, mybir.dt.from_np(a.dtype), kind="ExternalInput").ap()

    d = {}
    for name in _INS:
        d[_INS[name]] = dram_in("in_" + name, np.ascontiguousarray(inputs[name]))
    for name, a in shape_constants().items():
        d[_CONSTS[name]] = dram_in("const_" + name, a)
    t.__dict__.update(d)
    t.out = nc.dram_tensor("out", (B, S, D), F32, kind="ExternalOutput").ap()
    build(nc, t)
    r = run_bass_kernel_spmd(nc, [arrays], core_ids=[0])
    return r.results[0]["out"]
```

```python
from contextlib import ExitStack

import numpy as np
import concourse.bass as bass
from concourse import mybir

F32 = mybir.dt.float32
BF16 = mybir.dt.bfloat16
I32 = mybir.dt.int32
ALU = mybir.AluOpType
ACT = mybir.ActivationFunctionType
AX = mybir.AxisListType

P = 128
B, S, D = 4, 1024, 128
CHUNKS = B * S // P
PAIRS = CHUNKS // 2
PAIRS_B = PAIRS // B
COLS = B * (S + 1)

AHD = 8
AG = 4
GROUPS = D // AHD // AG

LAYERS = 6
HEADS, HD = 16, 64
INNER = HEADS * HD
BAND = 32
KEYS = BAND + P
SIM_SCALE = 8.0
FF = int(D * 4 * 2 / 3)
FPARTS = [(f, min(P, FF - f)) for f in range(0, FF, P)]
NF = len(FPARTS)
MASKED = -1e30
RSQRT_MAGIC = float(0x5F3759DF)


def wait(engine, semaphore, value):
    if isinstance(value, int) and value <= 0:
        return
    engine.wait_ge(semaphore, value)


RSQRT_STEPS = 2 + 3 * 3


def rsqrt_step(nc, n, y, x, half):
    v = nc.vector
    if n == 0:
        return v.tensor_scalar(y.bitcast(I32), x.bitcast(I32), 1, None, ALU.logical_shift_right)
    if n == 1:
        return v.tensor_scalar(y.bitcast(I32), y.bitcast(I32), -1.0, RSQRT_MAGIC, ALU.mult, ALU.add)
    if n % 3 == 2:
        return v.tensor_tensor(half, y, y, ALU.mult)
    if n % 3 == 0:
        return v.scalar_tensor_tensor(half, half, -0.5, x, ALU.mult, ALU.mult)
    return v.scalar_tensor_tensor(y, half, 1.5, y, ALU.add, ALU.mult)


def rsqrt_steps(nc, dve, link, link_from, y, x, half):
    for n in range(RSQRT_STEPS):
        rsqrt_step(nc, n, y, x, half).then_inc(link, 1)
        dve.wait_ge(link, link_from + n + 1)


def prepare(nc, t):
    with ExitStack() as ctx:
        stats = ctx.enter_context(nc.sbuf_tensor("pre_stats", [P, CHUNKS, 6], F32))
        mean_var = ctx.enter_context(nc.sbuf_tensor("pre_mean_var", [P, CHUNKS, 2], F32))
        var = ctx.enter_context(nc.sbuf_tensor("pre_var", [P, CHUNKS], F32))
        rstd = ctx.enter_context(nc.sbuf_tensor("pre_rstd", [P, CHUNKS], F32))
        half = ctx.enter_context(nc.sbuf_tensor("pre_half", [P, CHUNKS], F32))
        xn = ctx.enter_context(nc.sbuf_tensor("pre_xn", [P, CHUNKS, D], F32))
        turned = [ctx.enter_context(nc.psum_tensor(f"pre_turned{i}", [P, 512], F32)) for i in range(2)]
        x_loaded = ctx.enter_context(nc.semaphore("pre_x_loaded"))
        stats_done = ctx.enter_context(nc.semaphore("pre_stats_done"))
        link = ctx.enter_context(nc.semaphore("pre_link"))
        xn_done = ctx.enter_context(nc.semaphore("pre_xn_done"))
        turned_full = ctx.enter_context(nc.semaphore("pre_turned_full"))
        turned_read = ctx.enter_context(nc.semaphore("pre_turned_read"))
        padded = ctx.enter_context(nc.semaphore("pre_padded"))
        block = ctx.enter_context(nc.Block())

        @block.sync
        def _(sp):
            sp.dma_start(t.xtok[:], t.x.rearrange("b (c p) d -> p (b c) d", p=P)).then_inc(x_loaded, 16)
            sp.dma_start(t.ident[:], t.ident_d).then_inc(x_loaded, 16)
            sp.wait_ge(x_loaded, 32)

        @block.vector
        def _(dve):
            dve.wait_ge(x_loaded, 32)
            for c in range(CHUNKS):
                nc.vector.bn_stats(stats[:, c, :], t.xtok[:, c, :]).then_inc(stats_done, 1)
            for c in range(CHUNKS):
                dve.wait_ge(stats_done, c + 1)
                nc.vector.bn_aggr(mean_var[:, c, :], stats[:, c, :]).then_inc(stats_done, 1)
            dve.wait_ge(stats_done, 2 * CHUNKS)
            nc.vector.tensor_scalar(var[:], mean_var[:, :, 1], 1e-5, None, ALU.add).then_inc(link, 1)
            dve.wait_ge(link, 1)
            rsqrt_steps(nc, dve, link, 1, rstd[:], var[:], half[:])
            for c in range(CHUNKS):
                nc.vector.tensor_scalar(xn[:, c, :], t.xtok[:, c, :], mean_var[:, c, 0:1], rstd[:, c:c + 1],
                                        ALU.subtract, ALU.mult).then_inc(xn_done, 1)

        @block.tensor
        def _(pe):
            for n in range(CHUNKS // 4):
                pe.wait_ge(xn_done, 4 * n + 4)
                if n >= 2:
                    pe.wait_ge(turned_read, n - 1)
                for k in range(4):
                    mm = nc.tensor.transpose(turned[n % 2][:, k * P:(k + 1) * P], xn[:, 4 * n + k, :], t.ident[:])
                mm.then_inc(turned_full, 1)

        @block.scalar
        def _(act):
            act.wait_ge(padded, 1)
            for n in range(CHUNKS // 4):
                at = 4 * n * P + (4 * n) // (S // P) + 1
                act.wait_ge(turned_full, n + 1)
                nc.scalar.copy(t.xa[:, at:at + 512], turned[n % 2][:]).then_inc(turned_read, 1)

        @block.gpsimd
        def _(pool):
            nc.gpsimd.memset(t.xa[:], 0.0).then_inc(padded, 1)
            nc.gpsimd.memset(t.xb[:], 0.0).then_inc(padded, 1)


def attention(nc, t):
    N_TURNS = 2 * B * S // 512
    with ExitStack() as ctx:
        def sb(name, shape, dt=F32):
            return ctx.enter_context(nc.sbuf_tensor("a_" + name, shape, dt))

        def sem(name):
            return ctx.enter_context(nc.semaphore("a_" + name))

        v_all = sb("v_all", [P, CHUNKS, D])
        w_out = sb("w_out", [P, D])
        ident_bf = sb("ident_bf", [P, P], BF16)
        mask_qk = sb("mask_qk", [P, P], BF16)
        mask_kq = sb("mask_kq", [P, P], BF16)
        q_stack = [sb(f"q_stack{n}", [P, AG, S], BF16) for n in range(GROUPS)]
        k_stack = [sb(f"k_stack{n}", [P, AG, S], BF16) for n in range(GROUPS)]
        v_pad = [sb(f"v_pad{n}", [P, S // P, AG, BAND]) for n in range(2)]
        neg_max = sb("neg_max", [P, S // P, AG, BAND], BF16)

        with ExitStack() as pre:
            def psb(name, shape, dt=F32):
                return pre.enter_context(nc.sbuf_tensor("ap_" + name, shape, dt))

            def psem(name):
                return pre.enter_context(nc.semaphore("ap_" + name))

            wqkv = psb("wqkv", [P, 3 * D])
            masks = psb("masks", [P, 2, P])
            qk = psb("qk", [P, 2, CHUNKS, D])
            stats = psb("stats", [P, 2 * CHUNKS, 6])
            mean_var = psb("mean_var", [P, 2 * CHUNKS, 2])
            var = psb("var", [P, 2 * CHUNKS])
            rstd = psb("rstd", [P, 2 * CHUNKS])
            half = psb("half", [P, 2 * CHUNKS])
            cols = psb("cols", [P, 2])
            SLOTS = 4
            full = [psb(f"full{n}", [P, 512]) for n in range(SLOTS)]
            parts = [psb(f"parts{n}", [P, 3, 512], BF16) for n in range(SLOTS)]
            rest = [psb(f"rest{n}", [P, 512]) for n in range(SLOTS)]
            bank = [pre.enter_context(nc.psum_tensor(f"ap_bank{n}", [P, 512], F32)) for n in range(4)]
            loaded, proj_full, proj_read, stats_done = psem("loaded"), psem("proj_full"), psem("proj_read"), psem("stats_done")
            link, normal, cols_ready, filled = psem("link"), psem("normal"), psem("cols_ready"), psem("filled")
            turned, scaled, rested, parted, last_part = (psem("turned"), psem("scaled"), psem("rested"), psem("parted"),
                                                         psem("last_part"))
            stored = [psem(f"stored{n}") for n in range(SLOTS)]
            LOADED = 16 * 5
            block = pre.enter_context(nc.Block())

            @block.sync
            def _(sp):
                sp.dma_start(wqkv[:], t.awqkv_d).then_inc(loaded, 16)
                sp.dma_start(w_out[:], t.awout_d).then_inc(loaded, 16)
                sp.dma_start(cols[:, 0:1], t.aqs_d.unsqueeze(1)).then_inc(loaded, 16)
                sp.dma_start(cols[:, 1:2], t.aks_d.unsqueeze(1)).then_inc(loaded, 16)
                sp.dma_start(masks[:], t.amasks_d).then_inc(loaded, 16)
                for n in range(N_TURNS):
                    sp.wait_ge(last_part, n + 1)
                    dst = (t.q_parts_d, t.k_parts_d)[n % 2][:, :, (n // 2) * 512:(n // 2 + 1) * 512]
                    sp.dma_start(dst.rearrange("a f t -> f a t"), parts[n % SLOTS][:]
                                 ).then_inc(stored[n % SLOTS], 16)
                for n in range(SLOTS):
                    sp.wait_ge(stored[n], 16 * (N_TURNS // SLOTS))

            @block.tensor
            def _(pe):
                pe.wait_ge(loaded, LOADED)
                for c in range(CHUNKS):
                    if c >= 4:
                        pe.wait_ge(stats_done, 2 * (c - 3))
                    at = c * P + c // (S // P) + 1
                    nc.tensor.matmul(bank[c % 4][:, 0:3 * D], t.xa[:, at:at + P], wqkv[:], start=True, stop=True
                                     ).then_inc(proj_full, 1)
                pe.wait_ge(stats_done, 2 * CHUNKS)
                for n in range(N_TURNS):
                    if n >= 4:
                        pe.wait_ge(scaled, n - 3)
                    pe.wait_ge(normal, 4 * n + 4)
                    for k in range(4):
                        mm = nc.tensor.transpose(bank[n % 4][:, k * P:(k + 1) * P], qk[:, n % 2, 4 * (n // 2) + k, :], t.ident[:])
                    mm.then_inc(turned, 1)

            @block.vector
            def _(dve):
                for c in range(CHUNKS):
                    dve.wait_ge(proj_full, c + 1)
                    dve.wait_ge(proj_read, c + 1)
                    for w in range(2):
                        nc.vector.bn_stats(stats[:, 2 * c + w, :], bank[c % 4][:, w * D:(w + 1) * D]).then_inc(stats_done, 1)
                for c in range(2 * CHUNKS):
                    dve.wait_ge(stats_done, c + 1)
                    nc.vector.bn_aggr(mean_var[:, c, :], stats[:, c, :]).then_inc(link, 1)
                dve.wait_ge(link, 2 * CHUNKS)
                nc.vector.tensor_scalar(var[:], mean_var[:, :, 1], 1e-6, None, ALU.add).then_inc(link, 1)
                dve.wait_ge(link, 2 * CHUNKS + 1)
                rsqrt_steps(nc, dve, link, 2 * CHUNKS + 1, rstd[:], var[:], half[:])
                dve.wait_ge(loaded, LOADED)
                nc.vector.tensor_scalar(cols[:, 0:1], cols[:, 0:1], float(AHD) ** -0.5, None, ALU.mult).then_inc(cols_ready, 1)
                for n in range(N_TURNS + 2):
                    if n < N_TURNS:
                        for k in range(4):
                            c, w = 4 * (n // 2) + k, n % 2
                            m = 2 * c + w
                            nc.vector.tensor_scalar(qk[:, w, c, :], qk[:, w, c, :], mean_var[:, m, 0:1], rstd[:, m:m + 1],
                                                    ALU.subtract, ALU.mult).then_inc(normal, 1)
                    if n >= 2:
                        unit = n - 2
                        s = unit % SLOTS
                        dve.wait_ge(parted, max(2 * unit, 1))
                        if unit >= SLOTS:
                            dve.wait_ge(last_part, unit - SLOTS + 1)
                        nc.vector.tensor_tensor(rest[s][:], full[s][:], parts[s][:, 0, :], ALU.subtract).then_inc(rested, 1)
                dve.wait_ge(filled, 1)
                for n in range(GROUPS):
                    nc.vector.memset(k_stack[n][96:99, :, :], 1.0)
                for n in range(2):
                    nc.vector.memset(v_pad[n][:, :, :, AHD:AHD + 1], 1.0)

            @block.scalar
            def _(act):
                act.wait_ge(loaded, LOADED)
                nc.scalar.copy(ident_bf[:], t.ident[:])
                nc.scalar.copy(mask_qk[:], masks[:, 0, :])
                nc.scalar.copy(mask_kq[:], masks[:, 1, :])
                for c in range(CHUNKS):
                    act.wait_ge(proj_full, c + 1)
                    nc.scalar.copy(qk[:, :, c, :], bank[c % 4][:, 0:2 * D].rearrange("p (w d) -> p w d", w=2))
                    nc.scalar.copy(v_all[:, c, :], bank[c % 4][:, 2 * D:3 * D]).then_inc(proj_read, 1)
                act.wait_ge(cols_ready, 1)
                for n in range(N_TURNS):
                    s = n % SLOTS
                    act.wait_ge(turned, n + 1)
                    if n >= SLOTS:
                        act.wait_ge(rested, n - SLOTS + 1)
                        act.wait_ge(stored[s], 16 * (n // SLOTS))
                    nc.scalar.activation(full[s][:], bank[n % 4][:], ACT.Copy, scale=cols[:, n % 2:n % 2 + 1]).then_inc(scaled, 1)
                    act.wait_ge(scaled, n + 1)
                    nc.scalar.copy(parts[s][:, 0, :], full[s][:]).then_inc(parted, 1)
                    if n >= 1:
                        act.wait_ge(rested, n)
                        before = (n - 1) % SLOTS
                        nc.scalar.copy(parts[before][:, 1, :], rest[before][:]).then_inc(parted, 1)
                act.wait_ge(rested, N_TURNS)
                nc.scalar.copy(parts[SLOTS - 1][:, 1, :], rest[SLOTS - 1][:]).then_inc(parted, 1)

            @block.gpsimd
            def _(pool):
                for buf in (*k_stack, *v_pad, *q_stack, neg_max):
                    last = nc.gpsimd.memset(buf[:], 0.0)
                last.then_inc(filled, 1)
                for n in range(N_TURNS):
                    s = n % SLOTS
                    pool.wait_ge(parted, min(2 * n + 3, 2 * N_TURNS))
                    nc.gpsimd.tensor_tensor(parts[s][:, 2, :], rest[s][:], parts[s][:, 1, :], ALU.subtract
                                            ).then_inc(last_part, 1)

        probs = [sb(f"probs{n}", [P, AG, S]) for n in range(2)]
        row_max = sb("row_max", [P, AG, S // P])
        max_b = sb("max_b", [P, AG, S // P])
        max_rest = sb("max_rest", [P, AG, S // P])
        ctx_t = sb("ctx_t", [P, S])
        inv = sb("inv", [P, 2, 4, AG])
        ctx_tok = sb("ctx_tok", [P, S // P, D])
        ctx_f = sb("ctx_f", [P, S])

        ring = [ctx.enter_context(nc.psum_tensor(f"a_ring{n}", [P, 512], F32)) for n in range(2)]
        wide_bank = [ctx.enter_context(nc.psum_tensor(f"a_wide{n}", [P, S], F32)) for n in range(2)]
        out_bank = ctx.enter_context(nc.psum_tensor("a_out", [P, S], F32))

        stacked = [sem(f"stacked{n}") for n in range(GROUPS)]
        r_full, r_done = sem("r_full"), sem("r_done")
        split_done, max_placed = sem("split_done"), sem("max_placed")
        wide_full, exp_done, pv_done, pv_read = sem("wide_full"), sem("exp_done"), sem("pv_done"), sem("pv_read")
        v_ready, link = sem("v_ready"), sem("link")

        units = [(c, k0, min(512, (c + 1) * P - k0)) for c in range(S // P) for k0 in range(0, (c + 1) * P, 512)]
        KC = S // P
        NMAX = AG * len(units)
        TURN_MAX, TURN_CTX, PROJECT = NMAX, NMAX + 1, NMAX + 3
        STEP, BATCH = NMAX + 3, GROUPS * (NMAX + 3) + 4

        def ring_at(b, hg, n):
            if isinstance(b, int) and b == 0 and hg == 0:
                return n
            return BATCH * b + (STEP * hg + (4 if hg > 0 else 0) - 6 + n)

        def bank_at(hg, n):
            return ring[(STEP * hg + n) % 2]

        def is_first(b, hg):
            return isinstance(b, int) and b == 0 and hg == 0

        def over_batches(engine, step, last):
            for hg in range(GROUPS):
                step(0, hg)
            with engine.Fori(1, B) as b:
                for hg in range(GROUPS):
                    step(b, hg)
            last()

        block = ctx.enter_context(nc.Block())

        @block.sync
        def _(sp):
            def stacks(b, hg):
                toks = bass.ds(b * S, S)
                rows = slice(AG * AHD * hg, AG * AHD * (hg + 1))
                for a in range(3):
                    for j in range(3):
                        at = AHD * (3 * a + j)
                        for stack, src in ((q_stack, t.q_parts_d[a]), (k_stack, t.k_parts_d[j])):
                            sp.dma_start(stack[hg][at:at + AHD, :, :], src[rows, toks].rearrange("(h r) t -> r h t", h=AG)
                                         ).then_inc(stacked[hg], 16)

            for hg in range(GROUPS):
                stacks(0, hg)
            with sp.Fori(1, B) as b:
                for hg in range(GROUPS):
                    sp.wait_ge(wide_full, AG * KC * GROUPS * b + (AG * KC * (hg + 1 - GROUPS)))
                    stacks(b, hg)
            for hg in range(GROUPS):
                sp.wait_ge(stacked[hg], 16 * 18 * B)

        @block.tensor
        def _(pe):
            def maxima(b, hg, n):
                hh, (c, k0, width) = n // len(units), units[n % len(units)]
                wait(pe, r_done, ring_at(b, hg, n) - 1)
                bank = bank_at(hg, n)
                diagonal = k0 + width == (c + 1) * P
                mm = nc.tensor.matmul(bank[:, 0:width], q_stack[hg][0:96, hh, c * P:(c + 1) * P],
                                      k_stack[hg][0:96, hh, k0:k0 + width], start=True, stop=True)
                if diagonal:
                    mm = nc.tensor.matmul(bank[:, width - P:width], ident_bf[:], mask_qk[:], start=False, stop=True,
                                          skip_group_check=True)
                mm.then_inc(r_full, 1)

            def turn_maxima(b, hg):
                wait(pe, r_done, ring_at(b, hg, TURN_MAX) - 1)
                wait(pe, split_done, GROUPS * b + (hg + 1))
                bank = bank_at(hg, TURN_MAX)[:].bitcast(BF16)
                for c in range(KC):
                    mm = nc.tensor.transpose(bank[:, c * P:(c + 1) * P], neg_max[:, c, :, :].rearrange("p h k -> p (h k)"),
                                             ident_bf[:])
                mm.then_inc(r_full, 1)

            def scores(n2, hg, kc, hh):
                width = S - kc * P
                if kc == 0 and hh == 0:
                    wait(pe, max_placed, n2 + 1)
                w = AG * kc + hh
                wait(pe, exp_done, n2 * (AG * KC) + (w - 1))
                bank = wide_bank[w % 2]
                for at in range(0, width, 512):
                    n = min(512, width - at)
                    mm = nc.tensor.matmul(bank[:, at:at + n], k_stack[hg][:, hh, kc * P:(kc + 1) * P],
                                          q_stack[hg][:, hh, kc * P + at:kc * P + at + n], start=True, stop=True)
                mm = nc.tensor.matmul(bank[:, 0:P], ident_bf[:], mask_kq[:], start=False, stop=True, skip_group_check=True)
                mm.then_inc(wide_full, 1)

            def values(n2, hg, kc):
                wait(pe, exp_done, n2 * (AG * KC) + AG * (kc + 1))
                if kc == 0:
                    wait(pe, pv_read, n2)
                    wait(pe, v_ready, n2 + 1)
                for q0 in range(0, S, 512):
                    lo = max(q0, kc * P)
                    if lo >= q0 + 512:
                        continue
                    for hh in range(AG):
                        mm = nc.tensor.matmul(out_bank[BAND * hh:BAND * (hh + 1), lo:q0 + 512], v_pad[hg % 2][:, kc, hh, :],
                                              probs[kc % 2][:, hh, lo - kc * P:q0 + 512 - kc * P],
                                              start=(kc == 0), stop=(kc == KC - 1), skip_group_check=True)
                mm.then_inc(pv_done, 1)

            def turn_context(n2, b, hg, n0):
                wait(pe, pv_read, n2 + 1)
                for n in range(2):
                    wait(pe, r_done, ring_at(b, hg, n0 + n) - 1)
                    for k in range(4):
                        c = 4 * n + k
                        mm = nc.tensor.transpose(bank_at(hg, n0 + n)[:, k * P:(k + 1) * P], ctx_t[:, c * P:(c + 1) * P], t.ident[:])
                    mm.then_inc(r_full, 1)

            def project(b, hg, n0):
                for n in range(2):
                    wait(pe, r_done, ring_at(b, hg, n0))
                    if n == 1:
                        wait(pe, r_done, ring_at(b, hg, n0 + n) - 1)
                    for k in range(4):
                        mm = nc.tensor.transpose(bank_at(hg, n0 + n)[:, k * P:(k + 1) * P], ctx_tok[:, 4 * n + k, :], t.ident[:])
                    mm.then_inc(r_full, 1)
                for n in range(2):
                    wait(pe, r_done, ring_at(b, hg, n0 + 2))
                    for k in range(4):
                        c = 4 * n + k
                        mm = nc.tensor.matmul(bank_at(hg, n0 + 2 + n)[:, k * P:(k + 1) * P], ctx_f[:, c * P:(c + 1) * P],
                                              w_out[:], start=True, stop=True)
                    mm.then_inc(r_full, 1)

            def step(b, hg):
                wait(pe, stacked[hg], 16 * 18 * (b + 1))
                n2, before = GROUPS * b + (hg - 1), (hg - 1) % GROUPS
                share = NMAX // KC
                for kc in range(KC):
                    for m in range(share):
                        maxima(b, hg, kc * share + m)
                        if not is_first(b, hg) and m < AG:
                            scores(n2, before, kc, m)
                    if not is_first(b, hg) and kc >= 1:
                        values(n2, before, kc - 1)
                turn_maxima(b, hg)
                if not is_first(b, hg):
                    values(n2, before, KC - 1)
                    turn_context(n2, b, hg, TURN_CTX)
                    if hg == 0:
                        project(b, hg, PROJECT)

            def last():
                n2, before = GROUPS * B - 1, GROUPS - 1
                for kc in range(KC):
                    for hh in range(AG):
                        scores(n2, before, kc, hh)
                    if kc >= 1:
                        values(n2, before, kc - 1)
                values(n2, before, KC - 1)
                turn_context(n2, B, 0, 0)
                project(B, 0, 2)

            over_batches(pe, step, last)

        @block.scalar
        def _(act):
            def exps(n2):
                for kc in range(KC):
                    for hh in range(AG):
                        w = AG * kc + hh
                        width = S - kc * P
                        wait(act, wide_full, n2 * (AG * KC) + (w + 1))
                        if hh == 0:
                            wait(act, pv_done, n2 * KC + (kc - 1))
                        nc.scalar.activation(probs[kc % 2][:, hh, 0:width], wide_bank[w % 2][:, 0:width], ACT.Exp
                                             ).then_inc(exp_done, 1)

            def copy_context(n2, b, hg):
                wait(act, pv_done, n2 * KC + KC)
                nc.scalar.copy(ctx_t[:], out_bank[:]).then_inc(pv_read, 1)

            def step(b, hg):
                if is_first(b, hg):
                    return
                n2 = GROUPS * b + (hg - 1)
                exps(n2)
                copy_context(n2, b, hg)

            def last():
                exps(GROUPS * B - 1)
                copy_context(GROUPS * B - 1, B, 0)

            over_batches(act, step, last)

        @block.gpsimd
        def _(pool):
            def step(b, hg):
                wait(pool, pv_done, KC * GROUPS * b + KC * (hg - 1))
                src = v_all[:, bass.ds(b * KC, KC), AG * AHD * hg:AG * AHD * (hg + 1)]
                nc.gpsimd.tensor_copy(v_pad[hg % 2][:, :, :, 0:AHD], src.rearrange("p c (h d) -> p c h d", h=AG)
                                      ).then_inc(v_ready, 1)

            over_batches(pool, step, lambda: None)

        @block.vector
        def _(dve):
            def maxima(b, hg, n):
                hh, (c, k0, width) = n // len(units), units[n % len(units)]
                wait(dve, r_full, ring_at(b, hg, n) + 1)
                into = (max_b if k0 > 0 else row_max)[:, hh, c:c + 1]
                nc.vector.tensor_reduce(into, bank_at(hg, n)[:, 0:width], AX.X, ALU.max).then_inc(r_done, 1)

            def split_maxima(b, hg):
                dve.sem_clear(link)
                wait(dve, r_done, ring_at(b, hg, NMAX))
                part = [neg_max[:, :, :, n].rearrange("p c h -> p h c") for n in range(3)]
                half = KC // 2
                at = 0

                def linked(instruction):
                    nonlocal at
                    at += 1
                    instruction.then_inc(link, 1)
                    dve.wait_ge(link, at)

                linked(nc.vector.tensor_tensor(row_max[:, :, half:KC], row_max[:, :, half:KC], max_b[:, :, half:KC], ALU.max))
                linked(nc.vector.tensor_scalar(part[0], row_max[:], -1.0, None, ALU.mult))
                linked(nc.vector.scalar_tensor_tensor(max_rest[:], row_max[:], -1.0, part[0], ALU.mult, ALU.subtract))
                linked(nc.vector.tensor_copy(part[1], max_rest[:]))
                nc.vector.tensor_tensor(part[2], max_rest[:], part[1], ALU.subtract).then_inc(split_done, 1)

            def place_maxima(b, hg):
                wait(dve, r_full, ring_at(b, hg, TURN_MAX) + 1)
                bank = bank_at(hg, TURN_MAX)[:].bitcast(BF16)
                for hh in range(AG):
                    last = nc.vector.tensor_copy(q_stack[hg][96:P, hh, :], bank[BAND * hh:BAND * (hh + 1), :])
                    if hh < AG - 1:
                        last.then_inc(max_placed_parts, 1)
                last.then_inc(max_placed, 1)
                dve.wait_ge(max_placed, GROUPS * b + (hg + 1))
                dve.sem_inc(r_done, 1)

            def normalise(b, hg, n0, before):
                dve.sem_clear(link)
                for n in range(2):
                    wait(dve, r_full, ring_at(b, hg, n0 + n) + 1)
                    bank = bank_at(hg, n0 + n)[:].rearrange("p (c h d) -> p c h d", c=4, h=AG)
                    nc.vector.reciprocal(inv[:, n], bank[:, :, :, AHD]).then_inc(link, 1)
                    dve.wait_ge(link, n + 1)
                    out = ctx_tok[:, 4 * n:4 * n + 4, AG * AHD * before:AG * AHD * (before + 1)]
                    nc.vector.tensor_tensor(out.rearrange("p c (h d) -> p c h d", h=AG), bank[:, :, :, 0:AHD],
                                            inv[:, n].unsqueeze(3).broadcast_to([P, 4, AG, AHD]), ALU.mult).then_inc(r_done, 1)

            def project(b, hg, n0):
                for n in range(2):
                    wait(dve, r_full, ring_at(b, hg, n0 + n) + 1)
                    nc.vector.tensor_copy(ctx_f[:, 512 * n:512 * (n + 1)], bank_at(hg, n0 + n)[:]).then_inc(r_done, 1)
                for n in range(2):
                    wait(dve, r_full, ring_at(b, hg, n0 + 2 + n) + 1)
                    chunk = t.xtok[:, bass.ds((b - 1) * KC + 4 * n, 4), :].rearrange("p c d -> p (c d)")
                    nc.vector.tensor_tensor(chunk, bank_at(hg, n0 + 2 + n)[:], chunk, ALU.add).then_inc(r_done, 1)

            max_placed_parts = sem("max_placed_parts")

            def step(b, hg):
                for n in range(NMAX):
                    maxima(b, hg, n)
                split_maxima(b, hg)
                place_maxima(b, hg)
                if not is_first(b, hg):
                    normalise(b, hg, TURN_CTX, (hg - 1) % GROUPS)
                    if hg == 0:
                        project(b, hg, PROJECT)

            def last():
                normalise(B, 0, 0, GROUPS - 1)
                project(B, 0, 2)

            over_batches(dve, step, last)


def windowed(nc, t):
    with ExitStack() as ctx:
        def sb(name, shape, dt=F32):
            return ctx.enter_context(nc.sbuf_tensor("w_" + name, shape, dt))

        def sem(name):
            return ctx.enter_context(nc.semaphore("w_" + name))

        wqkv = sb("wqkv", [P, 2, 3 * INNER])
        scales = sb("scales", [P, 2, 4 * HD])
        wo = sb("wo", [P, HEADS // 2, D])
        w1 = sb("w1", [P, 2 * FF])
        w2 = sb("w2", [P, NF, D])
        b1 = sb("b1", [P, 2 * NF])
        vecs = sb("vecs", [P, 3])
        rope_tab = sb("rope_tab", [P, S // P, 4 * HD])
        mask_tab = sb("mask_tab", [P, PAIRS_B, KEYS + 1])
        mask_odd = sb("mask_odd", [P, KEYS])
        xs = [sb(f"xs{u}", [P, P]) for u in range(2)]
        raw = sb("raw", [P, 4, 512])
        sq = sb("sq", [P, 4, 512])
        rot = sb("rot", [P, 4, 512])
        rope = sb("rope", [P, 4, 512])
        tc = [sb(f"tc{u}", [P, 4 * HD]) for u in range(2)]
        ss = sb("ss", [P, 2 * HEADS])
        rn = [sb(f"rn{u}", [P, 2 * HEADS]) for u in range(2)]
        nhalf = sb("nhalf", [P, 2 * HEADS])
        qt = sb("qt", [P, HEADS // 2, P])
        kb = sb("kb", [P, HEADS // 2, 2, KEYS])
        mask = sb("mask", [P, KEYS + 1])
        v = [sb(f"v{u}", [P, INNER]) for u in range(2)]
        vr = [sb(f"vr{u}", [P, 4, HD]) for u in range(2)]
        p = [sb(f"p{u}", [P, HEADS, KEYS]) for u in range(2)]
        pc = [sb(f"pc{u}", [P, 4, 4, BAND]) for u in range(2)]
        nb = [sb(f"nb{u}", [P, HEADS]) for u in range(2)]
        rs = [sb(f"rs{u}", [P, HEADS]) for u in range(2)]
        rinv = [sb(f"rinv{u}", [P, HEADS]) for u in range(2)]
        pts = sb("pts", [P, 2, 512])
        bd = sb("bd", [P, 4, 4, BAND])
        ot = sb("ot", [P, HEADS // 2, P])
        xf = sb("xf", [P, 2 * P])
        st = sb("st", [P, 2, 6])
        mv = sb("mv", [P, 2, 2])
        ve = sb("ve", [P, 2])
        vh = sb("vh", [P, 2])
        vr_std = sb("vr_std", [P, 2])
        xnt = sb("xnt", [P, 2, P])
        xnf = sb("xnf", [P, 2 * P])
        gl = sb("gl", [P, 2 * P])
        hid = sb("hid", [P, NF, 2 * P])

        def banks(name, n):
            return [ctx.enter_context(nc.psum_tensor(f"w_{name}{i}", [P, 512], F32)) for i in range(n)]

        px, pt, ps = banks("px", 2), banks("pt", 2), banks("ps", 2)
        po, pm = banks("po", 1)[0], banks("pm", 1)[0]

        w_early = sem("w_early")
        w_wo = sem("w_wo")
        w_ffn = sem("w_ffn")
        consts = sem("consts")
        xs_built = sem("xs_built")
        x_full, x_done = sem("x_full"), sem("x_done")
        sq_pool, sq_act, red_done = sem("sq_pool"), sem("sq_act"), sem("red_done")
        POOL_SQUARES = 2
        kn_ready, tc_ready, rot_ready, rope_ready = sem("kn_ready"), sem("tc_ready"), sem("rot_ready"), sem("rope_ready")
        t_full, t_act, t_dve = sem("t_full"), sem("t_act"), sem("t_dve")
        s_full, s_done = sem("s_full"), sem("s_done")
        mask_ready = sem("mask_ready")
        corner_ready = sem("corner_ready")
        exp_done, rinv_ready, p_ready = sem("exp_done"), sem("rinv_ready"), sem("p_ready")
        pv_full, o_done = sem("pv_full"), sem("o_done")
        vr_ready = [sem(f"vr_ready{u}") for u in range(2)]
        m_full, m_done, g_ready = sem("m_full"), sem("m_done"), sem("g_ready")
        xf_ready, xa_ready = sem("xf_ready"), sem("xa_ready")
        link, ffn_link = sem("link"), sem("ffn_link")
        DVE_STRAIGHT = 2
        mult_done, carried = sem("mult_done"), sem("carried")
        apart = sem("apart")
        CONSTS = 3 * 16

        with nc.Block() as block:
            @block.sync
            def _(sp):
                sp.dma_start(rope_tab[:], t.rope_d).then_inc(consts, 16)
                sp.dma_start(mask_tab[:], t.mask_d).then_inc(consts, 16)
                sp.dma_start(mask_odd[:], t.mask_odd_d).then_inc(consts, 16)
                sp.wait_ge(consts, CONSTS)

            @block.vector
            def _(dve):
                for bank in ps:
                    nc.vector.memset(bank[:], 0.0)

            @block.gpsimd
            def _(pool):
                for buf in (rope, kb, v[0], v[1], vr[0], vr[1], p[0], p[1], pc[0], pc[1], bd, rn[0], rn[1], qt, raw):
                    nc.gpsimd.memset(buf[:], 0.0)

        def m_use(pp, k):
            if isinstance(pp, int) and pp < 2:
                return 2 * pp + (k == M_WO[1])
            return 8 * pp + (k - 12)

        def m_read(pp, k):
            if isinstance(pp, int) and pp < 2:
                return 2 * pp + (k == M_WO[1])
            return 7 * pp + (min(k, M_OUT) - 10)

        M_TURN, M_BACK, M_HID0, M_HID1, M_HID2, M_OUT = 0, 1, 3, 4, 5, 6
        M_WO = (2, 7)
        M_HID = (M_HID0, M_HID1, M_HID2)

        UNIT_AT = (2, 3, 0, 1, 4, 5)
        T_UNIT = (0, 2, 1, 3)
        T_P, T_CORNER, T_USES = (4, 5, 7, 8), 6, 9

        def wide(ap, heads=8):
            return ap.unsqueeze(1).broadcast_to([P, heads, ap.shape[-1]])

        def col0(pair):
            q = pair % PAIRS
            return q * (2 * P) + q // PAIRS_B + 1

        def straight(engine, ops, g, u, i):
            if i in (0, DVE_STRAIGHT):
                wait(engine, tc_ready, g + 1)
            wait(engine, x_done, 6 * g + i + 1)
            wait(engine, t_full, T_USES * g + T_UNIT.index(i) + 1)
            which = 1 - i // 2
            ins = ops.tensor_tensor(rope[:, i, :].rearrange("p (h d) -> p h d", d=HD),
                                    raw[:, i, :].rearrange("p (h d) -> p h d", d=HD),
                                    wide(tc[u][:, 2 * which * HD:(2 * which + 1) * HD]), ALU.mult)
            if i < DVE_STRAIGHT:
                ins.then_inc(mult_done, 1)

        block = ctx.enter_context(nc.Block())

        @block.sync
        def _(sp):
            def load_early(layer, slot):
                sp.dma_start(wqkv[:, bass.ds(slot, 1), :].rearrange("p s n -> p (s n)"), t.wqkv_d[bass.ds(layer, 1)].rearrange("l p n -> (l p) n")
                             ).then_inc(w_early, 16)
                for which, scale in ((0, t.qs_d), (2, t.ks_d)):
                    row = scale[bass.ds(layer, 1)]
                    for n, half in enumerate((row, row[:, HD // 2:HD], row[:, 0:HD // 2])):
                        at = which * HD + (0, HD, HD + HD // 2)[n]
                        width = half.shape[-1]
                        sp.dma_start(scales[:, bass.ds(slot, 1), at:at + width].rearrange("p s n -> p (s n)"), half.broadcast_to([P, width])
                                     ).then_inc(w_early, 16)

            def load_wo(layer):
                sp.dma_start(wo[:], t.wo_d[bass.ds(layer, 1)].rearrange("l (j p) n -> p (l j) n", p=P)
                             ).then_inc(w_wo, 16)

            def load_ffn(layer):
                one = bass.ds(layer, 1)
                sp.dma_start(w1[:], t.w1_d[one].rearrange("l p n -> (l p) n")).then_inc(w_ffn, 16)
                for n, (f, m) in enumerate(FPARTS):
                    sp.dma_start(w2[0:m, n, :], t.w2_d[one, f:f + m].rearrange("l p n -> (l p) n")).then_inc(w_ffn, 16)
                    for half in range(2):
                        src = t.b1_d[one, half * FF + f:half * FF + f + m].rearrange("l p -> p l")
                        at = half * NF + n
                        sp.dma_start(b1[0:m, at:at + 1], src).then_inc(w_ffn, 16)
                for n, vec in enumerate((t.g_d, t.b_d, t.b2_d)):
                    sp.dma_start(vecs[:, n:n + 1], vec[one].rearrange("l p -> p l")).then_inc(w_ffn, 16)

            def v_tail(pair, u):
                g = 2 * pair + u
                wait(sp, x_done, 6 * g + 6)
                wait(sp, pv_full, 2 * g + 4)
                src = v[u][P - BAND:P, :].rearrange("p (r h e d) -> p h r e d", r=2, h=4, e=2)
                for hh in range(4):
                    for r in range(2):
                        sp.dma_start(vr[u][BAND * hh:BAND * (hh + 1), 2 * r:2 * r + 2, :], src[:, hh, r]
                                     ).then_inc(vr_ready[u], 16)

            load_early(0, 0)
            load_wo(0)
            load_ffn(0)
            v_tail(0, 0)
            v_tail(0, 1)
            load_early(1, 1)
            with sp.Fori(1, PAIRS) as q:
                v_tail(q, 0)
                v_tail(q, 1)

            def layer_loads(layer, more):
                first = layer * PAIRS
                v_tail(first, 0)
                sp.wait_ge(m_full, m_use(first, M_WO[1]) + 1)
                load_wo(layer)
                v_tail(first, 1)
                v_tail(first + 1, 0)
                sp.wait_ge(xa_ready, first + PAIRS)
                load_ffn(layer)
                v_tail(first + 1, 1)
                if more:
                    load_early(layer + 1, (layer + 1) % 2)
                with sp.Fori(2, PAIRS) as q:
                    v_tail(first + q, 0)
                    v_tail(first + q, 1)

            if LAYERS > 2:
                with sp.Fori(1, LAYERS - 1) as layer:
                    layer_loads(layer, True)
            layer_loads(LAYERS - 1, False)
            v_tail(LAYERS * PAIRS, 0)
            v_tail(LAYERS * PAIRS, 1)
            for u in range(2):
                sp.wait_ge(vr_ready[u], 128 * (LAYERS * PAIRS + 1))

        steps = LAYERS * PAIRS + 2

        def over_pairs(engine, body):
            body(0)
            body(1)
            with engine.Fori(2, steps - 2) as pair:
                body(pair)
            body(steps - 2)
            body(steps - 1)

        def layer_loaded(engine, semaphore, per_layer, pair, lag):
            if isinstance(pair, int):
                layer = min(max(pair - lag, 0) // PAIRS, LAYERS - 1)
                engine.wait_ge(semaphore, per_layer * (layer + 1))
            else:
                engine.wait_ge(semaphore, ((pair + (PAIRS - lag)) // PAIRS) * per_layer)

        N_EARLY, N_WO, N_FFN = 16 * 7, 16, 16 * (1 + 3 * NF + 3)

        @block.tensor
        def _(pe):
            def qkv(pair, g, u, i):
                if i == 0:
                    layer_loaded(pe, w_early, N_EARLY, pair, 0)
                    wait(pe, xs_built, g + 1)
                wait(pe, x_done, 6 * g + i - 1)
                slot = (pair // PAIRS) % 2
                at = UNIT_AT[i] * 512
                rhs = wqkv[:, bass.ds(slot, 1), at:at + 512].rearrange("p s n -> p (s n)")
                nc.tensor.matmul(px[i % 2][:], xs[u][:], rhs, start=True, stop=True).then_inc(x_full, 1)

            def t_bank(u, k):
                return pt[(T_USES * u + k) % 2]

            def turn_qk(g, u, i):
                unit = T_UNIT[i]
                if unit < 2:
                    wait(pe, kn_ready, 2 * g + unit + 1)
                else:
                    wait(pe, rope_ready, 4 * g + unit + 1)
                wait(pe, t_act, T_USES * g + i - 1)
                if i == 2:
                    wait(pe, t_dve, 2 * g + 1)
                for j in range(4):
                    mm = nc.tensor.transpose(t_bank(u, i)[:, j * P:(j + 1) * P], rope[:, unit, j * P:(j + 1) * P], t.ident[:])
                mm.then_inc(t_full, 1)

            def turn_p(g, u, i):
                k = T_P[i]
                wait(pe, p_ready, 4 * g + i + 1)
                wait(pe, t_act, T_USES * g + k - 1)
                if i == 0:
                    wait(pe, t_dve, 2 * g + 2)
                for j in range(4):
                    mm = nc.tensor.transpose(t_bank(u, k)[:, j * P:(j + 1) * P], p[u][:, 4 * i + j, BAND:KEYS], t.ident[:])
                mm.then_inc(t_full, 1)

            def turn_corner(g, u):
                wait(pe, corner_ready, 4 * g + 4)
                wait(pe, t_act, T_USES * g + T_CORNER - 1)
                pe.sem_inc(apart, 1)
                for s in range(4):
                    src = pc[u][0:BAND, s, :, :].rearrange("p h k -> p (h k)")
                    mm = nc.tensor.transpose(t_bank(u, 6)[:, s * BAND:(s + 1) * BAND], src, t.ident[0:BAND, 0:BAND])
                mm.then_inc(t_full, 1)

            def scores(g, u, j):
                if j == 0:
                    wait(pe, t_act, T_USES * g + 4)
                    wait(pe, t_dve, 2 * g + 2)
                wait(pe, s_done, 8 * g + j - 1)
                for half in range(2):
                    rows, keys = slice(HD * half, HD * (half + 1)), slice(HD * half, HD * half + HD + BAND)
                    out = ps[j % 2][rows, 0:2 * KEYS].rearrange("p (e k) -> p e k", e=2)[:, :, keys]
                    mm = nc.tensor.matmul(out, qt[:, j, rows], kb[:, j, :, keys], start=True, stop=True)
                mm.then_inc(s_full, 1)

            def context(pair, g, u, r):
                wait(pe, t_act, T_USES * g + (T_CORNER, T_P[3])[r] + 1)
                wait(pe, o_done, 2 * g + r)
                if r == 0:
                    wait(pe, x_done, 6 * (g - 2) + 6)
                    wait(pe, vr_ready[1 - u], 128 * (pair - 1 + u))
                for j in range(4):
                    for e in range(2):
                        h = 2 * (4 * r + j) + e
                        nc.tensor.matmul(po[HD * e:HD * (e + 1), j * P:(j + 1) * P], v[u][:, h * HD:(h + 1) * HD],
                                         pts[:, (h // 4) % 2, (h % 4) * P:(h % 4 + 1) * P],
                                         start=(j == 0), stop=False, skip_group_check=True)
                for e in range(2):
                    out = po[HD * e:HD * (e + 1), :].rearrange("p (j i) -> p j i", j=4)[:, :, 0:BAND]
                    mm = nc.tensor.matmul(out, vr[1 - u][:, 2 * r + e, :], bd[:, 2 * r + e, :, :],
                                          start=False, stop=True, skip_group_check=True)
                mm.then_inc(pv_full, 1)

            def project(pair, g, u):
                if u == 0:
                    layer_loaded(pe, w_wo, N_WO, pair, 1)
                wait(pe, o_done, 2 * g + 2)
                wait(pe, m_done, m_read(pair, M_WO[u]))
                if u == 1 and not (isinstance(pair, int) and pair < 2):
                    wait(pe, xa_ready, pair + (PAIRS - 1))
                for j in range(HEADS // 2):
                    mm = nc.tensor.matmul(pm[:, 0:P], wo[:, j, :], ot[:, j, :], start=(j == 0), stop=(j == HEADS // 2 - 1))
                mm.then_inc(m_full, 1)

            def ffn(pair, k):
                if isinstance(pair, int) and pair < 2:
                    return
                wait(pe, m_done, m_read(pair, k))
                if k == M_TURN:
                    wait(pe, xf_ready, pair - 1)
                    for c in range(2):
                        mm = nc.tensor.transpose(pm[:, c * P:(c + 1) * P], xf[:, c * P:(c + 1) * P], t.ident[:])
                elif k == M_BACK:
                    for c in range(2):
                        mm = nc.tensor.transpose(pm[:, c * P:(c + 1) * P], xnt[:, c, :], t.ident[:])
                elif k == M_OUT:
                    for n, (f, m) in enumerate(FPARTS):
                        mm = nc.tensor.matmul(pm[:, 0:2 * P], w2[0:m, n, :], hid[0:m, n, :], start=(n == 0), stop=(n == NF - 1))
                else:
                    n = M_HID.index(k)
                    if n == 0:
                        layer_loaded(pe, w_ffn, N_FFN, pair, 2)
                    f, m = FPARTS[n]
                    nc.tensor.matmul(pm[0:m, 0:2 * P], w1[:, FF + f:FF + f + m], xnf[:], start=True, stop=True)
                    mm = nc.tensor.matmul(pm[0:m, 2 * P:4 * P], w1[:, f:f + m], xnf[:], start=True, stop=True)
                mm.then_inc(m_full, 1)

            def body(pair):
                u = 0
                g = 2 * pair
                turn_qk(g, u, 0)
                turn_qk(g, u, 1)
                qkv(pair, g, u, 0)
                turn_qk(g, u, 2)
                turn_qk(g, u, 3)
                qkv(pair, g, u, 1)
                qkv(pair, g, u, 2)
                scores(g, u, 0)
                scores(g, u, 1)
                ffn(pair, M_TURN)
                qkv(pair, g, u, 3)
                turn_p(g, u, 0)
                turn_p(g, u, 1)
                scores(g, u, 2)
                turn_corner(g, u)
                scores(g, u, 3)
                context(pair, g, u, 0)
                scores(g, u, 4)
                turn_p(g, u, 2)
                scores(g, u, 5)
                turn_p(g, u, 3)
                scores(g, u, 6)
                context(pair, g, u, 1)
                ffn(pair, M_BACK)
                qkv(pair, g, u, 4)
                scores(g, u, 7)
                qkv(pair, g, u, 5)
                project(pair, g, u)

                u = 1
                g = 2 * pair + u
                turn_qk(g, u, 0)
                qkv(pair, g, u, 0)
                turn_qk(g, u, 1)
                qkv(pair, g, u, 1)
                turn_qk(g, u, 2)
                turn_qk(g, u, 3)
                ffn(pair, M_HID0)
                scores(g, u, 0)
                qkv(pair, g, u, 2)
                scores(g, u, 1)
                ffn(pair, M_HID1)
                qkv(pair, g, u, 3)
                turn_p(g, u, 0)
                turn_p(g, u, 1)
                scores(g, u, 2)
                scores(g, u, 3)
                turn_corner(g, u)
                ffn(pair, M_HID2)
                context(pair, g, u, 0)
                turn_p(g, u, 2)
                scores(g, u, 4)
                scores(g, u, 5)
                turn_p(g, u, 3)
                scores(g, u, 6)
                scores(g, u, 7)
                context(pair, g, u, 1)
                ffn(pair, M_OUT)
                qkv(pair, g, u, 4)
                qkv(pair, g, u, 5)
                project(pair, g, u)

            over_pairs(pe, body)

        @block.scalar
        def _(act):
            def build_xs(pair, u):
                g = 2 * pair + u
                wait(act, xa_ready, pair + 1)
                wait(act, x_full, 6 * (g - 1))
                at = col0(pair) + u * P
                nc.scalar.copy(xs[u][0:D // 2, :], t.xa[0:D // 2, bass.ds(at, P)])
                nc.scalar.copy(xs[u][D // 2:D, :], t.xa[D // 2:D, bass.ds(at - 1, P)]).then_inc(xs_built, 1)

            def build_xf(pair):
                wait(act, m_done, m_read(pair - 1, M_WO[1]) + 1)
                at = col0(pair - 2 + PAIRS)
                nc.scalar.copy(xf[0:D // 2, :], t.xb[0:D // 2, bass.ds(at, 2 * P)])
                nc.scalar.copy(xf[D // 2:D, :], t.xb[D // 2:D, bass.ds(at - 1, 2 * P)]).then_inc(xf_ready, 1)

            def copy_raw(g, i):
                wait(act, x_full, 6 * g + i + 1)
                if i >= POOL_SQUARES:
                    wait(act, red_done, 4 * g + i - 3)
                    nc.scalar.activation(sq[:, i, :], px[i % 2][:], ACT.Square).then_inc(sq_act, 1)
                wait(act, rope_ready, 4 * g + i + 1)
                nc.scalar.copy(raw[:, i, :], px[i % 2][:]).then_inc(x_done, 1)

            def copy_v(pair, g, u, i):
                wait(act, x_full, 6 * g + i + 1)
                wait(act, pv_full, 2 * g + 2)
                wait(act, vr_ready[u], 128 * pair)
                nc.scalar.copy(v[u][:, (i - 4) * 512:(i - 3) * 512], px[i % 2][:]).then_inc(x_done, 1)

            def t_bank(u, k):
                return pt[(T_USES * u + k) % 2]

            def copy_qt(g, u, i):
                k = 2 * i + 1
                wait(act, t_full, T_USES * g + k + 1)
                wait(act, s_full, 8 * g)
                nc.scalar.copy(qt[:, 4 * i:4 * i + 4, :].rearrange("p j n -> p (j n)"), t_bank(u, k)[:]).then_inc(t_act, 1)

            def copy_kb(g, u, i):
                k = 2 * i
                wait(act, t_full, T_USES * g + k + 1)
                if i == 0:
                    wait(act, carried, g + 1)
                nc.scalar.copy(kb[HD:P, 4 * i:4 * (i + 1), 1, BAND:KEYS],
                               t_bank(u, k)[HD:P, :].rearrange("p (j n) -> p j n", j=4)).then_inc(t_act, 1)

            def copy_pt(g, u, i):
                wait(act, t_full, T_USES * g + T_P[i] + 1)
                wait(act, pv_full, 2 * g + i // 2)
                nc.scalar.copy(pts[:, i % 2, :], t_bank(u, T_P[i])[:]).then_inc(t_act, 1)

            def copy_corner(g, u):
                wait(act, t_full, T_USES * g + T_CORNER + 1)
                wait(act, pv_full, 2 * g)
                for hh in range(4):
                    rows = slice(BAND * hh, BAND * (hh + 1))
                    src = t_bank(u, 6)[rows, 0:P].rearrange("p (s i) -> p s i", s=4)
                    last = nc.scalar.copy(bd[rows, :, hh, :], src)
                last.then_inc(t_act, 1)

            def exps(g, u, q):
                wait(act, s_done, 8 * g + 2 * q + 2)
                for h in range(4 * q, 4 * q + 4):
                    last = nc.scalar.activation(p[1 - u][:, h, :], p[1 - u][:, h, :], ACT.Exp, bias=nb[u][:, h:h + 1],
                                                scale=-1.0, accum_out=rs[u][:, h:h + 1])
                last.then_inc(exp_done, 1)

            def copy_context(pair, g, u, r):
                wait(act, pv_full, 2 * g + r + 1)
                if not isinstance(g, int) or g > 0:
                    wait(act, m_full, m_use(pair - 1 + u, M_WO[1 - u]) + 1)
                nc.scalar.copy(ot[:, 4 * r:4 * r + 4, :].rearrange("p j n -> p (j n)"), po[:]).then_inc(o_done, 1)

            def ffn(pair, k):
                if isinstance(pair, int) and pair < 2:
                    return
                wait(act, m_full, m_use(pair, k) + 1)
                if k == M_BACK:
                    layer_loaded(act, w_ffn, N_FFN, pair, 2)
                    nc.scalar.activation(xnf[:], pm[:, 0:2 * P], ACT.Identity, bias=vecs[:, 1:2], scale=vecs[:, 0:1]
                                         ).then_inc(m_done, 1)
                else:
                    n = M_HID.index(k)
                    m = FPARTS[n][1]
                    nc.scalar.activation(gl[0:m, :], pm[0:m, 0:2 * P], ACT.Gelu, bias=b1[0:m, NF + n:NF + n + 1]
                                         ).then_inc(g_ready, 1)

            def body(pair):
                u = 0
                g = 2 * pair
                copy_kb(g, u, 0)
                copy_qt(g, u, 0)
                copy_raw(g, 0)
                copy_kb(g, u, 1)
                copy_qt(g, u, 1)
                copy_raw(g, 1)
                if not (isinstance(pair, int) and pair < 2):
                    build_xf(pair)
                copy_raw(g, 2)
                copy_pt(g, u, 0)
                copy_pt(g, u, 1)
                copy_corner(g, u)
                copy_raw(g, 3)
                exps(g, u, 0)
                copy_context(pair, g, u, 0)
                copy_pt(g, u, 2)
                copy_pt(g, u, 3)
                exps(g, u, 1)
                copy_context(pair, g, u, 1)
                ffn(pair, M_BACK)
                copy_v(pair, g, u, 4)
                exps(g, u, 2)
                build_xs(pair + u, 1 - u)
                copy_v(pair, g, u, 5)
                exps(g, u, 3)

                u = 1
                g = 2 * pair + u
                copy_kb(g, u, 0)
                copy_qt(g, u, 0)
                copy_raw(g, 0)
                copy_kb(g, u, 1)
                copy_qt(g, u, 1)
                ffn(pair, M_HID0)
                copy_raw(g, 1)
                copy_raw(g, 2)
                ffn(pair, M_HID1)
                copy_raw(g, 3)
                copy_pt(g, u, 0)
                copy_pt(g, u, 1)
                copy_corner(g, u)
                ffn(pair, M_HID2)
                exps(g, u, 0)
                copy_pt(g, u, 2)
                copy_context(pair, g, u, 0)
                copy_pt(g, u, 3)
                exps(g, u, 1)
                build_xs(pair + u, 1 - u)
                copy_context(pair, g, u, 1)
                exps(g, u, 2)
                exps(g, u, 3)
                copy_v(pair, g, u, 4)
                copy_v(pair, g, u, 5)

            build_xs(0, 0)
            over_pairs(act, body)

        @block.gpsimd
        def _(pool):
            def squares(g, i):
                wait(pool, x_done, 6 * g + i + 1)
                wait(pool, red_done, 4 * g + i - 3)
                nc.gpsimd.tensor_tensor(sq[:, i, :], raw[:, i, :], raw[:, i, :], ALU.mult).then_inc(sq_pool, 1)

            def tables(pair, g, u):
                layer_loaded(pool, w_early, N_EARLY, pair, 0)
                wait(pool, rope_ready, 4 * g)
                pos = (pair % PAIRS_B) * 2 + u
                slot = (pair // PAIRS) % 2
                nc.gpsimd.tensor_tensor(tc[u][:], rope_tab[:, bass.ds(pos, 1), :].rearrange("p s n -> p (s n)"),
                                        scales[:, bass.ds(slot, 1), :].rearrange("p s n -> p (s n)"), ALU.mult
                                        ).then_inc(tc_ready, 1)

            def choose_mask(pair, g):
                wait(pool, s_done, 8 * g)
                pos = pair % PAIRS_B
                nc.gpsimd.tensor_copy(mask[:], mask_tab[:, bass.ds(pos, 1), :].rearrange("p s n -> p (s n)")
                                      ).then_inc(mask_ready, 1)

            def rotated(g, u, i):
                if i == 0:
                    wait(pool, tc_ready, g + 1)
                if i >= POOL_SQUARES:
                    wait(pool, x_done, 6 * g + i + 1)
                wait(pool, rope_ready, 4 * g + i + 1)
                hh = HD // 2
                src = raw[:, i, :].rearrange("p (h d) -> p h d", d=HD)
                dst = rot[:, i, :].rearrange("p (h d) -> p h d", d=HD)
                which = 1 - i // 2
                tab = tc[u][:, (1 + 2 * which) * HD:(2 + 2 * which) * HD]
                nc.gpsimd.tensor_tensor(dst[:, :, 0:hh], src[:, :, hh:HD], wide(tab[:, 0:hh]), ALU.mult)
                nc.gpsimd.tensor_tensor(dst[:, :, hh:HD], src[:, :, 0:hh], wide(tab[:, hh:HD]), ALU.mult
                                        ).then_inc(rot_ready, 1)

            def normalise(g, u, q):
                wait(pool, rinv_ready, 4 * g + q + 1)
                heads = p[1 - u][:, 4 * q:4 * q + 4, BAND:KEYS]
                nc.gpsimd.tensor_tensor(heads, heads, rinv[u][:, 4 * q:4 * q + 4].unsqueeze(2).broadcast_to([P, 4, P]),
                                        ALU.mult).then_inc(p_ready, 1)
                r, hh = q // 2, 2 * (q % 2)
                corner = pc[1 - u][:, 2 * r:2 * r + 2, hh:hh + 2, :].rearrange("p e h k -> p h e k")
                nc.gpsimd.tensor_tensor(corner, p[1 - u][:, 4 * q:4 * q + 4, 0:BAND].rearrange("p (h e) k -> p h e k", e=2),
                                        rinv[u][:, 4 * q:4 * q + 4].rearrange("p (h e) -> p h e", e=2).unsqueeze(3)
                                        .broadcast_to([P, 2, 2, BAND]), ALU.mult).then_inc(corner_ready, 1)

            pool.sem_inc(p_ready, 4)
            pool.sem_inc(corner_ready, 4)

            def body(pair):
                u = 0
                g = 2 * pair
                tables(pair, g, u)
                squares(g, 0)
                squares(g, 1)
                if not isinstance(g, int) or g > 0:
                    normalise(g - 1, 1 - u, 3)
                rotated(g, u, 0)
                rotated(g, u, 1)
                choose_mask(pair, g)
                straight(pool, nc.gpsimd, g, u, 2)
                rotated(g, u, 2)
                straight(pool, nc.gpsimd, g, u, 3)
                rotated(g, u, 3)
                normalise(g, u, 0)
                normalise(g, u, 1)
                normalise(g, u, 2)

                u = 1
                g = 2 * pair + u
                normalise(g - 1, 1 - u, 3)
                tables(pair, g, u)
                squares(g, 0)
                rotated(g, u, 0)
                squares(g, 1)
                rotated(g, u, 1)
                straight(pool, nc.gpsimd, g, u, 2)
                rotated(g, u, 2)
                straight(pool, nc.gpsimd, g, u, 3)
                rotated(g, u, 3)
                normalise(g, u, 0)
                normalise(g, u, 1)
                normalise(g, u, 2)

            over_pairs(pool, body)

        @block.vector
        def _(dve):
            def t_bank(u, k):
                return pt[(T_USES * u + k) % 2]

            def linked(instruction, value):
                instruction.then_inc(link, 1)
                dve.wait_ge(link, value)

            def carry(pair, g, u):
                wait(dve, s_full, 8 * g)
                flat = kb[:].rearrange("p j e k -> p (j e) k")
                if u == 1:
                    wait(dve, mask_ready, pair + 1)
                    ins = nc.vector.tensor_scalar(flat[:, :, 0:BAND], flat[:, :, P:KEYS], mask[:, KEYS:KEYS + 1], None, ALU.mult)
                else:
                    ins = nc.vector.tensor_copy(flat[:, :, 0:BAND], flat[:, :, P:KEYS])
                ins.then_inc(carried, 1)

            def copy_kb(g, u, i):
                k = 2 * i
                wait(dve, t_full, T_USES * g + k + 1)
                if i == 0:
                    wait(dve, carried, g + 1)
                nc.vector.tensor_copy(kb[0:HD, 4 * i:4 * (i + 1), 0, BAND:KEYS],
                                      t_bank(u, k)[0:HD, :].rearrange("p (j n) -> p j n", j=4)).then_inc(t_dve, 1)

            def head_norms(g, i):
                if i < POOL_SQUARES:
                    wait(dve, sq_pool, POOL_SQUARES * g + i + 1)
                else:
                    wait(dve, sq_act, (4 - POOL_SQUARES) * g + i - POOL_SQUARES + 1)
                nc.vector.tensor_reduce(ss[:, 8 * i:8 * i + 8], sq[:, i, :].rearrange("p (h d) -> p h d", d=HD),
                                        AX.X, ALU.add).then_inc(red_done, 1)

            FACTORS = RSQRT_STEPS + 2
            Q_HEADS = slice(HEADS, 2 * HEADS)

            def factors(g, u, n):
                if n == 0:
                    wait(dve, red_done, 4 * g + 4)
                    ins = nc.vector.tensor_scalar(ss[:], ss[:], 1e-24, None, ALU.max)
                elif n <= RSQRT_STEPS:
                    dve.wait_ge(link, n)
                    ins = rsqrt_step(nc, n - 1, rn[u][:], ss[:], nhalf[:])
                else:
                    dve.wait_ge(link, n)
                    ins = nc.vector.tensor_scalar(rn[u][:, Q_HEADS], rn[u][:, Q_HEADS], -SIM_SCALE, None, ALU.mult)
                ins.then_inc(link, 1)

            def masked_scores(pair, g, u, j, e):
                if e == 0:
                    wait(dve, s_full, 8 * g + j + 1)
                    if j == 0:
                        wait(dve, t_full, T_USES * g)
                    dve.sem_inc(apart, 1)
                m = mask[:, 0:KEYS] if u == 1 else mask_odd[:]
                h = 2 * j + e
                factor = rn[1 - u][:, HEADS + h:HEADS + h + 1]
                ins = nc.vector.tensor_tensor_reduce(p[1 - u][:, h, :], ps[j % 2][:, e * KEYS:(e + 1) * KEYS], m,
                                                     factor, 3e38, ALU.add, ALU.min, nb[u][:, h:h + 1])
                if e == 1:
                    ins.then_inc(s_done, 1)

            def inverse_sums(g, u, q):
                wait(dve, exp_done, 4 * g + q + 1)
                nc.vector.reciprocal(rinv[u][:, 4 * q:4 * q + 4], rs[u][:, 4 * q:4 * q + 4]).then_inc(rinv_ready, 1)

            def add_rotated(g, i):
                if i < DVE_STRAIGHT:
                    dve.wait_ge(mult_done, i + 1)
                wait(dve, rot_ready, 4 * g + i + 1)
                nc.vector.tensor_tensor(rope[:, i, :], rope[:, i, :], rot[:, i, :], ALU.add).then_inc(rope_ready, 1)

            def k_normalised(g, u, i):
                if i == 0:
                    dve.wait_ge(link, 1 + RSQRT_STEPS)
                wait(dve, rope_ready, 4 * g + 4 + i + 1)
                heads = rope[:, i, :].rearrange("p (h d) -> p h d", d=HD)
                nc.vector.tensor_tensor(heads, heads, rn[u][:, 8 * i:8 * i + 8].unsqueeze(2).broadcast_to([P, 8, HD]),
                                        ALU.mult).then_inc(kn_ready, 1)

            def add_attention(pair, g, u):
                wait(dve, m_full, m_use(pair, M_WO[u]) + 1)
                at = col0(pair - 1 + PAIRS) + u * P
                nc.vector.tensor_tensor(t.xb[:, bass.ds(at, P)], pm[:, 0:P], t.xa[:, bass.ds(at, P)], ALU.add
                                        ).then_inc(m_done, 1)

            LN_STEPS = RSQRT_STEPS + 4

            def layer_norm(pair, n):
                if isinstance(pair, int) and pair < 2:
                    return
                if n == 0:
                    wait(dve, m_full, m_use(pair, M_TURN) + 1)
                    for c in range(2):
                        nc.vector.bn_stats(st[:, c, :], pm[:, c * P:(c + 1) * P]).then_inc(ffn_link, 1)
                elif n == 1:
                    for c in range(2):
                        dve.wait_ge(ffn_link, c + 1)
                        nc.vector.bn_aggr(mv[:, c, :], st[:, c, :]).then_inc(ffn_link, 1)
                elif n == 2:
                    dve.wait_ge(ffn_link, 4)
                    nc.vector.tensor_scalar(ve[:], mv[:, :, 1], 1e-5, None, ALU.add).then_inc(ffn_link, 1)
                elif n < LN_STEPS - 1:
                    dve.wait_ge(ffn_link, 2 + n)
                    rsqrt_step(nc, n - 3, vr_std[:], ve[:], vh[:]).then_inc(ffn_link, 1)
                else:
                    dve.wait_ge(ffn_link, 2 + n)
                    for c in range(2):
                        last = nc.vector.tensor_scalar(xnt[:, c, :], pm[:, c * P:(c + 1) * P], mv[:, c, 0:1],
                                                       vr_std[:, c:c + 1], ALU.subtract, ALU.mult)
                    last.then_inc(m_done, 1)

            def ffn(pair, k):
                if isinstance(pair, int) and pair < 2:
                    return
                wait(dve, m_full, m_use(pair, k) + 1)
                if k == M_OUT:
                    wait(dve, xs_built, 2 * pair - 1)
                    at = col0(pair - 2 + PAIRS)
                    nc.vector.scalar_tensor_tensor(t.xa[:, bass.ds(at, 2 * P)], pm[:, 0:2 * P], vecs[:, 2:3],
                                                   t.xb[:, bass.ds(at, 2 * P)], ALU.add, ALU.add).then_inc(xa_ready, 1)
                else:
                    n = M_HID.index(k)
                    m = FPARTS[n][1]
                    wait(dve, g_ready, NF * pair + (n + 1 - 2 * NF))
                    nc.vector.scalar_tensor_tensor(hid[0:m, n, :], pm[0:m, 2 * P:4 * P], b1[0:m, n:n + 1], gl[0:m, :],
                                                   ALU.add, ALU.mult).then_inc(m_done, 1)

            dve.sem_inc(rope_ready, 4)
            dve.sem_inc(kn_ready, 2)
            dve.sem_inc(xa_ready, PAIRS)

            def body(pair):
                u = 0
                g = 2 * pair
                if not isinstance(g, int) or g > 0:
                    dve.wait_ge(link, FACTORS)
                dve.sem_clear(link)
                dve.sem_clear(mult_done)
                dve.sem_clear(ffn_link)
                carry(pair, g, u)
                if not isinstance(g, int) or g > 0:
                    inverse_sums(g - 1, 1 - u, 3)
                if not isinstance(g, int) or g > 0:
                    add_attention(pair - 1 + u, g - 1, 1 - u)
                copy_kb(g, u, 0)
                copy_kb(g, u, 1)
                straight(dve, nc.vector, g, u, 0)
                head_norms(g, 0)
                straight(dve, nc.vector, g, u, 1)
                masked_scores(pair, g, u, 0, 0)
                layer_norm(pair, 0)
                masked_scores(pair, g, u, 0, 1)
                masked_scores(pair, g, u, 1, 0)
                layer_norm(pair, 1)
                masked_scores(pair, g, u, 1, 1)
                head_norms(g, 1)
                layer_norm(pair, 2)
                layer_norm(pair, 3)
                layer_norm(pair, 4)
                layer_norm(pair, 5)
                masked_scores(pair, g, u, 2, 0)
                masked_scores(pair, g, u, 2, 1)
                layer_norm(pair, 6)
                masked_scores(pair, g, u, 3, 0)
                layer_norm(pair, 7)
                masked_scores(pair, g, u, 3, 1)
                layer_norm(pair, 8)
                layer_norm(pair, 9)
                head_norms(g, 2)
                head_norms(g, 3)
                layer_norm(pair, 10)
                masked_scores(pair, g, u, 4, 0)
                factors(g, u, 0)
                layer_norm(pair, 11)
                factors(g, u, 1)
                masked_scores(pair, g, u, 4, 1)
                layer_norm(pair, 12)
                factors(g, u, 2)
                masked_scores(pair, g, u, 5, 0)
                factors(g, u, 3)
                layer_norm(pair, 13)
                masked_scores(pair, g, u, 5, 1)
                layer_norm(pair, 14)
                factors(g, u, 4)
                add_rotated(g, 0)
                factors(g, u, 5)
                add_rotated(g, 1)
                factors(g, u, 6)
                masked_scores(pair, g, u, 6, 0)
                factors(g, u, 7)
                masked_scores(pair, g, u, 6, 1)
                factors(g, u, 8)
                inverse_sums(g, u, 0)
                inverse_sums(g, u, 1)
                masked_scores(pair, g, u, 7, 0)
                factors(g, u, 9)
                factors(g, u, 10)
                factors(g, u, 11)
                add_rotated(g, 2)
                factors(g, u, 12)
                k_normalised(g, u, 0)
                masked_scores(pair, g, u, 7, 1)
                k_normalised(g, u, 1)
                add_rotated(g, 3)
                inverse_sums(g, u, 2)

                u = 1
                g = 2 * pair + u
                dve.wait_ge(link, FACTORS)
                dve.sem_clear(link)
                dve.sem_clear(mult_done)
                carry(pair, g, u)
                copy_kb(g, u, 0)
                add_attention(pair - 1 + u, g - 1, 1 - u)
                inverse_sums(g - 1, 1 - u, 3)
                copy_kb(g, u, 1)
                straight(dve, nc.vector, g, u, 0)
                ffn(pair, M_HID0)
                head_norms(g, 0)
                straight(dve, nc.vector, g, u, 1)
                masked_scores(pair, g, u, 0, 0)
                masked_scores(pair, g, u, 0, 1)
                masked_scores(pair, g, u, 1, 0)
                ffn(pair, M_HID1)
                masked_scores(pair, g, u, 1, 1)
                head_norms(g, 1)
                masked_scores(pair, g, u, 2, 0)
                masked_scores(pair, g, u, 2, 1)
                masked_scores(pair, g, u, 3, 0)
                masked_scores(pair, g, u, 3, 1)
                head_norms(g, 2)
                head_norms(g, 3)
                factors(g, u, 0)
                factors(g, u, 1)
                factors(g, u, 2)
                masked_scores(pair, g, u, 4, 0)
                masked_scores(pair, g, u, 4, 1)
                masked_scores(pair, g, u, 5, 0)
                factors(g, u, 3)
                masked_scores(pair, g, u, 5, 1)
                add_rotated(g, 0)
                factors(g, u, 4)
                ffn(pair, M_HID2)
                factors(g, u, 5)
                factors(g, u, 6)
                inverse_sums(g, u, 0)
                masked_scores(pair, g, u, 6, 0)
                add_rotated(g, 1)
                factors(g, u, 7)
                masked_scores(pair, g, u, 6, 1)
                masked_scores(pair, g, u, 7, 0)
                factors(g, u, 8)
                factors(g, u, 9)
                factors(g, u, 10)
                inverse_sums(g, u, 1)
                masked_scores(pair, g, u, 7, 1)
                ffn(pair, M_OUT)
                add_rotated(g, 2)
                inverse_sums(g, u, 2)
                factors(g, u, 11)
                factors(g, u, 12)
                k_normalised(g, u, 0)
                add_rotated(g, 3)
                k_normalised(g, u, 1)

            over_pairs(dve, body)
            add_attention(steps - 1, 2 * steps - 1, 1)


def finish(nc, t):
    with ExitStack() as ctx:
        turned = [ctx.enter_context(nc.psum_tensor(f"fin_turned{i}", [P, 512], F32)) for i in range(2)]
        full = ctx.enter_context(nc.semaphore("fin_full"))
        summed = ctx.enter_context(nc.semaphore("fin_summed"))
        stored = ctx.enter_context(nc.semaphore("fin_stored"))
        block = ctx.enter_context(nc.Block())
        out = t.out.rearrange("b (c p) d -> p (b c) d", p=P)

        @block.tensor
        def _(pe):
            for n in range(CHUNKS // 4):
                if n >= 2:
                    pe.wait_ge(summed, n - 1)
                at = 4 * n * P + (4 * n) // (S // P) + 1
                for k in range(4):
                    mm = nc.tensor.transpose(turned[n % 2][:, k * P:(k + 1) * P], t.xa[:, at + k * P:at + (k + 1) * P], t.ident[:])
                mm.then_inc(full, 1)

        @block.vector
        def _(dve):
            for n in range(CHUNKS // 4):
                dve.wait_ge(full, n + 1)
                chunk = t.xtok[:, 4 * n:4 * n + 4, :].rearrange("p c d -> p (c d)")
                nc.vector.tensor_tensor(chunk, turned[n % 2][:], chunk, ALU.add).then_inc(summed, 1)

        @block.sync
        def _(sp):
            for n in range(CHUNKS // 4):
                sp.wait_ge(summed, n + 1)
                sp.dma_start(out[:, 4 * n:4 * n + 4, :], t.xtok[:, 4 * n:4 * n + 4, :]).then_inc(stored, 16)
            sp.wait_ge(stored, 16 * (CHUNKS // 4))


class Tensors:
    pass


def build(nc, t, with_attention=True):
    t.q_parts_d = nc.dram_tensor("q_parts", (3, D, B * S), BF16, kind="Internal").ap()
    t.k_parts_d = nc.dram_tensor("k_parts", (3, D, B * S), BF16, kind="Internal").ap()
    with ExitStack() as ctx:
        def sb(name, shape):
            return ctx.enter_context(nc.sbuf_tensor(name, shape, F32))

        t.xtok = sb("xtok", [P, CHUNKS, D])
        t.xa = sb("xa", [P, COLS])
        t.xb = sb("xb", [P, COLS])
        t.ident = sb("ident", [P, P])
        prepare(nc, t)
        if with_attention:
            attention(nc, t)
        windowed(nc, t)
        finish(nc, t)


def shape_constants():
    f = np.float32
    half = np.arange(0, HD, 2, dtype=f)
    inv_freq = (f(1.0) / f(10000.0) ** (half / f(HD))).astype(f)
    tok = np.arange(S, dtype=f)
    freqs = tok[:, None] * inv_freq[None, :]
    freqs = np.concatenate([freqs, freqs], -1)
    base = (half + f(0.4 * HD)) / f(1.4 * HD)
    power = (tok - f(S // 2)) / f(BAND // 2)
    scale = base[None, :] ** power[:, None]
    scale = np.concatenate([scale, scale], -1).astype(f)
    cos, sin = np.cos(freqs).astype(f), np.sin(freqs).astype(f)
    sign = np.where(np.arange(HD) < HD // 2, -1, 1).astype(f)
    inv = f(1.0) / scale
    tab = np.concatenate([cos * scale, sin * scale * sign, cos * inv, sin * inv * sign], 1)
    rope = np.ascontiguousarray(tab.reshape(S // P, P, 4 * HD).transpose(1, 0, 2)).astype(f)
    i, j = np.arange(P)[:, None], np.arange(KEYS)[None, :] - BAND
    odd = np.where((j <= i) & (i <= j + BAND), 0.0, MASKED).astype(f)
    first = np.where(j < 0, f(MASKED), odd).astype(f)
    masks = np.ones((P, PAIRS_B, KEYS + 1), f)
    masks[:, :, :KEYS] = odd[:, None, :]
    masks[:, 0, :KEYS] = first
    masks[:, 0, KEYS] = 0.0
    later = np.where(np.arange(P)[None, :] > np.arange(P)[:, None], f(MASKED), f(0.0)).astype(f)
    return {"ident": np.eye(P, dtype=f), "rope_tab": rope, "mask_tab": masks, "mask_odd": odd,
            "a_masks": np.ascontiguousarray(np.stack([later, later.T], 1))}


_INS = {"L0_attn_x": "x", "L0_attn_W_qkv": "awqkv_d", "L0_attn_q_scale": "aqs_d", "L0_attn_k_scale": "aks_d",
        "L0_attn_W_out": "awout_d", "L0_ffn_Wqkv": "wqkv_d", "L0_ffn_q_scale": "qs_d", "L0_ffn_k_scale": "ks_d",
        "L0_ffn_Wo": "wo_d", "L0_ffn_ln_g": "g_d", "L0_ffn_ln_b": "b_d", "L0_ffn_W1": "w1_d", "L0_ffn_b1": "b1_d",
        "L0_ffn_W2": "w2_d", "L0_ffn_b2": "b2_d"}
_CONSTS = {"ident": "ident_d", "rope_tab": "rope_d", "mask_tab": "mask_d", "mask_odd": "mask_odd_d",
           "a_masks": "amasks_d"}


def kernel(**inputs):
    import concourse.bacc as bacc
    from concourse.bass_utils import run_bass_kernel_spmd

    nc = bacc.Bacc("TRN2", target_bir_lowering=False, num_devices=1)
    t = Tensors()
    arrays = {}

    def dram_in(name, a):
        arrays[name] = a
        return nc.dram_tensor(name, a.shape, mybir.dt.from_np(a.dtype), kind="ExternalInput").ap()

    d = {}
    for name in _INS:
        d[_INS[name]] = dram_in("in_" + name, np.ascontiguousarray(inputs[name]))
    for name, a in shape_constants().items():
        d[_CONSTS[name]] = dram_in("const_" + name, a)
    t.__dict__.update(d)
    t.out = nc.dram_tensor("out", (B, S, D), F32, kind="ExternalOutput").ap()
    build(nc, t)
    r = run_bass_kernel_spmd(nc, [arrays], core_ids=[0])
    return r.results[0]["out"]
```
